# Optimizing a Trainium2 kernel written in Bass

```python
import numpy as np
import jax
import jax.numpy as jnp

def _softmax(x, axis=-1):
    return jax.nn.softmax(x, axis=axis)

def _gelu(x):
    return jax.nn.gelu(x, approximate=True)

def _silu(x):
    return jax.nn.silu(x)

def _sigmoid(x):
    return jax.nn.sigmoid(x)

def _layernorm(x, axis=-1, eps=1e-05):
    m = jnp.mean(x, axis=axis, keepdims=True)
    v = jnp.var(x, axis=axis, keepdims=True)
    return (x - m) / jnp.sqrt(v + eps)

def _scatter_add(tgt, idx, src, axis=0):
    return tgt.at[idx].add(src)

def _segment_sum(src, seg, n):
    return jax.ops.segment_sum(src, seg, n)
kernel_name = 'mk_decoder_postln_d2_seqx_r8_89e35b'

def setup_inputs(seed: int=0):
    np.random.seed(seed)
    _w = jnp.asarray

    def _rec_inputs():
        import jax
        import jax.numpy as jnp
        _rk = jax.random.key(seed)
        x = 7.22e-05 + 1 * jax.random.normal(jax.random.fold_in(_rk, 1), (32, 128, 128), jnp.float32)
        _lenS = 128 - jax.random.randint(jax.random.fold_in(_rk, 7), (32,), 0, max(1, 128 // 4) + 1, jnp.int32)
        _lenS2 = 128 - jax.random.randint(jax.random.fold_in(_rk, 8), (32,), 0, max(1, 128 // 4) + 1, jnp.int32)
        _ctx_1024P = jax.random.normal(jax.random.fold_in(_rk, 11), (32, 16, 128), jnp.float32)
        _ctx_1024c = jax.random.dirichlet(jax.random.fold_in(_rk, 511), 0.3 * jnp.ones((16,), jnp.float32), (32, 128))
        _ctx_1024t = jnp.einsum('bsk,bkd->bsd', _ctx_1024c, _ctx_1024P)
        _ctx_1024t = _ctx_1024t * jax.lax.rsqrt(jnp.mean(jnp.square(_ctx_1024t)) + 1e-12) * 0.953939
        ctx_1024 = 4.13588e-05 + 0.999923 * (_ctx_1024t + 0.3 * jax.random.normal(jax.random.fold_in(_rk, 611), (32, 128, 128), jnp.float32))
        _validS = jnp.arange(128)[None, :] < _lenS[:, None]
        _validS2 = jnp.arange(128)[None, :] < _lenS2[:, None]
        _causal = jnp.tril(jnp.ones((128, 128), dtype=bool))
        mask_BxS2_ff1 = jnp.where(jnp.ones((32, 128), dtype=bool), 1.0, 0.0).astype(jnp.float32)
        return (x, ctx_1024, mask_BxS2_ff1)
    x, ctx_1024, mask_BxS2_ff1 = _rec_inputs()

    def _L0_attn_setup():
        import jax, jax.numpy as jnp
        import numpy as np
        DIM_IN, DIM_K, DIM_V, NH = (128, 128, 128, 16)
        DK, DV = (DIM_K // NH, DIM_V // NH)
        key = jax.random.key(seed)
        kx, kq, kk, kv = jax.random.split(key, 4)
        x = jax.random.normal(kx, (4, 256, DIM_IN), dtype=jnp.float32)
        Wq = jax.random.normal(kq, (DIM_K, DIM_IN), dtype=jnp.float32) / np.sqrt(DIM_IN)
        Wk = jax.random.normal(kk, (DK, DIM_IN), dtype=jnp.float32) / np.sqrt(DIM_IN)
        Wv = jax.random.normal(kv, (DV, DIM_IN), dtype=jnp.float32) / np.sqrt(DIM_IN)
        return {'x': x, 'Wq': Wq, 'Wk': Wk, 'Wv': Wv}
    _L0_attn_all = _L0_attn_setup()
    _L0_attn_in = {k: v for k, v in _L0_attn_all.items() if k in ('Wq', 'Wk', 'Wv')}
    del _L0_attn_all

    def _L0_xattn_setup():
        import jax, jax.numpy as jnp
        import numpy as np
        D_MODEL = 128
        NUM_HEADS = 16
        HEAD_DIM = D_MODEL // NUM_HEADS
        B, T = (4, 256)
        key = jax.random.key(seed)
        ks = jax.random.split(key, 6)
        s = 1.0 / np.sqrt(D_MODEL)
        return {'x_q': jax.random.normal(ks[0], (B, T, D_MODEL), jnp.float32), 'x_kv': jax.random.normal(ks[1], (B, T, D_MODEL), jnp.float32), 'Wq': jax.random.uniform(ks[2], (D_MODEL, D_MODEL), jnp.float32, -s, s), 'Wk': jax.random.uniform(ks[3], (D_MODEL, D_MODEL), jnp.float32, -s, s), 'Wv': jax.random.uniform(ks[4], (D_MODEL, D_MODEL), jnp.float32, -s, s), 'Wo': jax.random.uniform(ks[5], (D_MODEL, D_MODEL), jnp.float32, -s, s)}
    _L0_xattn_all = _L0_xattn_setup()
    _L0_xattn_in = {k: v for k, v in _L0_xattn_all.items() if k in ('Wq', 'Wk', 'Wv', 'Wo')}
    del _L0_xattn_all

    def _L0_ffn_setup():
        import jax, jax.numpy as jnp
        import numpy as np
        DIM = 128
        DEPTH = 2
        HEADS = 8
        DIM_HEAD = 64
        WINDOW = 64
        INNER = HEADS * DIM_HEAD
        HID = int(DIM * 4 * 2 / 3)
        B, N = (2, 1024)
        QK_SCALE = 8.0

        def shift_token(t):
            t1, t2 = jnp.split(t, 2, axis=-1)
            t2 = jnp.pad(t2, ((0, 0), (1, 0), (0, 0)))[:, :-1]
            return jnp.concatenate([t1, t2], axis=-1)

        def l2norm(t):
            return t / jnp.clip(jnp.linalg.norm(t, axis=-1, keepdims=True), 1e-12)

        def rotate_half(x):
            x1, x2 = jnp.split(x, 2, axis=-1)
            return jnp.concatenate([-x2, x1], axis=-1)

        def rotary_xpos(q, k):
            n = q.shape[-2]
            half_idx = jnp.arange(0, DIM_HEAD, 2, dtype=jnp.float32)
            inv_freq = 1.0 / 10000.0 ** (half_idx / DIM_HEAD)
            t = jnp.arange(n, dtype=jnp.float32)
            freqs = t[:, None] * inv_freq[None, :]
            freqs = jnp.concatenate([freqs, freqs], axis=-1)
            base = (half_idx + 0.4 * DIM_HEAD) / (1.4 * DIM_HEAD)
            power = (t - n // 2) / float(WINDOW // 2)
            scale = base[None, :] ** power[:, None]
            scale = jnp.concatenate([scale, scale], axis=-1)
            cos, sin = (jnp.cos(freqs), jnp.sin(freqs))
            q = q * cos * scale + rotate_half(q) * sin * scale
            k = k * cos / scale + rotate_half(k) * sin / scale
            return (q, k)

        def local_attention(q, k, v):
            b, h, n, d = q.shape
            w = n // WINDOW
            bq = q.reshape(b, h, w, WINDOW, d) * QK_SCALE
            bk = k.reshape(b, h, w, WINDOW, d)
            bv = v.reshape(b, h, w, WINDOW, d)

            def look_around(t):
                p = jnp.pad(t, ((0, 0), (0, 0), (1, 0), (0, 0), (0, 0)))
                return jnp.concatenate([p[:, :, :w], p[:, :, 1:]], axis=3)
            bk, bv = (look_around(bk), look_around(bv))
            bt = jnp.arange(n).reshape(w, WINDOW)
            btp = jnp.pad(bt, ((1, 0), (0, 0)), constant_values=-1)
            btk = jnp.concatenate([btp[:w], btp[1:]], axis=1)
            sim = jnp.einsum('bhwid,bhwjd->bhwij', bq, bk)
            i = bt[:, :, None]
            j = btk[:, None, :]
            mask = (i < j) | (i > j + WINDOW) | (j == -1)
            sim = jnp.where(mask, -jnp.finfo(sim.dtype).max, sim)
            attn = jax.nn.softmax(sim, axis=-1)
            out = jnp.einsum('bhwij,bhwjd->bhwid', attn, bv)
            return out.reshape(b, h, n, d)

        def _layer(x, wqkv, qs, ksc, wo, lg, lb, w1, b1, w2, b2):
            b, n, _ = x.shape
            h = shift_token(x)
            qkv = h @ wqkv
            q, k, v = jnp.split(qkv, 3, axis=-1)
            to_heads = lambda t: t.reshape(b, n, HEADS, DIM_HEAD).transpose(0, 2, 1, 3)
            q, k, v = (to_heads(q), to_heads(k), to_heads(v))
            q = l2norm(q) * qs
            k = l2norm(k) * ksc
            q, k = rotary_xpos(q, k)
            o = local_attention(q, k, v)
            o = o.transpose(0, 2, 1, 3).reshape(b, n, INNER)
            x = x + o @ wo
            h = shift_token(x)
            mu = h.mean(-1, keepdims=True)
            var = h.var(-1, keepdims=True)
            h = (h - mu) / jnp.sqrt(var + 1e-05) * lg + lb
            h = h @ w1 + b1
            a, g = jnp.split(h, 2, axis=-1)
            h = a * jax.nn.gelu(g, approximate=False)
            x = x + h @ w2 + b2
            return x
        key = jax.random.key(seed)
        ks = jax.random.split(key, 6)
        return {'x': jax.random.normal(ks[0], (B, N, DIM), jnp.float32), 'wqkv': jax.random.normal(ks[1], (DEPTH, DIM, 3 * INNER), jnp.float32) * 0.02, 'q_scale': jnp.ones((DEPTH, DIM_HEAD), jnp.float32), 'k_scale': jnp.ones((DEPTH, DIM_HEAD), jnp.float32), 'wo': jax.random.normal(ks[2], (DEPTH, INNER, DIM), jnp.float32) * 0.02, 'ln_g': jnp.ones((DEPTH, DIM), jnp.float32), 'ln_b': jnp.zeros((DEPTH, DIM), jnp.float32), 'w1': jax.random.normal(ks[3], (DEPTH, DIM, 2 * HID), jnp.float32) * 0.02, 'b1': jnp.zeros((DEPTH, 2 * HID), jnp.float32), 'w2': jax.random.normal(ks[4], (DEPTH, HID, DIM), jnp.float32) * 0.02, 'b2': jnp.zeros((DEPTH, DIM), jnp.float32)}
    _L0_ffn_all = _L0_ffn_setup()
    _L0_ffn_in = {k: v for k, v in _L0_ffn_all.items() if k in ('wqkv', 'q_scale', 'k_scale', 'wo', 'ln_g', 'ln_b', 'w1', 'b1', 'w2', 'b2')}
    del _L0_ffn_all

    def _L1_attn_setup():
        import jax, jax.numpy as jnp
        import numpy as np
        import math
        D_MODEL, D_C, D_R, NH = (128, 128, 32, 16)
        HD = D_MODEL // NH
        B, T = (2, 256)

        def _rope_tables(T, d_R):
            inv_freq = 1.0 / 10000.0 ** (jnp.arange(0, d_R, 2, dtype=jnp.float32) / d_R)
            t = jnp.arange(T, dtype=jnp.float32)
            freqs = jnp.outer(t, inv_freq)
            return (jnp.cos(freqs), jnp.sin(freqs))

        def _rotary_apply(x, cos, sin):
            d = x.shape[-1]
            x1, x2 = (x[..., :d // 2], x[..., d // 2:])
            return jnp.concatenate([x1 * cos - x2 * sin, x2 * cos + x1 * sin], axis=-1)
        key = jax.random.key(seed)
        ks = jax.random.split(key, 8)
        s = lambda fan_in: 1.0 / math.sqrt(fan_in)
        return {'x': jax.random.normal(ks[0], (B, T, D_MODEL), jnp.float32), 'W_kv_down': jax.random.normal(ks[1], (D_MODEL, D_C), jnp.float32) * s(D_MODEL), 'W_k_up': jax.random.normal(ks[2], (D_C, D_MODEL), jnp.float32) * s(D_C), 'W_v_up': jax.random.normal(ks[3], (D_C, D_MODEL), jnp.float32) * s(D_C), 'W_q': jax.random.normal(ks[4], (D_MODEL, D_MODEL), jnp.float32) * s(D_MODEL), 'W_q_rope': jax.random.normal(ks[5], (D_MODEL, D_R), jnp.float32) * s(D_MODEL), 'W_k_rope': jax.random.normal(ks[6], (D_C, D_R), jnp.float32) * s(D_C), 'W_o': jax.random.normal(ks[7], (D_MODEL, D_MODEL), jnp.float32) * s(D_MODEL)}
    _L1_attn_all = _L1_attn_setup()
    _L1_attn_in = {k: v for k, v in _L1_attn_all.items() if k in ('W_kv_down', 'W_k_up', 'W_v_up', 'W_q', 'W_q_rope', 'W_k_rope', 'W_o')}
    del _L1_attn_all

    def _L1_xattn_setup():
        import jax, jax.numpy as jnp
        import numpy as np
        D_MODEL = 128
        HEADS = 16
        DEPTH = D_MODEL // HEADS
        B, S = (4, 512)
        EPS_K = 1e-06
        EPS_LN = 1e-06

        def _layernorm(x, g, b):
            m = jnp.mean(x, axis=-1, keepdims=True)
            var = jnp.var(x, axis=-1, keepdims=True)
            return (x - m) * jax.lax.rsqrt(var + EPS_LN) * g + b

        def _split_heads(x):
            bsz, sl, _ = x.shape
            return x.reshape(bsz, sl, HEADS, DEPTH).transpose(0, 2, 1, 3)
        key = jax.random.key(seed)
        ks = jax.random.split(key, 8)
        lecun = 1.0 / np.sqrt(D_MODEL)
        glorot = np.sqrt(2.0 / (D_MODEL + D_MODEL))
        return {'q': jax.random.normal(ks[0], (B, S, D_MODEL), jnp.float32), 'k': jax.random.normal(ks[1], (B, S, D_MODEL), jnp.float32), 'v': jax.random.normal(ks[2], (B, S, D_MODEL), jnp.float32), 'mask': jnp.ones((B, S), jnp.float32), 'wq': jax.random.normal(ks[3], (D_MODEL, D_MODEL), jnp.float32) * lecun, 'wk': jax.random.normal(ks[4], (D_MODEL, D_MODEL), jnp.float32) * lecun, 'wv': jax.random.normal(ks[5], (D_MODEL, D_MODEL), jnp.float32) * lecun, 'ln_gamma': jnp.ones((D_MODEL,), jnp.float32), 'ln_beta': jnp.zeros((D_MODEL,), jnp.float32), 'dense_w': jax.random.normal(ks[6], (D_MODEL, D_MODEL), jnp.float32) * glorot, 'dense_b': jnp.zeros((D_MODEL,), jnp.float32)}
    _L1_xattn_all = _L1_xattn_setup()
    _L1_xattn_in = {k: v for k, v in _L1_xattn_all.items() if k in ('wq', 'wk', 'wv', 'ln_gamma', 'ln_beta', 'dense_w', 'dense_b')}
    del _L1_xattn_all

    def _L1_ffn_setup():
        import jax, jax.numpy as jnp
        import numpy as np
        B, S, D = (8, 64, 128)
        H = 16
        DFF = 512
        E = 4
        K = 2
        EPS = 1e-05

        def _layernorm(x, w, b):
            m = x.mean(-1, keepdims=True)
            v = ((x - m) ** 2).mean(-1, keepdims=True)
            return (x - m) / jnp.sqrt(v + EPS) * w + b

        def _encoder_layer(x, iw, ib, ow, ob, l1w, l1b, l2w, l2b, n1w, n1b, n2w, n2b):
            b, s, d = x.shape
            hd = d // H
            qkv = x @ iw.T + ib
            q, k, v = jnp.split(qkv, 3, axis=-1)
            rs = lambda t: t.reshape(b, s, H, hd).transpose(0, 2, 1, 3)
            q, k, v = (rs(q), rs(k), rs(v))
            scale = jnp.asarray(hd, x.dtype) ** 0.5
            scores = jnp.einsum('bhqd,bhkd->bhqk', q, k) / scale
            attn = jax.nn.softmax(scores, axis=-1)
            o = jnp.einsum('bhqk,bhkd->bhqd', attn, v).transpose(0, 2, 1, 3).reshape(b, s, d)
            o = o @ ow.T + ob
            x = _layernorm(x + o, n1w, n1b)
            ff = jax.nn.relu(x @ l1w.T + l1b) @ l2w.T + l2b
            return _layernorm(x + ff, n2w, n2b)
        key = jax.random.key(seed)
        ks = jax.random.split(key, 12)
        g = lambda k, shape: jax.random.normal(k, shape, dtype=jnp.float32) * 0.02
        return {'x': jax.random.normal(ks[0], (B, S, D), dtype=jnp.float32), 'in_proj_w': g(ks[1], (E, 3 * D, D)), 'in_proj_b': g(ks[2], (E, 3 * D)), 'out_proj_w': g(ks[3], (E, D, D)), 'out_proj_b': g(ks[4], (E, D)), 'ln1_w': jnp.ones((E, D), jnp.float32), 'ln1_b': jnp.zeros((E, D), jnp.float32), 'lin1_w': g(ks[5], (E, DFF, D)), 'lin1_b': g(ks[6], (E, DFF)), 'lin2_w': g(ks[7], (E, D, DFF)), 'lin2_b': g(ks[8], (E, D)), 'ln2_w': jnp.ones((E, D), jnp.float32), 'ln2_b': jnp.zeros((E, D), jnp.float32), 'gate_w': g(ks[9], (E, D)), 'gate_b': g(ks[10], (E,))}
    _L1_ffn_all = _L1_ffn_setup()
    _L1_ffn_in = {k: v for k, v in _L1_ffn_all.items() if k in ('in_proj_w', 'in_proj_b', 'out_proj_w', 'out_proj_b', 'ln1_w', 'ln1_b', 'lin1_w', 'lin1_b', 'lin2_w', 'lin2_b', 'ln2_w', 'ln2_b', 'gate_w', 'gate_b')}
    del _L1_ffn_all
    return {'x': x, 'ctx_1024': ctx_1024, 'mask_BxS2_ff1': mask_BxS2_ff1, 'L0_attn_Wq': _L0_attn_in['Wq'], 'L0_attn_Wk': _L0_attn_in['Wk'], 'L0_attn_Wv': _L0_attn_in['Wv'], 'L0_xattn_Wq': _L0_xattn_in['Wq'], 'L0_xattn_Wk': _L0_xattn_in['Wk'], 'L0_xattn_Wv': _L0_xattn_in['Wv'], 'L0_xattn_Wo': _L0_xattn_in['Wo'], 'L0_ffn_wqkv': _L0_ffn_in['wqkv'], 'L0_ffn_q_scale': _L0_ffn_in['q_scale'], 'L0_ffn_k_scale': _L0_ffn_in['k_scale'], 'L0_ffn_wo': _L0_ffn_in['wo'], 'L0_ffn_ln_g': _L0_ffn_in['ln_g'], 'L0_ffn_ln_b': _L0_ffn_in['ln_b'], 'L0_ffn_w1': _L0_ffn_in['w1'], 'L0_ffn_b1': _L0_ffn_in['b1'], 'L0_ffn_w2': _L0_ffn_in['w2'], 'L0_ffn_b2': _L0_ffn_in['b2'], 'L1_attn_W_kv_down': _L1_attn_in['W_kv_down'], 'L1_attn_W_k_up': _L1_attn_in['W_k_up'], 'L1_attn_W_v_up': _L1_attn_in['W_v_up'], 'L1_attn_W_q': _L1_attn_in['W_q'], 'L1_attn_W_q_rope': _L1_attn_in['W_q_rope'], 'L1_attn_W_k_rope': _L1_attn_in['W_k_rope'], 'L1_attn_W_o': _L1_attn_in['W_o'], 'L1_xattn_wq': _L1_xattn_in['wq'], 'L1_xattn_wk': _L1_xattn_in['wk'], 'L1_xattn_wv': _L1_xattn_in['wv'], 'L1_xattn_ln_gamma': _L1_xattn_in['ln_gamma'], 'L1_xattn_ln_beta': _L1_xattn_in['ln_beta'], 'L1_xattn_dense_w': _L1_xattn_in['dense_w'], 'L1_xattn_dense_b': _L1_xattn_in['dense_b'], 'L1_ffn_in_proj_w': _L1_ffn_in['in_proj_w'], 'L1_ffn_in_proj_b': _L1_ffn_in['in_proj_b'], 'L1_ffn_out_proj_w': _L1_ffn_in['out_proj_w'], 'L1_ffn_out_proj_b': _L1_ffn_in['out_proj_b'], 'L1_ffn_ln1_w': _L1_ffn_in['ln1_w'], 'L1_ffn_ln1_b': _L1_ffn_in['ln1_b'], 'L1_ffn_lin1_w': _L1_ffn_in['lin1_w'], 'L1_ffn_lin1_b': _L1_ffn_in['lin1_b'], 'L1_ffn_lin2_w': _L1_ffn_in['lin2_w'], 'L1_ffn_lin2_b': _L1_ffn_in['lin2_b'], 'L1_ffn_ln2_w': _L1_ffn_in['ln2_w'], 'L1_ffn_ln2_b': _L1_ffn_in['ln2_b'], 'L1_ffn_gate_w': _L1_ffn_in['gate_w'], 'L1_ffn_gate_b': _L1_ffn_in['gate_b']}

def reference(x, ctx_1024, mask_BxS2_ff1, L0_attn_Wq, L0_attn_Wk, L0_attn_Wv, L0_xattn_Wq, L0_xattn_Wk, L0_xattn_Wv, L0_xattn_Wo, L0_ffn_wqkv, L0_ffn_q_scale, L0_ffn_k_scale, L0_ffn_wo, L0_ffn_ln_g, L0_ffn_ln_b, L0_ffn_w1, L0_ffn_b1, L0_ffn_w2, L0_ffn_b2, L1_attn_W_kv_down, L1_attn_W_k_up, L1_attn_W_v_up, L1_attn_W_q, L1_attn_W_q_rope, L1_attn_W_k_rope, L1_attn_W_o, L1_xattn_wq, L1_xattn_wk, L1_xattn_wv, L1_xattn_ln_gamma, L1_xattn_ln_beta, L1_xattn_dense_w, L1_xattn_dense_b, L1_ffn_in_proj_w, L1_ffn_in_proj_b, L1_ffn_out_proj_w, L1_ffn_out_proj_b, L1_ffn_ln1_w, L1_ffn_ln1_b, L1_ffn_lin1_w, L1_ffn_lin1_b, L1_ffn_lin2_w, L1_ffn_lin2_b, L1_ffn_ln2_w, L1_ffn_ln2_b, L1_ffn_gate_w, L1_ffn_gate_b):
    import jax
    import jax.numpy as jnp

    def _L0_attn_ref(x, Wq, Wk, Wv):
        import jax, jax.numpy as jnp
        import numpy as np
        DIM_IN, DIM_K, DIM_V, NH = (128, 128, 128, 16)
        DK, DV = (DIM_K // NH, DIM_V // NH)
        B, S, _ = x.shape
        scale = 1.0 / np.sqrt(DK)
        q = (x @ Wq.T).reshape(B, S, NH, DK).transpose(0, 2, 1, 3)
        k = x @ Wk.T
        v = x @ Wv.T
        dist = jnp.einsum('bhqd,bkd->bhqk', q, k) * scale
        dist = jax.nn.softmax(dist, axis=-1)
        att = jnp.einsum('bhqk,bkd->bhqd', dist, v)
        return att.transpose(0, 2, 1, 3).reshape(B, S, DIM_V)

    def _L0_xattn_ref(x_q, x_kv, Wq, Wk, Wv, Wo):
        import jax, jax.numpy as jnp
        import numpy as np
        D_MODEL = 128
        NUM_HEADS = 16
        HEAD_DIM = D_MODEL // NUM_HEADS
        B, T = (4, 256)
        Bq, Tq, C = x_q.shape
        Tk = x_kv.shape[1]
        q = (x_q @ Wq.T).reshape(Bq, Tq, NUM_HEADS, HEAD_DIM).transpose(0, 2, 1, 3)
        k = (x_kv @ Wk.T).reshape(Bq, Tk, NUM_HEADS, HEAD_DIM).transpose(0, 2, 1, 3)
        v = (x_kv @ Wv.T).reshape(Bq, Tk, NUM_HEADS, HEAD_DIM).transpose(0, 2, 1, 3)
        scores = jnp.einsum('bhqd,bhkd->bhqk', q, k) / jnp.sqrt(jnp.asarray(HEAD_DIM, x_q.dtype))
        causal = jnp.triu(jnp.ones((Tq, Tk), bool), k=1)
        scores = jnp.where(causal, -jnp.inf, scores)
        attn = jax.nn.softmax(scores, axis=-1)
        out = jnp.einsum('bhqk,bhkd->bhqd', attn, v)
        out = out.transpose(0, 2, 1, 3).reshape(Bq, Tq, C)
        return out @ Wo.T

    def _L0_ffn_ref(x, wqkv, q_scale, k_scale, wo, ln_g, ln_b, w1, b1, w2, b2):
        import jax, jax.numpy as jnp
        import numpy as np
        DIM = 128
        DEPTH = 2
        HEADS = 8
        DIM_HEAD = 64
        WINDOW = 64
        INNER = HEADS * DIM_HEAD
        HID = int(DIM * 4 * 2 / 3)
        B, N = (2, 1024)
        QK_SCALE = 8.0

        def shift_token(t):
            t1, t2 = jnp.split(t, 2, axis=-1)
            t2 = jnp.pad(t2, ((0, 0), (1, 0), (0, 0)))[:, :-1]
            return jnp.concatenate([t1, t2], axis=-1)

        def l2norm(t):
            return t / jnp.clip(jnp.linalg.norm(t, axis=-1, keepdims=True), 1e-12)

        def rotate_half(x):
            x1, x2 = jnp.split(x, 2, axis=-1)
            return jnp.concatenate([-x2, x1], axis=-1)

        def rotary_xpos(q, k):
            n = q.shape[-2]
            half_idx = jnp.arange(0, DIM_HEAD, 2, dtype=jnp.float32)
            inv_freq = 1.0 / 10000.0 ** (half_idx / DIM_HEAD)
            t = jnp.arange(n, dtype=jnp.float32)
            freqs = t[:, None] * inv_freq[None, :]
            freqs = jnp.concatenate([freqs, freqs], axis=-1)
            base = (half_idx + 0.4 * DIM_HEAD) / (1.4 * DIM_HEAD)
            power = (t - n // 2) / float(WINDOW // 2)
            scale = base[None, :] ** power[:, None]
            scale = jnp.concatenate([scale, scale], axis=-1)
            cos, sin = (jnp.cos(freqs), jnp.sin(freqs))
            q = q * cos * scale + rotate_half(q) * sin * scale
            k = k * cos / scale + rotate_half(k) * sin / scale
            return (q, k)

        def local_attention(q, k, v):
            b, h, n, d = q.shape
            w = n // WINDOW
            bq = q.reshape(b, h, w, WINDOW, d) * QK_SCALE
            bk = k.reshape(b, h, w, WINDOW, d)
            bv = v.reshape(b, h, w, WINDOW, d)

            def look_around(t):
                p = jnp.pad(t, ((0, 0), (0, 0), (1, 0), (0, 0), (0, 0)))
                return jnp.concatenate([p[:, :, :w], p[:, :, 1:]], axis=3)
            bk, bv = (look_around(bk), look_around(bv))
            bt = jnp.arange(n).reshape(w, WINDOW)
            btp = jnp.pad(bt, ((1, 0), (0, 0)), constant_values=-1)
            btk = jnp.concatenate([btp[:w], btp[1:]], axis=1)
            sim = jnp.einsum('bhwid,bhwjd->bhwij', bq, bk)
            i = bt[:, :, None]
            j = btk[:, None, :]
            mask = (i < j) | (i > j + WINDOW) | (j == -1)
            sim = jnp.where(mask, -jnp.finfo(sim.dtype).max, sim)
            attn = jax.nn.softmax(sim, axis=-1)
            out = jnp.einsum('bhwij,bhwjd->bhwid', attn, bv)
            return out.reshape(b, h, n, d)

        def _layer(x, wqkv, qs, ksc, wo, lg, lb, w1, b1, w2, b2):
            b, n, _ = x.shape
            h = shift_token(x)
            qkv = h @ wqkv
            q, k, v = jnp.split(qkv, 3, axis=-1)
            to_heads = lambda t: t.reshape(b, n, HEADS, DIM_HEAD).transpose(0, 2, 1, 3)
            q, k, v = (to_heads(q), to_heads(k), to_heads(v))
            q = l2norm(q) * qs
            k = l2norm(k) * ksc
            q, k = rotary_xpos(q, k)
            o = local_attention(q, k, v)
            o = o.transpose(0, 2, 1, 3).reshape(b, n, INNER)
            x = x + o @ wo
            h = shift_token(x)
            mu = h.mean(-1, keepdims=True)
            var = h.var(-1, keepdims=True)
            h = (h - mu) / jnp.sqrt(var + 1e-05) * lg + lb
            h = h @ w1 + b1
            a, g = jnp.split(h, 2, axis=-1)
            h = a * jax.nn.gelu(g, approximate=False)
            x = x + h @ w2 + b2
            return x
        for l in range(DEPTH):
            x = _layer(x, wqkv[l], q_scale[l], k_scale[l], wo[l], ln_g[l], ln_b[l], w1[l], b1[l], w2[l], b2[l])
        return x

    def _L1_attn_ref(x, W_kv_down, W_k_up, W_v_up, W_q, W_q_rope, W_k_rope, W_o):
        import jax, jax.numpy as jnp
        import numpy as np
        import math
        D_MODEL, D_C, D_R, NH = (128, 128, 32, 16)
        HD = D_MODEL // NH
        B, T = (2, 256)

        def _rope_tables(T, d_R):
            inv_freq = 1.0 / 10000.0 ** (jnp.arange(0, d_R, 2, dtype=jnp.float32) / d_R)
            t = jnp.arange(T, dtype=jnp.float32)
            freqs = jnp.outer(t, inv_freq)
            return (jnp.cos(freqs), jnp.sin(freqs))

        def _rotary_apply(x, cos, sin):
            d = x.shape[-1]
            x1, x2 = (x[..., :d // 2], x[..., d // 2:])
            return jnp.concatenate([x1 * cos - x2 * sin, x2 * cos + x1 * sin], axis=-1)
        Bb, Tt, _ = x.shape
        cos, sin = _rope_tables(Tt, D_R)
        cos = cos[None]
        sin = sin[None]
        c_kv = x @ W_kv_down
        k_rope = _rotary_apply(c_kv @ W_k_rope, cos, sin)
        k = (c_kv @ W_k_up).reshape(Bb, Tt, NH, HD)
        v = (c_kv @ W_v_up).reshape(Bb, Tt, NH, HD)
        q = (x @ W_q).reshape(Bb, Tt, NH, HD)
        q_rope = _rotary_apply(x @ W_q_rope, cos, sin)
        scale = math.sqrt(HD + D_R)
        scores = jnp.einsum('bqhd,bkhd->bhqk', q, k)
        scores = scores + jnp.einsum('bqr,bkr->bqk', q_rope, k_rope)[:, None]
        scores = scores / scale
        causal = jnp.triu(jnp.ones((Tt, Tt), dtype=bool), k=1)
        scores = jnp.where(causal[None, None], -jnp.inf, scores)
        w = jax.nn.softmax(scores, axis=-1)
        attn = jnp.einsum('bhqk,bkhd->bqhd', w, v).reshape(Bb, Tt, D_MODEL)
        return attn @ W_o

    def _L1_xattn_ref(q, k, v, mask, wq, wk, wv, ln_gamma, ln_beta, dense_w, dense_b):
        import jax, jax.numpy as jnp
        import numpy as np
        D_MODEL = 128
        HEADS = 16
        DEPTH = D_MODEL // HEADS
        B, S = (4, 512)
        EPS_K = 1e-06
        EPS_LN = 1e-06

        def _layernorm(x, g, b):
            m = jnp.mean(x, axis=-1, keepdims=True)
            var = jnp.var(x, axis=-1, keepdims=True)
            return (x - m) * jax.lax.rsqrt(var + EPS_LN) * g + b

        def _split_heads(x):
            bsz, sl, _ = x.shape
            return x.reshape(bsz, sl, HEADS, DEPTH).transpose(0, 2, 1, 3)
        bsz = q.shape[0]
        em = mask[:, None, :, None]
        qh = _split_heads(_layernorm(q @ wq, ln_gamma, ln_beta))
        kh = _split_heads(_layernorm(k @ wk, ln_gamma, ln_beta))
        vh = _split_heads(_layernorm(v @ wv, ln_gamma, ln_beta))
        q_prime = jax.nn.relu(qh) + EPS_K
        k_prime = (jax.nn.relu(kh) + EPS_K) * em
        vh = vh * em
        kv = jnp.einsum('bhnd,bhne->bhde', k_prime, vh)
        z = 1.0 / (jnp.einsum('bhnd,bhd->bhn', q_prime, k_prime.sum(axis=-2)) + EPS_K)
        att = jnp.einsum('bhnd,bhde,bhn->bhne', q_prime, kv, z)
        att = att.reshape(bsz, -1, D_MODEL)
        out = att @ dense_w + dense_b
        return _layernorm(out, ln_gamma, ln_beta)

    def _L1_ffn_ref(x, in_proj_w, in_proj_b, out_proj_w, out_proj_b, ln1_w, ln1_b, lin1_w, lin1_b, lin2_w, lin2_b, ln2_w, ln2_b, gate_w, gate_b):
        import jax, jax.numpy as jnp
        import numpy as np
        B, S, D = (8, 64, 128)
        H = 16
        DFF = 512
        E = 4
        K = 2
        EPS = 1e-05

        def _layernorm(x, w, b):
            m = x.mean(-1, keepdims=True)
            v = ((x - m) ** 2).mean(-1, keepdims=True)
            return (x - m) / jnp.sqrt(v + EPS) * w + b

        def _encoder_layer(x, iw, ib, ow, ob, l1w, l1b, l2w, l2b, n1w, n1b, n2w, n2b):
            b, s, d = x.shape
            hd = d // H
            qkv = x @ iw.T + ib
            q, k, v = jnp.split(qkv, 3, axis=-1)
            rs = lambda t: t.reshape(b, s, H, hd).transpose(0, 2, 1, 3)
            q, k, v = (rs(q), rs(k), rs(v))
            scale = jnp.asarray(hd, x.dtype) ** 0.5
            scores = jnp.einsum('bhqd,bhkd->bhqk', q, k) / scale
            attn = jax.nn.softmax(scores, axis=-1)
            o = jnp.einsum('bhqk,bhkd->bhqd', attn, v).transpose(0, 2, 1, 3).reshape(b, s, d)
            o = o @ ow.T + ob
            x = _layernorm(x + o, n1w, n1b)
            ff = jax.nn.relu(x @ l1w.T + l1b) @ l2w.T + l2b
            return _layernorm(x + ff, n2w, n2b)
        gate_logits = x.mean(axis=1) @ gate_w.T + gate_b
        _, top_idx = jax.lax.top_k(gate_logits, K)
        gate_weights = jax.nn.softmax(gate_logits, axis=-1)
        mask = jnp.zeros_like(gate_weights).at[jnp.arange(x.shape[0])[:, None], top_idx].set(1.0)
        expert_outs = jax.vmap(_encoder_layer, in_axes=(None, 0, 0, 0, 0, 0, 0, 0, 0, 0, 0, 0, 0))(x, in_proj_w, in_proj_b, out_proj_w, out_proj_b, lin1_w, lin1_b, lin2_w, lin2_b, ln1_w, ln1_b, ln2_w, ln2_b)
        return jnp.einsum('be,ebsd->bsd', gate_weights * mask, expert_outs)
    x = _layernorm(x + _L0_attn_ref(x, L0_attn_Wq, L0_attn_Wk, L0_attn_Wv), axis=-1)
    x = _layernorm(x + _L0_xattn_ref(x, ctx_1024, L0_xattn_Wq, L0_xattn_Wk, L0_xattn_Wv, L0_xattn_Wo), axis=-1)
    x = _layernorm(x + _L0_ffn_ref(x, L0_ffn_wqkv, L0_ffn_q_scale, L0_ffn_k_scale, L0_ffn_wo, L0_ffn_ln_g, L0_ffn_ln_b, L0_ffn_w1, L0_ffn_b1, L0_ffn_w2, L0_ffn_b2), axis=-1)
    x = _layernorm(x + _L1_attn_ref(x, L1_attn_W_kv_down, L1_attn_W_k_up, L1_attn_W_v_up, L1_attn_W_q, L1_attn_W_q_rope, L1_attn_W_k_rope, L1_attn_W_o), axis=-1)
    x = _layernorm(x + _L1_xattn_ref(x, ctx_1024, ctx_1024, mask_BxS2_ff1, L1_xattn_wq, L1_xattn_wk, L1_xattn_wv, L1_xattn_ln_gamma, L1_xattn_ln_beta, L1_xattn_dense_w, L1_xattn_dense_b), axis=-1)
    x = _layernorm(x + _L1_ffn_ref(x, L1_ffn_in_proj_w, L1_ffn_in_proj_b, L1_ffn_out_proj_w, L1_ffn_out_proj_b, L1_ffn_ln1_w, L1_ffn_ln1_b, L1_ffn_lin1_w, L1_ffn_lin1_b, L1_ffn_lin2_w, L1_ffn_lin2_b, L1_ffn_ln2_w, L1_ffn_ln2_b, L1_ffn_gate_w, L1_ffn_gate_b), axis=-1)
    return x

_drawn_inputs = setup_inputs


def setup_inputs(seed=0):
    import zlib

    import numpy as np

    out = dict(_drawn_inputs(seed))
    spreads = {'L0_ffn_q_scale': (1.0, 0.6),
     'L0_ffn_k_scale': (1.0, 0.6),
     'L0_ffn_ln_g': (1.0, 0.6),
     'L0_ffn_ln_b': (0.0, 0.8),
     'L0_ffn_b1': (0.0, 0.8),
     'L0_ffn_b2': (0.0, 0.1),
     'L1_xattn_ln_gamma': (1.0, 0.2),
     'L1_xattn_ln_beta': (0.0, 0.1),
     'L1_xattn_dense_b': (0.0, 0.1),
     'L1_ffn_ln1_w': (1.0, 0.2),
     'L1_ffn_ln1_b': (0.0, 0.34),
     'L1_ffn_ln2_w': (1.0, 0.2),
     'L1_ffn_ln2_b': (0.0, 0.301)}
    factors = {'L0_ffn_w1': 3.963,
     'L0_ffn_w2': 5.851,
     'L1_ffn_in_proj_w': 8.0,
     'L1_ffn_in_proj_b': 8.0,
     'L1_ffn_out_proj_w': 8.0,
     'L1_ffn_out_proj_b': 21.772,
     'L1_ffn_lin1_w': 3.797,
     'L1_ffn_lin1_b': 8.0,
     'L1_ffn_lin2_w': 3.081,
     'L1_ffn_lin2_b': 8.0,
     'L1_ffn_gate_b': 8.0}
    for name, (base, spread) in spreads.items():
        noise = np.random.default_rng([zlib.crc32(name.encode()), seed]).standard_normal(out[name].shape)
        drawn = base * np.exp(spread * noise) if base else spread * noise
        out[name] = jnp.asarray(drawn.astype(out[name].dtype))
    for name, factor in factors.items():
        out[name] = (out[name] * factor).astype(out[name].dtype)
    return out
```

```python
import numpy as np

import concourse.bass as bass
from concourse import mybir

F32 = mybir.dt.float32
BF16 = mybir.dt.bfloat16
ACT = mybir.ActivationFunctionType
ALU = mybir.AluOpType
AXX = mybir.AxisListType.X

B, S, D = 32, 128, 128
G = 4
NG = B // G
H, HD = 16, 8
HU = 4
NU = H // HU
LH, LD, WINDOW = 8, 64, 64
DEPTH = 2
HID = D * 4 * 2 // 3
HCH = [(0, 128), (128, 128), (256, HID - 256)]
RD = 32
E, DFF = 4, 512
NEG = -1.0e30
CREDIT = 8


class Memory:
    pass


def bcast(ap, dim, n):
    a = ap.unsqueeze(dim)
    shape = list(a.shape)
    shape[dim] = n
    return a.broadcast_to(shape)


class Signal:

    def __init__(self, nc, name):
        self.name = name
        self.sem = nc.alloc_semaphore(name)
        self.base = CREDIT

    def __call__(self, n):
        return self.sem, n + self.base


class Signals:

    def __init__(self, nc):
        self.all = []
        self.c_done = self.new(nc, "c_done")
        self.c_ready = self.new(nc, "c_ready")
        self.unit_done = self.new(nc, "unit_done")
        self.unit_ready = self.new(nc, "unit_ready")
        self.rotated = self.new(nc, "rotated")
        self.stats2 = self.new(nc, "stats2")
        self.means2 = self.new(nc, "means2")
        self.spread2 = self.new(nc, "spread2")
        self.vars2 = self.new(nc, "vars2")
        self.rstd2 = self.new(nc, "rstd2")
        self.nmean2 = self.new(nc, "nmean2")
        self.norm2 = self.new(nc, "norm2")
        self.g_steps = self.new(nc, "g_steps")
        self.g_compared = self.new(nc, "g_compared")
        self.g_rows = self.new(nc, "g_rows")
        self.fin_added = self.new(nc, "fin_added")
        self.em_ready = self.new(nc, "em_ready")
        self.zm_ready = self.new(nc, "zm_ready")
        self.scaled = self.new(nc, "scaled")
        self.based = self.new(nc, "based")
        self.kv_done = self.new(nc, "kv_done")
        self.kv_ready = self.new(nc, "kv_ready")
        self.at_done = self.new(nc, "at_done")
        self.z_added = self.new(nc, "z_added")
        self.z_ready = self.new(nc, "z_ready")
        self.at_ready = self.new(nc, "at_ready")
        self.at_turned = self.new(nc, "at_turned")
        self.att_ready = self.new(nc, "att_ready")
        self.ebias = self.new(nc, "ebias")
        self.h_done = self.new(nc, "h_done")
        self.h_ready = self.new(nc, "h_ready")
        self.res_added = self.new(nc, "res_added")
        self.fin_norm = self.new(nc, "fin_norm")
        self.fin_scaled = self.new(nc, "fin_scaled")
        self.fin_based = self.new(nc, "fin_based")
        self.tables = self.new(nc, "tables")
        self.xs_ready = self.new(nc, "xs_ready")
        self.ht_ready = self.new(nc, "ht_ready")
        self.q_sq = self.new(nc, "q_sq")
        self.k_sq = self.new(nc, "k_sq")
        self.q_rot = self.new(nc, "q_rot")
        self.k_rot = self.new(nc, "k_rot")
        self.q_ss = self.new(nc, "q_ss")
        self.k_ss = self.new(nc, "k_ss")
        self.q_norm = self.new(nc, "q_norm")
        self.k_norm = self.new(nc, "k_norm")
        self.q_turned = self.new(nc, "q_turned")
        self.k_turned = self.new(nc, "k_turned")
        self.floored = self.new(nc, "floored")
        self.powered = self.new(nc, "powered")
        self.parts_added = self.new(nc, "parts_added")
        self.biased = self.new(nc, "biased")
        self.x_shifted = self.new(nc, "x_shifted")
        self.shift_in = self.new(nc, "shift_in")
        self.g_done = self.new(nc, "g_done")
        self.a_done = self.new(nc, "a_done")
        self.gelued = self.new(nc, "gelued")
        self.gated = self.new(nc, "gated")
        self.staged = self.new(nc, "staged")
        self.v_staged = self.new(nc, "v_staged")
        self.oe_ready = self.new(nc, "oe_ready")
        self.o_turned = self.new(nc, "o_turned")
        self.scored = self.new(nc, "scored")
        self.maxed = self.new(nc, "maxed")
        self.shifted = self.new(nc, "shifted")
        self.exped = self.new(nc, "exped")
        self.turned = self.new(nc, "turned")
        self.pt_ready = self.new(nc, "pt_ready")
        self.mixed = self.new(nc, "mixed")
        self.inverted = self.new(nc, "inverted")
        self.divided = self.new(nc, "divided")
        self.added = self.new(nc, "added")
        self.on_turned = self.new(nc, "on_turned")
        self.ot_ready = self.new(nc, "ot_ready")
        self.projected = self.new(nc, "projected")
        self.xn_ready = self.new(nc, "xn_ready")
        self.x_turned = self.new(nc, "x_turned")
        self.xt_ready = self.new(nc, "xt_ready")
        self.xt_kept = self.new(nc, "xt_kept")
        self.x_kept = self.new(nc, "x_kept")
        self.q_done = self.new(nc, "q_done")
        self.k_done = self.new(nc, "k_done")
        self.v_done = self.new(nc, "v_done")
        self.q_ready = self.new(nc, "q_ready")
        self.k_ready = self.new(nc, "k_ready")
        self.v_ready = self.new(nc, "v_ready")
        self.stats = self.new(nc, "stats")
        self.means = self.new(nc, "means")
        self.spread = self.new(nc, "spread")
        self.vars = self.new(nc, "vars")
        self.rstd = self.new(nc, "rstd")
        self.nmean = self.new(nc, "nmean")
        self.summed = self.new(nc, "summed")
        self.stored = self.new(nc, "stored")
        self.ct_loaded = [self.new(nc, "ct_loaded0"), self.new(nc, "ct_loaded1")]
        self.second = Memory()
        self.second.stats, self.second.means, self.second.spread = self.stats2, self.means2, self.spread2
        self.second.vars, self.second.rstd, self.second.nmean = self.vars2, self.rstd2, self.nmean2

    def new(self, nc, name):
        self.all.append(Signal(nc, name))
        return self.all[-1]

    def close(self, **counts):
        for signal in self.all:
            signal.base += counts.get(signal.name, 0)


def pipeline(eng, n, depth, step):
    head = (depth - 1) + (depth - 1) % 2
    for k in range(head):
        step(k, k % 2, [0 <= k - d < n for d in range(depth)])
    with eng.Fori(head // 2, n // 2) as i:
        for p in range(2):
            step(i * 2 + p, p, [True] * depth)
    for k in range(n, n + depth - 1):
        step(k, k % 2, [0 <= k - d < n for d in range(depth)])


def dyn(start, size):
    return slice(start, start + size) if isinstance(start, int) else bass.ds(start, size)


def columns(parts):
    place, at = {}, 0
    for name, n in parts:
        place[name] = (at, n)
        at += n
    return place, at


CONSTS = [("ident", D), ("kmask", HU), ("kmask_wide", HU), ("qmask", NU), ("qmask_wide", 2), ("causal", S), ("band", S), ("shift", S),
          ("ones", D), ("blocks_sel", D + H), ("qcos", LD), ("qsin", LD), ("kcos", LD), ("ksin", LD),
          ("ropecos", S), ("ropesin", S), ("minus_half", 16), ("place", 4 * H), ("block", HD), ("lower", E * E),
          ("seqsel", B * E)]
FFN = [("wqkv", 3 * LH * LD), ("qs", LD), ("ks", LD), ("wo", LH * LD), ("lg", 1), ("lb", 1), ("w1", 2 * HID),
       ("b1", 6), ("w2", 3 * D), ("b2", D)]
EXPERT = [("wq", D), ("wk", D), ("wv", D), ("bq", 1), ("bk", 1), ("bv", D), ("ow", D), ("ob", D), ("n1w", D),
          ("n1b", D), ("n1wc", 1), ("n1bc", 1), ("l1", DFF), ("l1b", DFF // D), ("l2", DFF), ("l2b", D), ("n2w", D), ("n2b", D)]
WEIGHTS = ([("a_wq", D), ("a_wk", D), ("a_wv", D), ("x_wq", D), ("x_wk", D), ("x_wv", D), ("x_wo", D)]
           + [(f"f{d}_{n}", w) for d in range(DEPTH) for n, w in FFN]
           + [("m_down", D), ("m_q", 3 * D), ("m_k", 3 * D), ("m_v", D), ("m_o", D)]
           + [("y_wq", D), ("y_wkv", 2 * D), ("y_gamma", D), ("y_beta", D), ("y_dw", D), ("y_db", D),
              ("em", B)]
           + [("gate_w", E), ("gate_b", E)])
CPLACE, CCOLS = columns(CONSTS)
WPLACE, WCOLS = columns(WEIGHTS)
EPLACE, ECOLS = columns(EXPERT)


def attention(nc, m, s, *, causal, scale, wide, w_out, target):
    kmask = m.c("kmask_wide") if wide else m.c("kmask")

    with nc.Block() as block:
        @block.gpsimd
        def _(pool):
            def stage(b, p, on):
                pool.wait_ge(*s.scored((b - 1) * NU))
                if wide:
                    qkt = m.QKT[:, dyn(b, 1), :].rearrange("p a (t s) -> p (a t) s", t=4)
                    pool.tensor_tensor(m.QS[:, p].rearrange("p (t h) s -> p t h s", h=2),
                                       bcast(qkt[:, 0:2, :], 2, 2),
                                       bcast(bcast(m.c("qmask_wide"), 1, 2), 3, S), ALU.mult)
                    for t in range(2):
                        last = pool.tensor_tensor(m.KM[:, p, t], bcast(qkt[:, 2 + t, :], 1, HU),
                                                  bcast(kmask, 2, S), ALU.mult)
                    last.then_inc(s.staged.sem, 1)
                else:
                    pool.tensor_tensor(m.QS[:, p], bcast(m.QT[:, dyn(b * S, S)], 1, NU),
                                       bcast(m.c("qmask"), 2, S), ALU.mult)
                    pool.tensor_tensor(m.KM[:, p, 0], bcast(m.KT[:, dyn(b * S, S)], 1, HU), bcast(kmask, 2, S),
                                       ALU.mult).then_inc(s.staged.sem, 1)
                pool.wait_ge(*s.mixed((b - 1) * NU))
                pool.tensor_copy(m.VS[:, p, :, 0:HD], m.V[:, dyn(b, 1), :, :].rearrange("p a h d -> p (a h) d")
                                 ).then_inc(s.v_staged.sem, 1)
            pipeline(pool, B, 1, stage)

        @block.tensor
        def _(pe):
            def mix(b, q, r):
                pe.wait_ge(*s.pt_ready(b * NU + r + 1))
                if r == 0:
                    pe.wait_ge(*s.v_staged(b + 1))
                    pe.wait_ge(*s.oe_ready(b))
                for j in range(HU):
                    last = pe.matmul(m.ps[6][32 * j:32 * j + 32, r * S:(r + 1) * S], m.VS[:, q, r * HU + j, :],
                                     m.PT[:, r % 2, j * S:(j + 1) * S], start=True, stop=True,
                                     skip_group_check=True)
                last.then_inc(s.mixed.sem, 1)

            def step(k, p, on):
                b, q = k - 1, 1 - p
                for r in range(NU):
                    if w_out is not None and on[3] and r == 0:
                        pe.wait_ge(*s.divided(k - 2))
                        pe.transpose(m.ps[7][:, 0:S], m.ON[:, q, :], m.c("ident")).then_inc(s.on_turned.sem, 1)
                    if w_out is not None and on[3] and r == 1:
                        pe.wait_ge(*s.ot_ready(k - 2))
                        pe.matmul(m.ps[7][:, 0:D], m.OT[:, :], w_out, start=True,
                                  stop=True).then_inc(s.projected.sem, 1)
                    if on[1]:
                        pe.wait_ge(*s.exped(b * NU + r + 1))
                        pe.wait_ge(*s.pt_ready(b * NU + r - 1))
                        for j in range(HU):
                            last = pe.transpose(m.ps[4 + r % 2][:, j * S:(j + 1) * S],
                                                m.PR[:, r, j * S:(j + 1) * S], m.c("ident"))
                        last.then_inc(s.turned.sem, 1)
                    if on[0]:
                        pe.wait_ge(*s.staged(k + 1))
                        pe.wait_ge(*s.shifted(k * NU + r - NU + 1))
                        if causal:
                            pe.matmul(m.ps[r][:, :], m.ident_bf[:, :], bcast(m.causal_bf[:, :], 1, HU),
                                      start=True, stop=False)
                        pe.matmul(m.ps[r][:, :], m.QS[:, p, r, :],
                                  m.KM[:, p, r // 2 if wide else 0].rearrange("p j s -> p (j s)"),
                                  start=not causal, stop=True).then_inc(s.scored.sem, 1)
                    if r > 0 and on[1]:
                        mix(b, q, r - 1)
                    if r == 0 and on[2]:
                        mix(k - 2, p, NU - 1)
                    if on[2] and r == 2:
                        pe.wait_ge(*s.oe_ready(k - 1))
                        pe.wait_ge(*(s.added if w_out is not None else s.divided)(k - 2))
                        for u in range(NU):
                            last = pe.transpose(m.ps[7][:, u * S:(u + 1) * S], m.OE[:, u * S:(u + 1) * S],
                                                m.c("ident"))
                        last.then_inc(s.o_turned.sem, 1)
            pipeline(pe, B, 4, step)

        @block.scalar
        def _(act):
            def evacuate(b, r):
                act.wait_ge(*s.turned(b * NU + r + 1))
                act.wait_ge(*s.mixed(b * NU + r - 1))
                act.activation(m.PT[:, r % 2, :], m.ps[4 + r % 2][:, :], ACT.Copy).then_inc(s.pt_ready.sem, 1)

            def exp(b, r):
                act.wait_ge(*s.shifted(b * NU + r + 1))
                act.activation(m.PR[:, r, :], m.PR[:, r, :], ACT.Exp, scale=scale).then_inc(s.exped.sem, 1)

            def step(k, p, on):
                for r in range(NU):
                    if on[1]:
                        evacuate(k - 1, r)
                    if w_out is not None and on[3] and r == 0:
                        act.wait_ge(*s.on_turned(k - 2))
                        act.activation(m.OT[:, :], m.ps[7][:, 0:S], ACT.Copy).then_inc(s.ot_ready.sem, 1)
                    if r < 2 and on[1]:
                        exp(k - 1, r + 2)
                    if r >= 2 and on[0]:
                        exp(k, r - 2)
                    if on[2] and r == 0:
                        act.wait_ge(*s.mixed((k - 1) * NU))
                        act.wait_ge(*s.o_turned(k - 2))
                        act.activation(m.OE[:, :], m.ps[6][:, :], ACT.Copy).then_inc(s.oe_ready.sem, 1)
            pipeline(act, B, 4, step)

        @block.vector
        def _(dve):
            def maximum(b, r):
                dve.wait_ge(*s.scored(b * NU + r + 1))
                dve.tensor_reduce(m.mx[:, r, :], m.ps[r][:, :].rearrange("p (j s) -> p j s", j=HU),
                                  AXX, ALU.max).then_inc(s.maxed.sem, 1)

            def shift(b, r):
                dve.wait_ge(*s.maxed(b * NU + r + 1))
                dve.wait_ge(*s.turned(b * NU + r - NU + 1))
                dve.tensor_tensor(m.PR[:, r, :].rearrange("p (j s) -> p j s", j=HU),
                                  m.ps[r][:, :].rearrange("p (j s) -> p j s", j=HU),
                                  bcast(m.mx[:, r, :], 2, S), ALU.subtract).then_inc(s.shifted.sem, 1)

            def divide(b, p):
                dve.wait_ge(*s.o_turned(b + 1))
                o = m.ps[7][:, :].rearrange("p (h d) -> p h d", h=H)
                dve.reciprocal(m.rs[:, :], o[:, :, HD]).then_inc(s.inverted.sem, 1)
                dve.wait_ge(*s.inverted(b + 1))
                if w_out is not None:
                    dve.wait_ge(*s.on_turned(b - 1))
                dve.tensor_tensor(m.ON[:, p, :].rearrange("p (h d) -> p h d", h=H), o[:, :, 0:HD],
                                  bcast(m.rs[:, :], 2, HD), ALU.mult).then_inc(s.divided.sem, 1)

            def add(b, p):
                x = m.X[:, dyn(b, 1), :].rearrange("p a d -> p (a d)")
                if w_out is not None:
                    dve.wait_ge(*s.projected(b + 1))
                    src = m.ps[7][:, 0:D]
                else:
                    dve.wait_ge(*s.divided(b + 1))
                    src = m.ON[:, p, :]
                dst = x if target == "x" else m.QT[:, dyn(b * S, S)]
                dve.tensor_tensor(dst, src, x, ALU.add).then_inc(s.added.sem, 1)

            def step(k, p, on):
                for r in range(NU):
                    if r == 1 and on[3]:
                        add(k - 3, 1 - p)
                    if r == 3 and on[2]:
                        divide(k - 2, p)
                    if on[0]:
                        maximum(k, r)
                        shift(k, r)
            pipeline(dve, B, 4, step)
    s.close(staged=B, v_staged=B, scored=NU * B, maxed=NU * B, shifted=NU * B, exped=NU * B, turned=NU * B,
            pt_ready=NU * B, mixed=NU * B, oe_ready=B, o_turned=B, inverted=B, divided=B, added=B)
    if w_out is not None:
        s.close(on_turned=B, ot_ready=B, projected=B)


def layernorm_on(dve, m, s, g, p, n, src, dst, eps):
    for j in range(n):
        last = dve.bn_stats(m.st[:, p, j, :], src(j))
    last.then_inc(s.stats.sem, 1)
    dve.wait_ge(*s.stats(g + 1))
    st = m.st[:, p, 0:n, :]
    dve.tensor_tensor(m.df[:, p, 0:n], st[:, :, 1], st[:, :, 4], ALU.subtract)
    dve.tensor_tensor(m.sm[:, p, 0:n], st[:, :, 1], st[:, :, 4], ALU.add)
    dve.scalar_tensor_tensor(m.cv[:, p, 0:n], st[:, :, 2], eps * D, st[:, :, 5], ALU.add,
                             ALU.add).then_inc(s.means.sem, 1)
    dve.wait_ge(*s.means(g + 1))
    dve.scalar_tensor_tensor(m.dd[:, p, 0:n], m.df[:, p, 0:n], 0.25, m.df[:, p, 0:n], ALU.mult,
                             ALU.mult).then_inc(s.spread.sem, 1)
    dve.wait_ge(*s.spread(g + 1))
    dve.scalar_tensor_tensor(m.ve[:, p, 0:n], m.cv[:, p, 0:n], 1.0 / D, m.dd[:, p, 0:n], ALU.mult,
                             ALU.add).then_inc(s.vars.sem, 1)
    dve.wait_ge(*s.rstd(g + 1))
    dve.scalar_tensor_tensor(m.nm[:, p, 0:n], m.sm[:, p, 0:n], -0.5, m.rv[:, p, 0:n], ALU.mult,
                             ALU.mult).then_inc(s.nmean.sem, 1)
    dve.wait_ge(*s.nmean(g + 1))
    for j in range(n):
        last = dve.tensor_scalar(dst(j), src(j), m.rv[:, p, j:j + 1], m.nm[:, p, j:j + 1], ALU.mult, ALU.add)
    return last


def rstd_on(pool, m, s, g, p, n):
    pool.wait_ge(*s.vars(g + 1))
    pool.tensor_tensor(m.rv[:, p, 0:n], m.ve[:, p, 0:n], m.c("minus_half")[:, 0:n], ALU.pow).then_inc(s.rstd.sem, 1)


def project(nc, m, s, *, ln, source, ctx, wq, wk, wv, bq=None, bk=None, bv=None, keep=False):
    with nc.Block() as block:
        if ctx is not None:
            @block.sync
            def _(sp):
                def step(g, p, on):
                    sp.wait_ge(*s.v_done(g - 1))
                    sp.dma_start(m.CT[:, p, :], ctx[:, dyn(g * G * S, G * S)]).then_inc(s.ct_loaded[p].sem, 16)
                pipeline(sp, NG, 1, step)

        @block.gpsimd
        def _(pool):
            def step(g, p, on):
                x = m.X[:, dyn(g * G, G), :]
                if source == "xt":
                    pool.wait_ge(*s.v_done(g - 1))
                    pool.tensor_copy(m.XT[:, p, :], m.XTA[:, dyn(g * G * S, G * S)]).then_inc(s.xt_ready.sem, 1)
                elif ln:
                    rstd_on(pool, m, s, g, p, G)
                    pool.wait_ge(*s.xn_ready(g + 1))
                    pool.tensor_copy(x, m.XN[:, p]).then_inc(s.x_kept.sem, 1)
                else:
                    pool.wait_ge(*s.x_turned(g - 1))
                    pool.tensor_copy(m.XN[:, p], x).then_inc(s.xn_ready.sem, 1)
                if keep:
                    pool.wait_ge(*s.xt_ready(g + 1))
                    pool.tensor_copy(m.XTA[:, dyn(g * G * S, G * S)], m.XT[:, p, :]).then_inc(s.xt_kept.sem, 1)
            pipeline(pool, NG, 1, step)

        @block.tensor
        def _(pe):
            def turn(g, p):
                pe.wait_ge(*s.xn_ready(g + 1))
                pe.wait_ge(*s.xt_ready(g - 1))
                for j in range(G):
                    last = pe.transpose(m.ps[p][:, j * S:(j + 1) * S], m.XN[:, p, j, :], m.c("ident"))
                last.then_inc(s.x_turned.sem, 1)

            def keys_values(g, p, src):
                pe.wait_ge(*s.k_ready(g - 1))
                pe.matmul(m.ps[4 + p][:, :], wk, src[:, p, :], start=True, stop=True).then_inc(s.k_done.sem, 1)
                pe.wait_ge(*s.v_ready(g - 1))
                for j in range(G):
                    last = pe.matmul(m.ps[6 + p][:, j * D:(j + 1) * D], src[:, p, j * S:(j + 1) * S], wv,
                                     start=True, stop=True)
                last.then_inc(s.v_done.sem, 1)

            def step(k, p, on):
                if source == "x" and on[0]:
                    turn(k, p)
                if on[1]:
                    g, q = k - 1, 1 - p
                    if ctx is not None:
                        pe.wait_ge(s.ct_loaded[q].sem, (k - 1 - q) * 8 + 16 + s.ct_loaded[q].base)
                        keys_values(g, q, m.CT)
                    pe.wait_ge(*s.xt_ready(g + 1))
                    pe.wait_ge(*s.q_ready(g - 1))
                    pe.matmul(m.ps[2 + q][:, :], wq, m.XT[:, q, :], start=True, stop=True).then_inc(s.q_done.sem, 1)
                    if ctx is None:
                        keys_values(g, q, m.XT)
            pipeline(pe, NG, 2, step)

        @block.scalar
        def _(act):
            def step(k, p, on):
                if source == "x" and on[0]:
                    act.wait_ge(*s.x_turned(k + 1))
                    act.wait_ge(*s.q_done(k - 1))
                    act.wait_ge(*s.v_done(k - 1))
                    if keep:
                        act.wait_ge(*s.xt_kept(k - 1))
                    act.activation(m.XT[:, p, :], m.ps[p][:, :], ACT.Copy).then_inc(s.xt_ready.sem, 1)
                if on[1]:
                    g, q = k - 1, 1 - p
                    cols = dyn(g * (G * S), G * S)
                    act.wait_ge(*s.q_done(g + 1))
                    if bq is None:
                        act.activation(m.QT[:, cols], m.ps[2 + q][:, :], ACT.Copy).then_inc(s.q_ready.sem, 1)
                    else:
                        act.activation(m.QT[:, cols], m.ps[2 + q][:, :], ACT.Identity,
                                       bias=bq).then_inc(s.q_ready.sem, 1)
                    act.wait_ge(*s.k_done(g + 1))
                    if bk is None:
                        act.activation(m.KT[:, cols], m.ps[4 + q][:, :], ACT.Copy).then_inc(s.k_ready.sem, 1)
                    else:
                        act.activation(m.KT[:, cols], m.ps[4 + q][:, :], ACT.Identity,
                                       bias=bk).then_inc(s.k_ready.sem, 1)
                    if bv is None:
                        act.wait_ge(*s.v_done(g + 1))
                        act.activation(m.V[:, dyn(g * G, G), :, 0:HD],
                                       m.ps[6 + q][:, :].rearrange("p (b h d) -> p b h d", b=G, h=H),
                                       ACT.Copy).then_inc(s.v_ready.sem, 1)
            pipeline(act, NG, 2, step)

        @block.vector
        def _(dve):
            def step(k, p, on):
                if ln and on[0]:
                    x = lambda j: m.X[:, dyn(k * G + j, 1), :].rearrange("p a d -> p (a d)")
                    dve.wait_ge(*s.x_turned(k - 1))
                    dve.wait_ge(*s.x_kept(k - 1))
                    layernorm_on(dve, m, s, k, p, G, x, lambda j: m.XN[:, p, j, :], 1e-5).then_inc(s.xn_ready.sem, 1)
                if bv is not None and on[1]:
                    g, q = k - 1, 1 - p
                    dve.wait_ge(*s.v_done(g + 1))
                    for j in range(G):
                        last = dve.tensor_tensor(
                            m.V[:, dyn(g * G + j, 1), :, 0:HD].rearrange("p a h d -> p (a h) d"),
                            m.ps[6 + q][:, j * D:(j + 1) * D].rearrange("p (h d) -> p h d", h=H),
                            bv.rearrange("p (h d) -> p h d", h=H), ALU.add)
                    last.then_inc(s.v_ready.sem, 1)
            if ln or bv is not None:
                pipeline(dve, NG, 2, step)
    s.close(q_done=NG, k_done=NG, v_done=NG, q_ready=NG, k_ready=NG, v_ready=NG, xt_ready=NG)
    if source == "x":
        s.close(xn_ready=NG, x_turned=NG)
    if ln:
        s.close(stats=NG, means=NG, spread=NG, vars=NG, rstd=NG, nmean=NG, x_kept=NG)
    if keep:
        s.close(xt_kept=NG)
    if ctx is not None:
        for q in range(2):
            s.ct_loaded[q].base += 16 * (NG // 2)


def local_attention(nc, m, s, d):
    W = LH // 2
    wqkv, wo = m.w(f"f{d}_wqkv"), m.w(f"f{d}_wo")
    half = LD // 2
    fields = m.local

    with nc.Block() as block:
        @block.vector
        def _(dve):
            for i, (co, si, sc) in enumerate((("qcos", "qsin", "qs"), ("kcos", "ksin", "ks"))):
                sc = m.w(f"f{d}_{sc}")
                dve.tensor_tensor(fields.straight[:, i, :], m.c(co), sc, ALU.mult)
                dve.tensor_tensor(fields.swapped[:, i, 0:half], m.c(si)[:, 0:half], sc[:, half:LD], ALU.mult)
                dve.tensor_tensor(fields.swapped[:, i, half:LD], m.c(si)[:, half:LD], sc[:, 0:half],
                                  ALU.mult).then_inc(s.tables.sem, 1)

        @block.gpsimd
        def _(pool):
            pool.memset(fields.HT[:, :, 0:1], 0.0)
            pool.memset(fields.QZ[:, :, :], 0.0)
            pool.memset(fields.V[:, :, :, LD:LD + 1], 1.0)
    s.close(tables=2)

    with nc.Block() as block:
        @block.gpsimd
        def _(pool):
            def finish(i, b, p, rotated, summed, turned, normed):
                pool.wait_ge(*rotated(b + 1))
                pool.wait_ge(*turned(b - 1))
                pool.tensor_tensor(fields.QN[:, p, i], fields.T1[:, i], fields.T2[:, i],
                                   ALU.add).then_inc(s.parts_added.sem, 1)
                pool.wait_ge(*summed(b + 1))
                pool.tensor_tensor(fields.RN[:, i], fields.SS[:, i], m.c("minus_half")[:, 0:LH],
                                   ALU.pow).then_inc(s.powered.sem, 1)
                pool.wait_ge(*s.powered(2 * b + i + 1))
                pool.wait_ge(*s.parts_added(2 * b + i + 1))
                qn = fields.QN[:, p, i].rearrange("p (h d) -> p h d", h=LH)
                pool.tensor_tensor(qn, qn, bcast(fields.RN[:, i], 2, LD), ALU.mult).then_inc(normed.sem, 1)

            def step(k, p, on):
                if on[0]:
                    pool.wait_ge(*s.x_turned(k - 1))
                    pool.tensor_copy(fields.XS[:, p, :], m.X[:, dyn(k, 1), :].rearrange("p a d -> p (a d)")
                                     ).then_inc(s.xs_ready.sem, 1)
                if on[1]:
                    finish(0, k - 1, 1 - p, s.q_rot, s.q_ss, s.q_turned, s.q_norm)
                    finish(1, k - 1, 1 - p, s.k_rot, s.k_ss, s.k_turned, s.k_norm)
            pipeline(pool, B, 2, step)

        @block.tensor
        def _(pe):
            def project_to(bank, at, q, done):
                pe.matmul(m.ps[bank][:, :], fields.HT[:, q, :], wqkv[:, at * LH * LD:(at + 1) * LH * LD],
                          start=True, stop=True).then_inc(done.sem, 1)

            def scores(b, u):
                pe.matmul(m.ps[4 + u][:, :], m.ident_bf[:, :], bcast(m.band_bf[:, :], 1, W),
                          start=True, stop=False, skip_group_check=True)
                for j in range(W):
                    h = u * W + j
                    last = pe.matmul(m.ps[4 + u][:, j * S:(j + 1) * S], fields.QZ[:, h, :],
                                     fields.KT[:, h // 2, :], start=False, stop=j == W - 1, skip_group_check=True)
                last.then_inc(s.scored.sem, 1)

            def turn_probs(b, u):
                pe.wait_ge(*s.exped(2 * b + u + 1))
                for j in range(W):
                    last = pe.transpose(m.ps[6 - 2 * u][:, j * S:(j + 1) * S], fields.PR[:, u, j * S:(j + 1) * S],
                                        m.c("ident"))
                last.then_inc(s.turned.sem, 1)

            def mix(b, p, u):
                pe.wait_ge(*s.pt_ready(2 * b + u + 1))
                for j in range(W):
                    last = pe.matmul(m.ps[7 if u == 0 else 2][:, j * (LD + 1):(j + 1) * (LD + 1)],
                                     fields.PT[:, u, j * S:(j + 1) * S], fields.V[:, p, u * W + j, :],
                                     start=True, stop=True)
                last.then_inc(s.mixed.sem, 1)

            def step(k, p, on):
                b, c, q = k - 2, k - 3, 1 - p
                if on[1]:
                    pe.wait_ge(*s.ht_ready(k))
                    project_to(0, 0, q, s.q_done)
                if on[4]:
                    pe.wait_ge(*s.ot_ready(k - 3))
                    for i in range(4):
                        last = pe.matmul(m.ps[3][:, 0:D], fields.OT[:, i * S:(i + 1) * S], wo[:, i * D:(i + 1) * D],
                                         start=i == 0, stop=i == 3)
                    last.then_inc(s.projected.sem, 1)
                if on[3]:
                    pe.wait_ge(*s.k_ready(c + 1))
                    turn_probs(c, 0)
                if on[1]:
                    pe.wait_ge(*s.k_rot(k - 1))
                    project_to(1, 1, q, s.k_done)
                if on[3]:
                    pe.wait_ge(*s.v_ready(c + 1))
                    pe.wait_ge(*s.divided(2 * c - 1))
                    turn_probs(c, 1)
                    mix(c, q, 0)
                if on[0]:
                    pe.wait_ge(*s.xs_ready(k + 1))
                    pe.wait_ge(*s.q_rot(k))
                    pe.transpose(m.ps[0][:, 0:S], fields.XS[:, p, :], m.c("ident")).then_inc(s.x_turned.sem, 1)
                if on[2]:
                    pe.wait_ge(*s.q_norm(b + 1))
                    pe.wait_ge(*s.added(k - 3))
                    for i in range(4):
                        last = pe.transpose(m.ps[3][:, i * S:(i + 1) * S], fields.QN[:, p, 0, i * S:(i + 1) * S],
                                            m.c("ident"))
                    last.then_inc(s.q_turned.sem, 1)
                    pe.wait_ge(*s.k_norm(b + 1))
                    pe.wait_ge(*s.pt_ready(2 * b - 1))
                    for i in range(4):
                        last = pe.transpose(m.ps[6][:, i * S:(i + 1) * S], fields.QN[:, p, 1, i * S:(i + 1) * S],
                                            m.c("ident"))
                    last.then_inc(s.k_turned.sem, 1)
                if on[3]:
                    if on[2]:
                        pe.wait_ge(*s.v_ready(k - 1))
                    mix(c, q, 1)
                if on[2]:
                    pe.wait_ge(*s.pt_ready(2 * b))
                    pe.wait_ge(*s.q_ready(b + 1))
                    pe.wait_ge(*s.k_ready(b + 1))
                    pe.wait_ge(*s.shifted(2 * b))
                    scores(b, 0)
                    scores(b, 1)
                if on[1]:
                    if on[3]:
                        pe.wait_ge(*s.divided(2 * c + 2))
                    pe.wait_ge(*s.v_ready(k - 1))
                    project_to(2, 2, q, s.v_done)
                if on[3]:
                    if on[2]:
                        pe.wait_ge(*s.q_ready(k - 1))
                    pe.wait_ge(*s.divided(2 * c + 2))
                    for i in range(4):
                        last = pe.transpose(m.ps[3][:, i * S:(i + 1) * S], fields.ON[:, i * S:(i + 1) * S],
                                            m.c("ident"))
                    last.then_inc(s.on_turned.sem, 1)
            pipeline(pe, B, 5, step)

        @block.scalar
        def _(act):
            def squares(i, b, done, summed, squared):
                act.wait_ge(*done(b + 1))
                act.wait_ge(*summed(b))
                act.activation(fields.SQ[:, i], m.ps[i][:, :], ACT.Square).then_inc(squared.sem, 1)

            def exp(b, u):
                act.wait_ge(*s.shifted(2 * b + u + 1))
                act.activation(fields.PR[:, u, :], fields.PR[:, u, :], ACT.Exp, scale=8.0).then_inc(s.exped.sem, 1)

            def evacuate(b, u):
                act.wait_ge(*s.turned(2 * b + u + 1))
                act.wait_ge(*s.mixed(2 * b + u - 1))
                act.activation(fields.PT[:, u, :], m.ps[6 - 2 * u][:, :], ACT.Copy).then_inc(s.pt_ready.sem, 1)

            def step(k, p, on):
                b, c = k - 2, k - 3
                if on[1]:
                    squares(0, k - 1, s.q_done, s.q_ss, s.q_sq)
                if on[3]:
                    evacuate(c, 0)
                if on[1]:
                    squares(1, k - 1, s.k_done, s.k_ss, s.k_sq)
                if on[3]:
                    evacuate(c, 1)
                if on[0]:
                    act.wait_ge(*s.x_turned(k + 1))
                    act.wait_ge(*s.v_done(k - 1))
                    act.activation(fields.HT[0:64, p, :], m.ps[0][0:64, 0:S], ACT.Copy)
                    act.activation(fields.HT[64:128, p, 1:S], m.ps[0][64:128, 0:S - 1],
                                   ACT.Copy).then_inc(s.ht_ready.sem, 1)
                if on[2]:
                    act.wait_ge(*s.q_turned(b + 1))
                    act.wait_ge(*s.scored(2 * b))
                    qz = fields.QZ[:, :, :].rearrange("p (c w) s -> p c w s", w=2)
                    qt = m.ps[3][:, :].rearrange("p (c s) -> p c s", c=4)
                    act.activation(qz[0:64, :, 0, :], qt[0:64], ACT.Copy)
                    act.activation(qz[64:128, :, 1, :], qt[64:128], ACT.Copy).then_inc(s.q_ready.sem, 1)
                    act.wait_ge(*s.k_turned(b + 1))
                    act.activation(fields.KT[:, :, :].rearrange("p c s -> p (c s)"), m.ps[6][:, :],
                                   ACT.Copy).then_inc(s.k_ready.sem, 1)
                    exp(b, 0)
                if on[1]:
                    act.wait_ge(*s.v_done(k))
                    act.wait_ge(*s.mixed(2 * (k - 2)))
                    act.activation(fields.V[:, 1 - p, :, 0:LD],
                                   m.ps[2][:, :].rearrange("p (h d) -> p h d", h=LH),
                                   ACT.Copy).then_inc(s.v_ready.sem, 1)
                if on[3]:
                    act.wait_ge(*s.on_turned(c + 1))
                    act.wait_ge(*s.projected(c))
                    act.activation(fields.OT[:, :], m.ps[3][:, :], ACT.Copy).then_inc(s.ot_ready.sem, 1)
                if on[2]:
                    exp(b, 1)
            pipeline(act, B, 4, step)

        @block.vector
        def _(dve):
            def rotate(i, b, squared, normed, rotated):
                dve.wait_ge(*squared(b + 1))
                dve.wait_ge(*normed(b))
                src = m.ps[i][:, :].rearrange("p (h d) -> p h d", h=LH)
                dve.tensor_tensor(fields.T1[:, i].rearrange("p (h d) -> p h d", h=LH), src,
                                  bcast(fields.straight[:, i, :], 1, LH), ALU.mult)
                t2 = fields.T2[:, i].rearrange("p (h d) -> p h d", h=LH)
                dve.tensor_tensor(t2[:, :, 0:half], src[:, :, half:LD],
                                  bcast(fields.swapped[:, i, 0:half], 1, LH), ALU.mult)
                dve.tensor_tensor(t2[:, :, half:LD], src[:, :, 0:half],
                                  bcast(fields.swapped[:, i, half:LD], 1, LH), ALU.mult).then_inc(rotated.sem, 1)

            def sums(i, b, squared, normed, summed):
                dve.wait_ge(*squared(b + 1))
                dve.wait_ge(*normed(b))
                dve.tensor_reduce(fields.SS[:, i], fields.SQ[:, i].rearrange("p (h d) -> p h d", h=LH), AXX,
                                  ALU.add).then_inc(s.floored.sem, 1)
                dve.wait_ge(*s.floored(2 * b + i + 1))
                dve.tensor_scalar(fields.SS[:, i], fields.SS[:, i], 1e-24, None, ALU.max).then_inc(summed.sem, 1)

            def soft(b, u):
                dve.wait_ge(*s.scored(2 * b + u + 1))
                sc = m.ps[4 + u][:, :].rearrange("p (j s) -> p j s", j=W)
                dve.tensor_reduce(m.mx[:, u, :], sc, AXX, ALU.max).then_inc(s.maxed.sem, 1)
                dve.wait_ge(*s.maxed(2 * b + u + 1))
                dve.wait_ge(*s.turned(2 * b + u - 1))
                dve.tensor_tensor(fields.PR[:, u, :].rearrange("p (j s) -> p j s", j=W), sc,
                                  bcast(m.mx[:, u, :], 2, S), ALU.subtract).then_inc(s.shifted.sem, 1)

            def divide(b, u):
                dve.wait_ge(*s.mixed(2 * b + u + 1))
                o = m.ps[7 if u == 0 else 2][:, 0:W * (LD + 1)].rearrange("p (j d) -> p j d", j=W)
                dve.reciprocal(m.rs[:, u * W:(u + 1) * W], o[:, :, LD]).then_inc(s.inverted.sem, 1)
                dve.wait_ge(*s.inverted(2 * b + u + 1))
                dve.wait_ge(*s.on_turned(b))
                dve.tensor_tensor(fields.ON[:, u * W * LD:(u + 1) * W * LD].rearrange("p (j d) -> p j d", j=W),
                                  o[:, :, 0:LD], bcast(m.rs[:, u * W:(u + 1) * W], 2, LD), ALU.mult).then_inc(s.divided.sem, 1)

            def step(k, p, on):
                if on[1]:
                    rotate(0, k - 1, s.q_sq, s.q_norm, s.q_rot)
                    sums(0, k - 1, s.q_sq, s.q_norm, s.q_ss)
                if on[4]:
                    dve.wait_ge(*s.projected(k - 3))
                    x = m.X[:, dyn(k - 4, 1), :].rearrange("p a d -> p (a d)")
                    dve.tensor_tensor(x, m.ps[3][:, 0:D], x, ALU.add).then_inc(s.added.sem, 1)
                if on[1]:
                    rotate(1, k - 1, s.k_sq, s.k_norm, s.k_rot)
                    sums(1, k - 1, s.k_sq, s.k_norm, s.k_ss)
                if on[3]:
                    divide(k - 3, 0)
                    divide(k - 3, 1)
                if on[2]:
                    soft(k - 2, 0)
                    soft(k - 2, 1)
            pipeline(dve, B, 5, step)
    s.close(xs_ready=B, x_turned=B, ht_ready=B, q_done=B, k_done=B, v_done=B, q_sq=B, k_sq=B, q_rot=B, k_rot=B,
            q_ss=B, k_ss=B, q_norm=B, k_norm=B, q_turned=B, k_turned=B, q_ready=B, k_ready=B, v_ready=B,
            scored=2 * B, maxed=2 * B, shifted=2 * B, exped=2 * B, turned=2 * B, pt_ready=2 * B, mixed=2 * B,
            inverted=2 * B, divided=2 * B, on_turned=B, ot_ready=B, projected=B, added=B, floored=2 * B,
            powered=2 * B, parts_added=2 * B)


def gated_mlp(nc, m, s, d):
    f = m.mlp
    w1, w2, b1, b2 = (m.w(f"f{d}_{n}") for n in ("w1", "w2", "b1", "b2"))
    lg, lb = m.w(f"f{d}_lg"), m.w(f"f{d}_lb")
    NC = len(HCH)

    with nc.Block() as block:
        @block.gpsimd
        def _(pool):
            def step(g, p, on):
                pool.wait_ge(*s.xn_ready(g - 1))
                pool.tensor_copy(f.XS[:, p], m.X[:, dyn(g * G, G), :]).then_inc(s.xs_ready.sem, 1)
                rstd_on(pool, m, s, g, p, G)
            pipeline(pool, NG, 1, step)

        @block.tensor
        def _(pe):
            def step(k, p, on):
                if on[0]:
                    pe.wait_ge(*s.xs_ready(k + 1))
                    pe.wait_ge(*s.xt_ready(k))
                    pe.matmul(m.ps[0][:, 0:G * 64], m.c("shift"), f.XS[:, p, :, 64:D], start=True,
                              stop=True).then_inc(s.x_shifted.sem, 1)
                if on[2]:
                    pe.wait_ge(*s.gated((k - 1) * NC))
                    pe.wait_ge(*s.added(k - 2))
                    for j in range(G):
                        for c, (at, n) in enumerate(HCH):
                            last = pe.matmul(m.ps[7][:, j * D:(j + 1) * D], f.HH[0:n, p, c, j * S:(j + 1) * S],
                                             w2[0:n, c * D:(c + 1) * D], start=c == 0, stop=c == NC - 1,
                                             skip_group_check=True)
                    last.then_inc(s.projected.sem, 1)
                if on[1]:
                    g, q = k - 1, 1 - p
                    pe.wait_ge(*s.xt_ready(g + 1))
                    for c, (at, n) in enumerate(HCH):
                        u = g * NC + c
                        pe.wait_ge(*s.gated(u - NC + 1))
                        pe.matmul(m.ps[1 + c][0:n, :], w1[:, HID + at:HID + at + n], f.HT[:, q, :], start=True,
                                  stop=True).then_inc(s.g_done.sem, 1)
                        pe.matmul(m.ps[4 + c][0:n, :], w1[:, at:at + n], f.HT[:, q, :], start=True,
                                  stop=True).then_inc(s.a_done.sem, 1)
                if on[0]:
                    pe.wait_ge(*s.xn_ready(k + 1))
                    for j in range(G):
                        last = pe.transpose(m.ps[0][:, j * S:(j + 1) * S], f.XN[:, p, j, :], m.c("ident"))
                    last.then_inc(s.x_turned.sem, 1)
            pipeline(pe, NG, 3, step)

        @block.scalar
        def _(act):
            def step(k, p, on):
                if on[1]:
                    for c, (at, n) in enumerate(HCH):
                        u = (k - 1) * NC + c
                        act.wait_ge(*s.g_done(u + 1))
                        act.wait_ge(*s.gated(u - NC + 1))
                        act.activation(f.GT[0:n, c, :], m.ps[1 + c][0:n, :], ACT.Gelu,
                                       bias=b1[0:n, NC + c:NC + c + 1]).then_inc(s.gelued.sem, 1)
                if on[0]:
                    act.wait_ge(*s.x_turned(k + 1))
                    act.wait_ge(*s.a_done((k - 1) * NC))
                    act.activation(f.HT[:, p, :], m.ps[0][:, :], ACT.Identity, bias=lb,
                                   scale=lg).then_inc(s.xt_ready.sem, 1)
            pipeline(act, NG, 2, step)

        @block.vector
        def _(dve):
            def step(k, p, on):
                if on[0]:
                    dve.wait_ge(*s.x_shifted(k + 1))
                    dve.tensor_copy(f.XS[:, p, :, 64:D], m.ps[0][:, 0:G * 64].rearrange("p (j d) -> p j d", j=G)
                                    ).then_inc(s.shift_in.sem, 1)
                    dve.wait_ge(*s.shift_in(k + 1))
                    dve.wait_ge(*s.x_turned(k - 1))
                    layernorm_on(dve, m, s, k, p, G, lambda j: f.XS[:, p, j, :], lambda j: f.XN[:, p, j, :],
                                 1e-5).then_inc(s.xn_ready.sem, 1)
                    x = m.X[:, dyn(k * G, G), :]
                    dve.tensor_tensor(x, x, bcast(b2, 1, G), ALU.add).then_inc(s.biased.sem, 1)
                if on[1]:
                    q = 1 - p
                    for c, (at, n) in enumerate(HCH):
                        u = (k - 1) * NC + c
                        dve.wait_ge(*s.gelued(u + 1))
                        dve.wait_ge(*s.a_done(u + 1))
                        dve.wait_ge(*s.projected(k - 2))
                        dve.scalar_tensor_tensor(f.HH[0:n, q, c, :], m.ps[4 + c][0:n, :], b1[0:n, c:c + 1],
                                                 f.GT[0:n, c, :], ALU.add, ALU.mult).then_inc(s.gated.sem, 1)
                if on[2]:
                    g = k - 2
                    dve.wait_ge(*s.projected(g + 1))
                    dve.wait_ge(*s.biased(g + 1))
                    x = m.X[:, dyn(g * G, G), :]
                    dve.tensor_tensor(x, m.ps[7][:, :].rearrange("p (j d) -> p j d", j=G), x,
                                      ALU.add).then_inc(s.added.sem, 1)
            pipeline(dve, NG, 3, step)
    s.close(xs_ready=NG, biased=NG, stats=NG, means=NG, spread=NG, vars=NG, rstd=NG, nmean=NG, x_shifted=NG,
            shift_in=NG, xn_ready=NG, x_turned=NG, xt_ready=NG, g_done=NG * NC, a_done=NG * NC, gelued=NG * NC,
            gated=NG * NC, projected=NG, added=NG)


def normalize(nc, m, s, *, add=None, keep_to=None, out=None):
    with nc.Block() as block:
        @block.gpsimd
        def _(pool):
            def step(g, p, on):
                if add is not None:
                    pool.wait_ge(*s.xn_ready(g - 1))
                    pool.tensor_tensor(m.XN2[:, p], m.X[:, dyn(g * G, G), :], add[:, dyn(g * G, G), :],
                                       ALU.add).then_inc(s.summed.sem, 1)
                rstd_on(pool, m, s, g, p, G)
                if keep_to is not None:
                    pool.wait_ge(*s.xn_ready(g + 1))
                    pool.tensor_copy(keep_to[:, dyn(g * G, G), :], m.X[:, dyn(g * G, G), :])
            pipeline(pool, NG, 1, step)

        @block.vector
        def _(dve):
            def step(g, p, on):
                x = lambda j: m.X[:, dyn(g * G + j, 1), :].rearrange("p a d -> p (a d)")
                src = x
                if add is not None:
                    src = lambda j: m.XN2[:, p, j, :]
                    dve.wait_ge(*s.summed(g + 1))
                layernorm_on(dve, m, s, g, p, G, src, x, 1e-5).then_inc(s.xn_ready.sem, 1)
            pipeline(dve, NG, 1, step)

        if out is not None:
            @block.sync
            def _(sp):
                def step(g, p, on):
                    sp.wait_ge(*s.xn_ready(g + 1))
                    sp.dma_start(out[dyn(g * G, G), :, :].rearrange("b s d -> s b d"),
                                 m.X[:, dyn(g * G, G), :]).then_inc(s.stored.sem, 16)
                pipeline(sp, NG, 1, step)
                sp.wait_ge(*s.stored(16 * NG))
    s.close(stats=NG, means=NG, spread=NG, vars=NG, rstd=NG, nmean=NG, xn_ready=NG)
    if add is not None:
        s.close(summed=NG)


def project_latent(nc, m, s):
    f = Memory()
    (f.XN, f.SUM, f.XT, f.CT, f.PART, f.STR
     ) = carve(m.ring, [(2, G, D), (G, D), (2, G * S), (2, G * S), (2, G * S), (2, 2, G * S)])
    weights = {0: m.w("m_q"), 1: m.w("m_k")}

    with nc.Block() as block:
        @block.gpsimd
        def _(pool):
            def add_up(g, which):
                for t in range(2):
                    pool.wait_ge(*s.unit_ready(6 * g + 3 * which + t + 2))
                    tile = 2 * which + t
                    pool.tensor_tensor(m.QKT[:, dyn(g * G, G), tile * S:(tile + 1) * S],
                                       f.STR[:, which, t].rearrange("p (b s) -> p b s", b=G),
                                       f.PART[:, which].rearrange("p (b s) -> p b s", b=G),
                                       ALU.add).then_inc(s.rotated.sem, 1)

            def step(k, p, on):
                if on[0]:
                    pool.wait_ge(*s.xn_ready(k))
                    pool.tensor_tensor(f.SUM[:, :, :], m.X[:, dyn(k * G, G), :], m.XR[:, dyn(k * G, G), :],
                                       ALU.add).then_inc(s.summed.sem, 1)
                if on[1]:
                    add_up(k - 1, 0)
                if on[0]:
                    rstd_on(pool, m, s, k, p, G)
                if on[1]:
                    add_up(k - 1, 1)
            pipeline(pool, NG, 2, step)

        @block.tensor
        def _(pe):
            def step(k, p, on):
                g, q = k - 1, 1 - p
                if on[1]:
                    pe.wait_ge(*s.xt_ready(g + 1))
                    pe.wait_ge(*s.c_ready(g))
                    pe.matmul(m.ps[2][:, :], m.w("m_down"), f.XT[:, q, :], start=True,
                              stop=True).then_inc(s.c_done.sem, 1)
                    for which, src in ((0, f.XT), (1, f.CT)):
                        if which == 1:
                            pe.wait_ge(*s.c_ready(g + 1))
                        for i in range(3):
                            u = 6 * g + 3 * which + i
                            pe.wait_ge(*s.unit_ready(u - 2))
                            pe.matmul(m.ps[5 + i][:, :], weights[which][:, i * D:(i + 1) * D], src[:, q, :],
                                      start=True, stop=True).then_inc(s.unit_done.sem, 1)
                    pe.wait_ge(*s.v_ready(g - 1))
                    for j in range(G):
                        last = pe.matmul(m.ps[3 + q][:, j * D:(j + 1) * D], f.CT[:, q, j * S:(j + 1) * S],
                                         m.w("m_v"), start=True, stop=True)
                    last.then_inc(s.v_done.sem, 1)
                if on[0]:
                    pe.wait_ge(*s.xn_ready(k + 1))
                    pe.wait_ge(*s.xt_ready(k - 1))
                    for j in range(G):
                        last = pe.transpose(m.ps[p][:, j * S:(j + 1) * S], f.XN[:, p, j, :], m.c("ident"))
                    last.then_inc(s.x_turned.sem, 1)
            pipeline(pe, NG, 2, step)

        @block.scalar
        def _(act):
            def step(k, p, on):
                g, q = k - 1, 1 - p
                if on[1]:
                    act.wait_ge(*s.c_done(g + 1))
                    act.wait_ge(*s.v_done(g - 1))
                    act.activation(f.CT[:, q, :], m.ps[2][:, :], ACT.Copy).then_inc(s.c_ready.sem, 1)
                    act.wait_ge(*s.v_done(g + 1))
                    act.activation(m.V[:, dyn(g * G, G), :, 0:HD],
                                   m.ps[3 + q][:, :].rearrange("p (b h d) -> p b h d", b=G, h=H),
                                   ACT.Copy).then_inc(s.v_ready.sem, 1)
                if on[0]:
                    act.wait_ge(*s.x_turned(k + 1))
                    act.wait_ge(*s.v_done(k - 1))
                    act.activation(f.XT[:, p, :], m.ps[p][:, :], ACT.Copy).then_inc(s.xt_ready.sem, 1)
                    act.wait_ge(*s.xn_ready(k + 1))
                    act.activation(m.X[:, dyn(k * G, G), :], f.XN[:, p], ACT.Copy).then_inc(s.x_kept.sem, 1)
            pipeline(act, NG, 2, step)

        @block.vector
        def _(dve):
            def rotate(g, which):
                for i in range(3):
                    dve.wait_ge(*s.unit_done(6 * g + 3 * which + i + 1))
                    dve.wait_ge(*s.rotated(4 * g - 2 + 2 * which))
                    dst = f.PART[:, which] if i == 0 else f.STR[:, which, i - 1]
                    dve.tensor_tensor(dst.rearrange("p (b s) -> p b s", b=G),
                                      m.ps[5 + i][:, :].rearrange("p (b s) -> p b s", b=G),
                                      bcast(m.c("ropesin" if i == 0 else "ropecos"), 1, G),
                                      ALU.mult).then_inc(s.unit_ready.sem, 1)

            def step(k, p, on):
                if on[1]:
                    rotate(k - 1, 0)
                if on[0]:
                    dve.wait_ge(*s.summed(k + 1))
                    dve.wait_ge(*s.x_turned(k - 1))
                    dve.wait_ge(*s.x_kept(k - 1))
                    layernorm_on(dve, m, s, k, p, G, lambda j: f.SUM[:, j, :], lambda j: f.XN[:, p, j, :],
                                 1e-5).then_inc(s.xn_ready.sem, 1)
                if on[1]:
                    rotate(k - 1, 1)
            pipeline(dve, NG, 2, step)
    s.close(summed=NG, rotated=4 * NG, xn_ready=NG, x_kept=NG, c_done=NG, c_ready=NG, unit_done=6 * NG,
            unit_ready=6 * NG, v_done=NG, v_ready=NG, x_turned=NG, xt_ready=NG, stats=NG, means=NG, spread=NG,
            vars=NG, rstd=NG, nmean=NG)


def project_linear(nc, m, s, ctx):
    f = Memory()
    (f.XN, f.XT, f.CT, f.U
     ) = carve(m.ring, [(2, G, D), (2, G * S), (2, G * S), (2, 3 * G, D)])
    places = [m.QT, m.KT, m.XTA]

    with nc.Block() as block:
        @block.sync
        def _(sp):
            def step(g, p, on):
                sp.wait_ge(*s.v_done(g - 1))
                sp.dma_start(f.CT[:, p, :], ctx[:, dyn(g * G * S, G * S)]).then_inc(s.ct_loaded[p].sem, 16)
            pipeline(sp, NG, 1, step)

        @block.gpsimd
        def _(pool):
            def step(k, p, on):
                if on[0]:
                    rstd_on(pool, m, s, k, p, G)
                if on[1]:
                    g, q = k - 1, 1 - p
                    rstd_on(pool, m.second, s.second, g, q, 3 * G)
                    for i in range(3):
                        u = f.U[:, q, i * G:(i + 1) * G]
                        pool.wait_ge(*s.norm2(g + 1))
                        pool.tensor_tensor(u, u, bcast(m.w("y_gamma"), 1, G), ALU.mult).then_inc(s.scaled.sem, 1)
            pipeline(pool, NG, 2, step)

        @block.tensor
        def _(pe):
            def tokens(bank, src, q, w, done):
                for j in range(G):
                    last = pe.matmul(m.ps[bank][:, j * D:(j + 1) * D], src[:, q, j * S:(j + 1) * S], w,
                                     start=True, stop=True)
                last.then_inc(done.sem, 1)

            def step(k, p, on):
                if on[0]:
                    pe.wait_ge(*s.xn_ready(k + 1))
                    pe.wait_ge(*s.xt_ready(k - 1))
                    for j in range(G):
                        last = pe.transpose(m.ps[p][:, j * S:(j + 1) * S], f.XN[:, p, j, :], m.c("ident"))
                    last.then_inc(s.x_turned.sem, 1)
                if on[1]:
                    g, q = k - 1, 1 - p
                    pe.wait_ge(*s.norm2(g - 1))
                    pe.wait_ge(s.ct_loaded[q].sem, g * 8 - q * 8 + 16 + s.ct_loaded[q].base)
                    tokens(4 + q, f.CT, q, m.w("y_wkv")[:, 0:D], s.k_done)
                    tokens(6 + q, f.CT, q, m.w("y_wkv")[:, D:2 * D], s.v_done)
                    pe.wait_ge(*s.xt_ready(g + 1))
                    tokens(2 + q, f.XT, q, m.w("y_wq"), s.q_done)
            pipeline(pe, NG, 2, step)

        @block.scalar
        def _(act):
            def step(k, p, on):
                act.wait_ge(*s.x_turned(k + 1))
                act.wait_ge(*s.q_done(k - 1))
                act.activation(f.XT[:, p, :], m.ps[p][:, :], ACT.Copy).then_inc(s.xt_ready.sem, 1)
                act.activation(m.X[:, dyn(k * G, G), :], f.XN[:, p], ACT.Copy).then_inc(s.x_kept.sem, 1)
            pipeline(act, NG, 1, step)

        @block.vector
        def _(dve):
            def step(k, p, on):
                if on[0]:
                    x = lambda j: m.X[:, dyn(k * G + j, 1), :].rearrange("p a d -> p (a d)")
                    dve.wait_ge(*s.x_turned(k - 1))
                    dve.wait_ge(*s.x_kept(k - 1))
                    layernorm_on(dve, m, s, k, p, G, x, lambda j: f.XN[:, p, j, :], 1e-5).then_inc(s.xn_ready.sem, 1)
                if on[1]:
                    g, q = k - 1, 1 - p
                    dve.wait_ge(*s.q_done(g + 1))
                    dve.wait_ge(*s.based(g - 1))
                    layernorm_on(dve, m.second, s.second, g, q, 3 * G,
                                 lambda j: m.ps[2 + 2 * (j // G) + q][:, (j % G) * D:(j % G + 1) * D],
                                 lambda j: f.U[:, q, j, :], 1e-6).then_inc(s.norm2.sem, 1)
                if on[2]:
                    g = k - 2
                    for i in range(3):
                        dve.wait_ge(*s.scaled(3 * g + i + 1))
                        last = dve.tensor_tensor(places[i][:, dyn(g * G * S, G * S)].rearrange("p (b d) -> p b d", b=G),
                                                 f.U[:, p, i * G:(i + 1) * G], bcast(m.w("y_beta"), 1, G), ALU.add)
                    last.then_inc(s.based.sem, 1)
            pipeline(dve, NG, 3, step)
    s.close(v_done=NG, k_done=NG, q_done=NG, norm2=NG, scaled=3 * NG, based=NG, xn_ready=NG, x_turned=NG,
            xt_ready=NG, x_kept=NG, **{n: NG for n in ("stats", "means", "spread", "vars", "rstd", "nmean", "stats2",
                                                       "means2", "spread2", "vars2", "rstd2", "nmean2")})
    for q in range(2):
        s.ct_loaded[q].base += 16 * (NG // 2)


def linear_attention(nc, m, s):
    N = D + H
    f = Memory()
    (f.Q, f.K, f.V1, f.QT, f.KV, f.ZM, f.AF, f.O, f.ON, f.DEN, f.RZ, f.EM
     ) = carve(m.ring, [(G, D), (G, D), (G, N), (2, G * S), (2, G, N), (G, H, HD), (G * S,), (G, D), (G, D),
        (G, H), (G, H), (G,)])
    spread = m.arena[:, 0:HD * G * S].rearrange("p (e b h n) -> p e b h n", e=HD, b=G, h=H)
    n2, eps = G // 2, 1e-6
    em = lambda g: bcast(m.w("em")[:, dyn(g * G, G)], 2, D)

    with nc.Block() as block:
        @block.vector
        def _(dve):
            dve.memset(f.V1[:, :, D:N], 1.0)

    with nc.Block() as block:
        @block.gpsimd
        def _(pool):
            def step(k, p, on):
                if on[0]:
                    pool.wait_ge(*s.kv_done(k))
                    pool.wait_ge(*s.v_staged(k))
                    pool.tensor_copy(f.EM[:, :], m.w("em")[:, dyn(k * G, G)]).then_inc(s.em_ready.sem, 1)
                    pool.tensor_tensor(f.V1[:, :, 0:D], m.XTA[:, dyn(k * G * S, G * S)].rearrange(
                        "p (b d) -> p b d", b=G), em(k), ALU.mult)
                    pool.wait_ge(*s.staged(k + 1))
                    pool.wait_ge(*s.em_ready(k + 1))
                    pool.tensor_tensor(f.K[:, :, :], f.K[:, :, :], bcast(f.EM[:, :], 2, D),
                                       ALU.mult).then_inc(s.v_staged.sem, 1)
                if on[2]:
                    g = k - 2
                    rstd_on(pool, m, s, g, p, G)
                    pool.wait_ge(*s.fin_norm(g + 1))
                    pool.tensor_tensor(f.ON[:, :, :], f.ON[:, :, :], bcast(m.w("y_gamma"), 1, G),
                                       ALU.mult).then_inc(s.fin_scaled.sem, 1)
            pipeline(pool, NG, 3, step)

        @block.tensor
        def _(pe):
            def step(k, p, on):
                if on[0]:
                    pe.wait_ge(*s.v_staged(k + 1))
                    pe.wait_ge(*s.q_ready(k))
                    for j in range(G):
                        last = pe.transpose(m.ps[0][:, j * S:(j + 1) * S], f.Q[:, j, :], m.c("ident"))
                    last.then_inc(s.q_done.sem, 1)
                    pe.wait_ge(*s.kv_ready(2 * k))
                    for j in range(G):
                        last = pe.matmul(m.ps[1 + j // n2][:, (j % n2) * N:(j % n2 + 1) * N], f.K[:, j, :],
                                         f.V1[:, j, :], start=True, stop=True)
                    last.then_inc(s.kv_done.sem, 1)
                if on[1]:
                    g, q = k - 1, 1 - p
                    pe.wait_ge(*s.q_ready(g + 1))
                    pe.wait_ge(*s.kv_ready(2 * g + 2))
                    pe.wait_ge(*s.at_ready(g))
                    for j in range(G):
                        last = pe.matmul(m.ps[3 + j // n2][:, (j % n2) * N:(j % n2 + 1) * N],
                                         f.QT[:, q, j * S:(j + 1) * S], f.KV[:, q, j, :], start=True, stop=True)
                    last.then_inc(s.at_done.sem, 1)
                if on[2]:
                    g = k - 2
                    pe.wait_ge(*s.att_ready(g + 1))
                    pe.wait_ge(*s.ebias(g))
                    for j in range(G):
                        last = pe.matmul(m.ps[6][:, j * D:(j + 1) * D], f.AF[:, j * S:(j + 1) * S], m.w("y_dw"),
                                         start=True, stop=True)
                    last.then_inc(s.projected.sem, 1)
                if on[1]:
                    pe.wait_ge(*s.at_ready(k))
                    pe.wait_ge(*s.att_ready(k - 1))
                    for e in range(HD):
                        at = e // 2 * 32
                        last = pe.matmul(m.ps[5][at:at + 32, :], m.c("place")[:, (e % 2) * 32:(e % 2) * 32 + 32],
                                         spread[:, e].rearrange("p b h n -> p (b h n)"), start=e % 2 == 0,
                                         stop=e % 2 == 1, skip_group_check=True)
                    last.then_inc(s.at_turned.sem, 1)
            pipeline(pe, NG, 3, step)

        @block.scalar
        def _(act):
            def step(k, p, on):
                if on[0]:
                    act.wait_ge(*s.q_done(k + 1))
                    act.wait_ge(*s.at_done(k - 1))
                    act.activation(f.QT[:, p, :], m.ps[0][:, :], ACT.Copy).then_inc(s.q_ready.sem, 1)
                if on[1]:
                    act.wait_ge(*s.at_turned(k))
                    act.wait_ge(*s.projected(k - 1))
                    act.activation(f.AF[:, :], m.ps[5][:, :], ACT.Copy).then_inc(s.att_ready.sem, 1)
            pipeline(act, NG, 2, step)

        @block.vector
        def _(dve):
            def group(area, g):
                return area[:, dyn(g * G * S, G * S)].rearrange("p (b d) -> p b d", b=G)

            def step(k, p, on):
                if on[0]:
                    dve.wait_ge(*s.kv_done(k))
                    dve.tensor_scalar(f.Q[:, :, :], group(m.QT, k), 0.0, eps, ALU.max, ALU.add)
                    dve.tensor_scalar(f.K[:, :, :], group(m.KT, k), 0.0, eps, ALU.max, ALU.add
                                      ).then_inc(s.staged.sem, 1)
                    dve.wait_ge(*s.kv_done(k + 1))
                    dve.wait_ge(*s.at_done(k - 1))
                    for i in range(2):
                        kv = m.ps[1 + i][:, 0:n2 * N].rearrange("p (b n) -> p b n", b=n2)
                        dve.tensor_tensor(f.KV[:, p, i * n2:(i + 1) * n2, :], kv, bcast(m.c("blocks_sel"), 1, n2),
                                          ALU.mult).then_inc(s.kv_ready.sem, 1)
                if on[1]:
                    g = k - 1
                    dve.wait_ge(*s.at_done(g + 1))
                    at = [m.ps[3 + i][:, 0:n2 * N].rearrange("p (b n) -> p b n", b=n2) for i in range(2)]
                    for i in range(2):
                        last = dve.tensor_scalar(f.DEN[:, i * n2:(i + 1) * n2, :], at[i][:, :, D:N], eps, None, ALU.add)
                    last.then_inc(s.z_added.sem, 1)
                    dve.wait_ge(*s.z_added(g + 1))
                    dve.reciprocal(f.RZ[:, :, :], f.DEN[:, :, :]).then_inc(s.z_ready.sem, 1)
                    dve.wait_ge(*s.z_ready(g + 1))
                    dve.tensor_tensor(f.ZM[:, :, :, :].rearrange("p b h n -> p (b h) n"),
                                      bcast(f.RZ[:, :, :].rearrange("p b h -> p (b h)"), 2, HD),
                                      bcast(m.c("block"), 1, G * H), ALU.mult).then_inc(s.zm_ready.sem, 1)
                    dve.wait_ge(*s.zm_ready(g + 1))
                    dve.wait_ge(*s.at_turned(g))
                    for j in range(G):
                        last = dve.tensor_tensor(
                            spread[:, :, j], bcast(at[j // n2][:, j % n2, 0:D].rearrange("p (h e) -> p e h", h=H), 3, HD),
                            bcast(f.ZM[:, j], 1, HD), ALU.mult)
                    last.then_inc(s.at_ready.sem, 1)
                if on[2]:
                    g = k - 2
                    dve.wait_ge(*s.projected(g + 1))
                    dve.tensor_tensor(f.O[:, :, :], m.ps[6][:, :].rearrange("p (b d) -> p b d", b=G),
                                      bcast(m.w("y_db"), 1, G), ALU.add).then_inc(s.ebias.sem, 1)
                    dve.wait_ge(*s.ebias(g + 1))
                    layernorm_on(dve, m, s, g, p, G, lambda j: f.O[:, j, :], lambda j: f.ON[:, j, :],
                                 eps).then_inc(s.fin_norm.sem, 1)
                    dve.wait_ge(*s.fin_scaled(g + 1))
                    x = m.X[:, dyn(g * G, G), :]
                    dve.tensor_tensor(f.ON[:, :, :], f.ON[:, :, :], bcast(m.w("y_beta"), 1, G),
                                      ALU.add).then_inc(s.fin_based.sem, 1)
                    dve.wait_ge(*s.fin_based(g + 1))
                    dve.tensor_tensor(x, f.ON[:, :, :], x, ALU.add).then_inc(s.added.sem, 1)
                    dve.wait_ge(*s.added(g + 1))
            pipeline(dve, NG, 3, step)
    s.close(**{n: NG for n in ("staged", "v_staged", "em_ready", "zm_ready", "q_done", "q_ready", "kv_done", "at_done", "at_ready", "projected",
                               "at_turned", "att_ready", "z_added", "z_ready", "ebias", "fin_norm", "fin_scaled",
                               "fin_based", "added", "stats", "means", "spread", "vars", "rstd", "nmean")},
            kv_ready=2 * NG)


def gates(nc, m, s):
    f = Memory()
    (f.SUM, f.MEAN, f.L, f.MX, f.SH, f.EX, f.ES, f.ER, f.PW, f.GTR, f.EQ, f.EQL, f.BEF, f.CNT, f.CH, f.GM,
     f.ROWS
     ) = carve(m.ring, [(B,), (B,), (E,), (1,), (E,), (E,), (1,), (1,), (E,), (E, E), (E, E), (E, E), (E, E),
        (E,), (E,), (E,), (B, E)])
    b = slice(0, B)
    with nc.Block() as block:
        @block.gpsimd
        def _(pool):
            pool.memset(m.XR[:, :, :], 0.0)

        @block.tensor
        def _(pe):
            pe.wait_ge(*s.g_steps(2))
            pe.matmul(m.ps[0][b, 0:E], f.MEAN[:, :], m.w("gate_w"), start=True, stop=True).then_inc(s.g_done.sem, 1)
            pe.wait_ge(*s.g_rows(1))
            pe.matmul(m.ps[1][:, 0:B * E], m.c("ones")[b, :], f.ROWS[b].rearrange("p b e -> p (b e)"), start=True,
                      stop=True).then_inc(s.g_done.sem, 1)

        @block.scalar
        def _(act):
            act.wait_ge(*s.g_steps(5))
            act.activation(f.EX[b], f.SH[b], ACT.Exp).then_inc(s.exped.sem, 1)

        @block.vector
        def _(dve):
            dve.tensor_reduce(f.SUM[:, :], m.XTA.rearrange("p (b s) -> p b s", b=B), AXX, ALU.add
                              ).then_inc(s.g_steps.sem, 1)
            dve.wait_ge(*s.g_steps(1))
            dve.tensor_scalar(f.MEAN[:, :], f.SUM[:, :], 1.0 / S, None, ALU.mult).then_inc(s.g_steps.sem, 1)
            dve.wait_ge(*s.g_done(1))
            dve.tensor_tensor(f.L[b], m.ps[0][b, 0:E], m.w("gate_b")[b], ALU.add).then_inc(s.g_steps.sem, 1)
            dve.wait_ge(*s.g_steps(3))
            dve.tensor_reduce(f.MX[b], f.L[b], AXX, ALU.max).then_inc(s.g_steps.sem, 1)
            mine, other = bcast(f.L[b], 2, E), bcast(f.L[b], 1, E)
            dve.tensor_tensor(f.GTR[b], other, mine, ALU.is_gt)
            dve.tensor_tensor(f.EQ[b], other, mine, ALU.is_equal).then_inc(s.g_compared.sem, 1)
            dve.wait_ge(*s.g_steps(4))
            dve.tensor_tensor(f.SH[b], f.L[b], bcast(f.MX[b, 0], 1, E), ALU.subtract).then_inc(s.g_steps.sem, 1)
            dve.wait_ge(*s.g_compared(1))
            dve.tensor_tensor(f.EQL[b], f.EQ[b], m.c("lower")[b].rearrange("p (j i) -> p j i", j=E),
                              ALU.mult).then_inc(s.g_compared.sem, 1)
            dve.wait_ge(*s.g_compared(2))
            dve.tensor_tensor(f.BEF[b], f.EQL[b], f.GTR[b], ALU.add).then_inc(s.g_compared.sem, 1)
            dve.wait_ge(*s.g_compared(3))
            dve.tensor_reduce(f.CNT[b], f.BEF[b], AXX, ALU.add).then_inc(s.g_compared.sem, 1)
            dve.wait_ge(*s.exped(1))
            dve.tensor_reduce(f.ES[b], f.EX[b], AXX, ALU.add).then_inc(s.g_steps.sem, 1)
            dve.wait_ge(*s.g_compared(4))
            dve.scalar_tensor_tensor(f.GM[b], f.CNT[b], 1.5, f.EX[b], ALU.is_lt, ALU.mult).then_inc(s.g_compared.sem, 1)
            dve.wait_ge(*s.g_steps(6))
            dve.reciprocal(f.ER[b], f.ES[b]).then_inc(s.g_steps.sem, 1)
            dve.wait_ge(*s.g_steps(7))
            dve.wait_ge(*s.g_compared(5))
            dve.scalar_tensor_tensor(f.ROWS[b], bcast(f.GM[b], 1, B), f.ER[b, 0:1],
                                     m.c("seqsel")[b].rearrange("p (b e) -> p b e", b=B), ALU.mult,
                                     ALU.mult).then_inc(s.g_rows.sem, 1)
            dve.wait_ge(*s.g_done(2))
            dve.tensor_copy(m.G[:, :], m.ps[1][:, 0:B * E])
    s.close(g_steps=7, g_compared=5, g_rows=1, g_done=2, exped=1)


def expert_mlp(nc, m, s, w, e):
    f = Memory()
    (f.YB, f.U, f.XT, f.R, f.O, f.ON, f.OW, f.NB
     ) = carve(m.ring, [(2, G, D), (2, G, D), (2, G * S), (2, G, D), (G, D), (G, D), (G, D), (D,)])
    HH = m.KT.rearrange("p (a c s) -> p a c s", a=2, c=DFF // D)
    NC = DFF // D
    ACC = m.XR

    with nc.Block() as block:
        @block.vector
        def _(dve):
            dve.tensor_tensor(f.NB[:, :], w("n1b"), w("l2b"), ALU.add)

    with nc.Block() as block:
        @block.gpsimd
        def _(pool):
            def step(k, p, on):
                if on[0]:
                    pool.wait_ge(*s.xn_ready(k - 1))
                    pool.tensor_tensor(f.YB[:, p], m.Y[:, dyn(k * G, G), :], bcast(w("ob"), 1, G),
                                       ALU.add).then_inc(s.summed.sem, 1)
                    rstd_on(pool, m, s, k, p, G)
                    pool.wait_ge(*s.xn_ready(k + 1))
                    pool.wait_ge(*s.res_added(k - 1))
                    pool.tensor_tensor(f.R[:, p], f.U[:, p], bcast(w("n1w"), 1, G), ALU.mult).then_inc(s.scaled.sem, 1)
                    pool.wait_ge(*s.scaled(k + 1))
                    pool.tensor_tensor(f.R[:, p], f.R[:, p], bcast(f.NB[:, :], 1, G), ALU.add
                                       ).then_inc(s.based.sem, 1)
                if on[2]:
                    g = k - 2
                    rstd_on(pool, m.second, s.second, g, p, G)
                    pool.wait_ge(*s.norm2(g + 1))
                    pool.wait_ge(*s.fin_based(g))
                    pool.tensor_tensor(f.OW[:, :, :], f.ON[:, :, :], bcast(w("n2w"), 1, G),
                                       ALU.mult).then_inc(s.fin_scaled.sem, 1)
            pipeline(pool, NG, 3, step)

        @block.tensor
        def _(pe):
            def step(k, p, on):
                q = 1 - p
                if on[2]:
                    g = k - 2
                    pe.wait_ge(*s.h_ready((g + 1) * NC))
                    pe.wait_ge(*s.res_added(g - 1))
                    for j in range(G):
                        for c in range(NC):
                            last = pe.matmul(m.ps[5 + p][:, j * D:(j + 1) * D], HH[:, p, c, j * S:(j + 1) * S],
                                             w("l2")[:, c * D:(c + 1) * D], start=c == 0, stop=c == NC - 1,
                                             skip_group_check=True)
                    last.then_inc(s.projected.sem, 1)
                if on[1]:
                    g = k - 1
                    pe.wait_ge(*s.xt_ready(g + 1))
                    for c in range(NC):
                        pe.wait_ge(*s.h_ready(g * NC + c - NC + 1))
                        pe.matmul(m.ps[1 + c][:, :], w("l1")[:, c * D:(c + 1) * D], f.XT[:, q, :], start=True,
                                  stop=True).then_inc(s.h_done.sem, 1)
                if on[0]:
                    pe.wait_ge(*s.xn_ready(k + 1))
                    pe.wait_ge(*s.xt_ready(k))
                    for j in range(G):
                        last = pe.transpose(m.ps[0][:, j * S:(j + 1) * S], f.U[:, p, j, :], m.c("ident"))
                    last.then_inc(s.x_turned.sem, 1)
            pipeline(pe, NG, 3, step)

        @block.scalar
        def _(act):
            def step(k, p, on):
                if on[1]:
                    g, q = k - 1, 1 - p
                    act.wait_ge(*s.projected(g - 1))
                    for c in range(NC):
                        act.wait_ge(*s.h_done(g * NC + c + 1))
                        act.activation(HH[:, q, c, :], m.ps[1 + c][:, :], ACT.Relu,
                                       bias=w("l1b")[:, c:c + 1]).then_inc(s.h_ready.sem, 1)
                if on[0]:
                    act.wait_ge(*s.x_turned(k + 1))
                    act.wait_ge(*s.h_done((k - 1) * NC))
                    act.activation(f.XT[:, p, :], m.ps[0][:, :], ACT.Identity, bias=w("n1bc"),
                                   scale=w("n1wc")).then_inc(s.xt_ready.sem, 1)
            pipeline(act, NG, 2, step)

        @block.vector
        def _(dve):
            def step(k, p, on):
                if on[0]:
                    dve.wait_ge(*s.summed(k + 1))
                    dve.wait_ge(*s.x_turned(k - 1))
                    dve.wait_ge(*s.scaled(k - 1))
                    layernorm_on(dve, m, s, k, p, G, lambda j: f.YB[:, p, j, :], lambda j: f.U[:, p, j, :],
                                 1e-5).then_inc(s.xn_ready.sem, 1)
                if on[2]:
                    g = k - 2
                    dve.wait_ge(*s.projected(g + 1))
                    dve.wait_ge(*s.based(g + 1))
                    dve.wait_ge(*s.norm2(g))
                    dve.tensor_tensor(f.O[:, :, :], m.ps[5 + p][:, :].rearrange("p (b d) -> p b d", b=G), f.R[:, p],
                                      ALU.add).then_inc(s.res_added.sem, 1)
                    dve.wait_ge(*s.res_added(g + 1))
                    dve.wait_ge(*s.fin_scaled(g))
                    layernorm_on(dve, m.second, s.second, g, p, G, lambda j: f.O[:, j, :], lambda j: f.ON[:, j, :],
                                 1e-5).then_inc(s.norm2.sem, 1)
                    dve.wait_ge(*s.fin_scaled(g + 1))
                    dve.tensor_tensor(f.OW[:, :, :], f.OW[:, :, :], bcast(w("n2b"), 1, G),
                                      ALU.add).then_inc(s.fin_added.sem, 1)
                    dve.wait_ge(*s.fin_added(g + 1))
                    for j in range(G):
                        acc = ACC[:, dyn(g * G + j, 1), :].rearrange("p a d -> p (a d)")
                        last = dve.scalar_tensor_tensor(acc, f.OW[:, j, :], m.G[:, dyn((g * G + j) * E + e, 1)], acc,
                                                        ALU.mult, ALU.add)
                    last.then_inc(s.fin_based.sem, 1)
            pipeline(dve, NG, 3, step)
    s.close(h_done=NG * NC, h_ready=NG * NC, **{n: NG for n in (
        "summed", "xn_ready", "scaled", "based", "norm2", "fin_scaled", "fin_added", "fin_based", "projected",
        "x_turned", "xt_ready", "res_added", "stats", "means", "spread", "vars", "rstd", "nmean", "stats2",
        "means2", "spread2", "vars2", "rstd2", "nmean2")})


def carve(area, shapes):
    views, at = [], 0
    for dims in shapes:
        n = int(np.prod(dims))
        ap = area[:, at:at + n]
        names = "abcd"[:len(dims)]
        if len(dims) > 1:
            ap = ap.rearrange(f"p ({' '.join(names)}) -> p {' '.join(names)}", **dict(zip(names, dims)))
        views.append(ap)
        at += n
    assert at <= area.shape[1]
    return views


def local_buffers(area, sb):
    C = LH * LD
    f = Memory()
    (f.straight, f.swapped, f.XS, f.HT, f.SQ, f.T1, f.T2, f.SS, f.RN, f.QN, f.QZ, f.KT, f.V, f.PR, f.PT,
     f.ON, f.OT
     ) = carve(area, [(2, LD), (2, LD), (2, D), (2, S), (2, C), (2, C), (2, C), (2, LH), (2, LH), (2, 2, C),
        (LH, S), (4, S), (2, LH, LD + 1), (2, C), (2, C), (C,), (C,)])
    return f


def mlp_buffers(area):
    f = Memory()
    (f.XS, f.XN, f.HT, f.GT, f.HH
     ) = carve(area, [(2, G, D), (2, G, D), (2, G * S), (3, G * S), (2, 3, G * S)])
    return f


def program(nc, x, ctx_t, weights, experts, consts, out):
    m = Memory()
    sb = nc.alloc_sbuf_tensor
    m.W = sb("W", [128, WCOLS], F32)
    m.C = sb("C", [128, CCOLS], F32)
    m.X = sb("X", [S, B, D], F32)

    def c(name):
        at, n = CPLACE[name]
        return m.C[:, at:at + n]

    def w(name):
        at, n = WPLACE[name]
        return m.W[:, at:at + n]
    m.c, m.w = c, w
    e0 = WPLACE["f0_wqkv"][0]
    assert e0 + 2 * ECOLS <= WPLACE["m_down"][0]
    m.EW = m.W[:, e0:e0 + 2 * ECOLS].rearrange("p (a c) -> p a c", a=2)
    TOK = B * S
    arena = sb("arena", [128, 4 * TOK + B * H * HD], F32)
    a0 = B * H * HD
    m.arena = arena
    m.V = arena[:, 0:a0].rearrange("p (b h d) -> p b h d", b=B, h=H)
    m.QT = arena[:, a0:a0 + TOK]
    m.KT = arena[:, a0 + TOK:a0 + 2 * TOK]
    m.XTA = arena[:, a0 + 2 * TOK:a0 + 3 * TOK]
    m.XR = arena[:, a0 + 3 * TOK:a0 + 4 * TOK].rearrange("p (b d) -> p b d", b=B)
    m.QKT = arena[:, a0:a0 + 4 * TOK].rearrange("p (b c) -> p b c", b=B)
    m.Y = m.QT.rearrange("p (b d) -> p b d", b=B)
    ring = sb("ring", [128, 7040], F32)
    m.ring = ring
    m.QS = ring[:, 0:1024].rearrange("p (a r s) -> p a r s", a=2, r=NU)
    m.KM = ring[:, 1024:3072].rearrange("p (a t j s) -> p a t j s", a=2, t=2, j=HU)
    m.PR = ring[:, 3072:5120].rearrange("p (a c) -> p a c", a=4)
    m.PT = ring[:, 5120:6144].rearrange("p (a c) -> p a c", a=2)
    m.ON = ring[:, 6144:6400].rearrange("p (a c) -> p a c", a=2)
    m.OT = ring[:, 6400:6528]
    m.OE = ring[:, 6528:7040]
    m.VS = sb("VS", [128, 2, H, 32], F32)
    m.XN = ring[:, 0:1024].rearrange("p (a b d) -> p a b d", a=2, b=G)
    m.XN2 = ring[:, 1024:2048].rearrange("p (a b d) -> p a b d", a=2, b=G)
    m.XT = ring[:, 2048:3072].rearrange("p (a c) -> p a c", a=2)
    m.CT = ring[:, 3072:4096].rearrange("p (a c) -> p a c", a=2)
    m.local = local_buffers(arena[:, 0:2 * TOK + a0], sb)
    m.mlp = mlp_buffers(arena[:, 0:2 * TOK + a0])
    m.mx = sb("mx", [128, 4, 4], F32)
    m.rs = sb("rs", [128, H], F32)
    m.st = sb("st", [128, 2, 3 * G, 6], F32)
    m.df, m.sm, m.cv, m.dd, m.ve, m.rv, m.nm = (sb(n, [128, 2, 3 * G], F32)
                                                for n in ("df", "sm", "cv", "dd", "ve", "rv", "nm"))
    t = m.second = Memory()
    t.st, t.c = sb("st2", [128, 2, 3 * G, 6], F32), c
    t.df, t.sm, t.cv, t.dd, t.ve, t.rv, t.nm = (sb(n + "2", [128, 2, 3 * G], F32)
                                                for n in ("df", "sm", "cv", "dd", "ve", "rv", "nm"))
    m.G = sb("gates", [128, B * E], F32)
    m.GW = sb("gate_work", [128, 64], F32)
    m.ident_bf = sb("ident_bf", [128, 128], BF16)
    m.causal_bf = sb("causal_bf", [128, 128], BF16)
    m.band_bf = sb("band_bf", [128, 128], BF16)
    m.ps = [nc.alloc_psum_tensor(f"bank{i}", [128, 512], F32) for i in range(8)]

    s = Signals(nc)
    e_loaded = [nc.alloc_semaphore(f"expert_loaded{q}") for q in range(2)]
    x_loaded, w_loaded, built = (nc.alloc_semaphore(n) for n in ("x_loaded", "w_loaded", "built"))

    with nc.Block() as block:
        @block.sync
        def _(sp):
            sp.dma_start(m.C[:, :], consts).then_inc(w_loaded, 16)
            sp.dma_start(m.X[:, :, :], x.rearrange("b s d -> s b d")).then_inc(x_loaded, 16)
            sp.dma_start(m.W[:, :], weights).then_inc(x_loaded, 16)
            sp.wait_ge(x_loaded, 32)

        @block.gpsimd
        def _(pool):
            for sig in s.all:
                pool.sem_inc(sig.sem, CREDIT)

        @block.vector
        def _(dve):
            dve.memset(m.VS[:, :, :, HD + 1:32], 0.0)
            dve.memset(m.VS[:, :, :, HD:HD + 1], 1.0)
            dve.wait_ge(w_loaded, 16)
            dve.tensor_copy(m.ident_bf[:, :], m.c("ident"))
            dve.tensor_copy(m.causal_bf[:, :], m.c("causal"))
            dve.tensor_copy(m.band_bf[:, :], m.c("band")).then_inc(built, 1)

    r8 = float(HD) ** -0.5
    project(nc, m, s, ln=False, source="x", ctx=None, wq=w("a_wq"), wk=w("a_wk"), wv=w("a_wv"))
    attention(nc, m, s, causal=False, scale=r8, wide=False, w_out=None, target="x")
    project(nc, m, s, ln=True, source="x", ctx=ctx_t, wq=w("x_wq"), wk=w("x_wk"), wv=w("x_wv"))
    attention(nc, m, s, causal=True, scale=r8, wide=False, w_out=w("x_wo"), target="x")
    normalize(nc, m, s, keep_to=m.XR)
    for d in range(DEPTH):
        local_attention(nc, m, s, d)
        gated_mlp(nc, m, s, d)
    with nc.Block() as block:
        @block.sync
        def _(sp):
            sp.dma_start(m.EW[:, 0, :], experts[0]).then_inc(e_loaded[0], 16)
    project_latent(nc, m, s)
    attention(nc, m, s, causal=True, scale=float(HD + RD) ** -0.5, wide=True, w_out=w("m_o"), target="x")
    project_linear(nc, m, s, ctx_t)
    linear_attention(nc, m, s)
    for e in range(E):
        with nc.Block() as block:
            @block.sync
            def _(sp):
                if e + 1 < E:
                    sp.dma_start(m.EW[:, (e + 1) % 2, :], experts[e + 1]).then_inc(e_loaded[(e + 1) % 2], 16)
                sp.wait_ge(e_loaded[e % 2], 16 * (e // 2 + 1))

        def we(name):
            at, n = EPLACE[name]
            return m.EW[:, e % 2, at:at + n]
        project(nc, m, s, ln=e == 0, source="x" if e == 0 else "xt", ctx=None, wq=we("wq"), wk=we("wk"), wv=we("wv"),
                bq=we("bq"), bk=we("bk"), bv=we("bv"), keep=e == 0)
        if e == 0:
            gates(nc, m, s)
        attention(nc, m, s, causal=False, scale=r8, wide=False, w_out=we("ow"), target="y")
        expert_mlp(nc, m, s, we, e)
    normalize(nc, m, s, add=m.XR, out=out)


def shape_tables():
    f = np.float32
    t = {n: np.zeros((128, k), f) for n, k in CONSTS}
    p = np.arange(128)
    t["ident"][p, p] = 1
    t["ones"][:] = 1
    t["minus_half"][:] = -0.5
    t["kmask"][p, (p // HD) % HU] = 1
    t["kmask_wide"][p, (p // HD) % HU] = 1
    t["kmask_wide"][(p % 64) >= 32] = 1
    i, j = p[:, None], p[None, :]
    t["qmask"][p, p // 32] = 1
    t["qmask_wide"][p, p // 64] = 1
    t["causal"][:] = np.where(j > i, NEG, 0)
    t["band"][:] = np.where((j > i) | (i > j + WINDOW), NEG, 0)
    t["shift"][p[:-1], p[:-1] + 1] = 1
    t["blocks_sel"][:, 0:D] = (i // HD) == (j // HD)
    t["blocks_sel"][p, D + p // HD] = 1
    half = np.arange(0, LD, 2, dtype=f)
    freqs = p[:, None].astype(f) * (f(1.0) / f(10000.0) ** (half / f(LD)))[None]
    base = (half + f(0.4 * LD)) / f(1.4 * LD)
    power = (p - S // 2).astype(f) / f(WINDOW // 2)
    sc = base[None] ** power[:, None]
    cos, sin = np.cos(freqs), np.sin(freqs)
    t["qcos"][:] = np.concatenate([cos * sc, cos * sc], 1)
    t["qsin"][:] = np.concatenate([-sin * sc, sin * sc], 1)
    t["kcos"][:] = np.concatenate([cos / sc, cos / sc], 1)
    t["ksin"][:] = np.concatenate([-sin / sc, sin / sc], 1)
    fr = np.outer(p.astype(f), f(1.0) / f(10000.0) ** (np.arange(0, RD, 2, dtype=f) / f(RD)))
    cos, sin = np.cos(fr).T, np.sin(fr).T
    still, none = np.ones((32, S), f), np.zeros((32, S), f)
    t["ropecos"][:] = np.concatenate([still, cos, cos] * 2)
    t["ropesin"][:] = np.concatenate([none, -sin, sin] * 2)
    for par in range(2):
        t["place"][p, par * 2 * H + par * H + p % H] = 1
    t["block"][p, p // H] = 1
    t["lower"][:] = [i < j for j in range(E) for i in range(E)]
    for b in range(B):
        t["seqsel"][b, b * E:(b + 1) * E] = 1
    return np.concatenate([t[n] for n, _ in CONSTS], 1)


def pack_weights(a):
    def rep(v):
        return np.broadcast_to(np.asarray(v).reshape(1, -1), (128, np.asarray(v).size))

    def pad(v, rows=128):
        z = np.zeros((rows, v.shape[1]), np.float32)
        z[:v.shape[0]] = v
        return z

    def rows_to_chunks(v):
        return v.reshape(-1, 128, v.shape[1]).transpose(1, 0, 2).reshape(128, -1)

    def latent(heads, rope):
        none = np.zeros((D, 32), np.float32)
        part = [heads[:, i:i + 32] for i in range(0, D, 32)]
        partner = np.concatenate([rope[:, RD // 2:], rope[:, :RD // 2]], 1)
        return np.concatenate([none, partner, none, partner, part[0], rope, part[1], rope,
                               part[2], rope, part[3], rope], 1)

    w = {
        "a_wq": a["L0_attn_Wq"].T, "a_wk": np.tile(a["L0_attn_Wk"].T, (1, H)),
        "a_wv": np.tile(a["L0_attn_Wv"].T, (1, H)),
        "x_wq": a["L0_xattn_Wq"].T, "x_wk": a["L0_xattn_Wk"].T, "x_wv": a["L0_xattn_Wv"].T,
        "x_wo": a["L0_xattn_Wo"].T,
        "m_down": a["L1_attn_W_kv_down"],
        "m_q": latent(a["L1_attn_W_q"], a["L1_attn_W_q_rope"]),
        "m_k": latent(a["L1_attn_W_k_up"], a["L1_attn_W_k_rope"]), "m_v": a["L1_attn_W_v_up"],
        "m_o": a["L1_attn_W_o"],
        "y_wq": a["L1_xattn_wq"], "y_wkv": np.concatenate([a["L1_xattn_wk"], a["L1_xattn_wv"]], 1),
        "y_gamma": rep(a["L1_xattn_ln_gamma"]), "y_beta": rep(a["L1_xattn_ln_beta"]),
        "y_dw": a["L1_xattn_dense_w"].reshape(H, HD, D).transpose(1, 0, 2).reshape(D, D), "y_db": rep(a["L1_xattn_dense_b"]),
        "em": a["mask_BxS2_ff1"].T,
        "gate_w": a["L1_ffn_gate_w"].T, "gate_b": rep(a["L1_ffn_gate_b"]),
    }
    for d in range(DEPTH):
        b1 = a["L0_ffn_b1"][d]
        cols = []
        for half in (0, HID):
            for at, n in HCH:
                cols.append(pad(b1[half + at:half + at + n].reshape(n, 1)))
        w.update({
            f"f{d}_wqkv": a["L0_ffn_wqkv"][d], f"f{d}_qs": rep(a["L0_ffn_q_scale"][d]),
            f"f{d}_ks": rep(a["L0_ffn_k_scale"][d]), f"f{d}_wo": rows_to_chunks(a["L0_ffn_wo"][d]),
            f"f{d}_lg": a["L0_ffn_ln_g"][d].reshape(D, 1), f"f{d}_lb": a["L0_ffn_ln_b"][d].reshape(D, 1),
            f"f{d}_w1": a["L0_ffn_w1"][d], f"f{d}_b1": np.concatenate(cols, 1),
            f"f{d}_w2": rows_to_chunks(pad(a["L0_ffn_w2"][d], 384)), f"f{d}_b2": rep(a["L0_ffn_b2"][d]),
        })
    for e in range(E):
        iw, ib = a["L1_ffn_in_proj_w"][e], a["L1_ffn_in_proj_b"][e]
        w.update({
            f"e{e}_wq": iw[0:D].T, f"e{e}_wk": iw[D:2 * D].T, f"e{e}_wv": iw[2 * D:].T,
            f"e{e}_bq": ib[0:D].reshape(D, 1), f"e{e}_bk": ib[D:2 * D].reshape(D, 1), f"e{e}_bv": rep(ib[2 * D:]),
            f"e{e}_ow": a["L1_ffn_out_proj_w"][e].T, f"e{e}_ob": rep(a["L1_ffn_out_proj_b"][e]),
            f"e{e}_n1w": rep(a["L1_ffn_ln1_w"][e]), f"e{e}_n1b": rep(a["L1_ffn_ln1_b"][e]),
            f"e{e}_n1wc": a["L1_ffn_ln1_w"][e].reshape(D, 1), f"e{e}_n1bc": a["L1_ffn_ln1_b"][e].reshape(D, 1),
            f"e{e}_l1": a["L1_ffn_lin1_w"][e].T, f"e{e}_l1b": a["L1_ffn_lin1_b"][e].reshape(DFF // D, D).T,
            f"e{e}_l2": rows_to_chunks(a["L1_ffn_lin2_w"][e].T), f"e{e}_l2b": rep(a["L1_ffn_lin2_b"][e]),
            f"e{e}_n2w": rep(a["L1_ffn_ln2_w"][e]), f"e{e}_n2b": rep(a["L1_ffn_ln2_b"][e]),
        })
    experts = np.stack([np.concatenate([w[f"e{e}_{n}"] for n, _ in EXPERT], 1) for e in range(E)])
    return np.ascontiguousarray(np.concatenate([w[n] for n, _ in WEIGHTS], 1)), experts


def kernel(**inputs):
    import concourse.bacc as _bacc
    from concourse.bass_utils import run_bass_kernel_spmd as _run

    a = {n: np.asarray(v) for n, v in inputs.items()}
    weights, experts = pack_weights(a)
    arrays = {
        "x": np.ascontiguousarray(a["x"]),
        "ctx_t": np.ascontiguousarray(a["ctx_1024"].reshape(B * S, D).T),
        "weights": weights,
        "experts": experts,
        "consts": shape_tables(),
    }
    nc = _bacc.Bacc("TRN2", target_bir_lowering=False, num_devices=1)
    args = [nc.dram_tensor(n, v.shape, F32, kind="ExternalInput").ap() for n, v in arrays.items()]
    out = nc.dram_tensor("out", (B, S, D), F32, kind="ExternalOutput").ap()
    program(nc, *args, out)
    r = _run(nc, [arrays], core_ids=[0])
    return r.results[0]["out"]
```

```python
import numpy as np

import concourse.bass as bass
from concourse import mybir

F32 = mybir.dt.float32
F32R = mybir.dt.float32r
U32 = mybir.dt.uint32
BF16 = mybir.dt.bfloat16
ACT = mybir.ActivationFunctionType
ALU = mybir.AluOpType
AXX = mybir.AxisListType.X

B, S, D = 32, 128, 128
G = 4
NG = B // G
H, HD = 16, 8
HU = 4
NU = H // HU
LH, LD, WINDOW = 8, 64, 64
DEPTH = 2
HID = D * 4 * 2 // 3
HCH = [(0, 128), (128, 128), (256, HID - 256)]
RD = 32
E, DFF = 4, 512
NEG = -1.0e30
HIGH_BITS = 0xFFFFF000
CREDIT = 8


class Memory:
    pass


def bcast(ap, dim, n):
    a = ap.unsqueeze(dim)
    shape = list(a.shape)
    shape[dim] = n
    return a.broadcast_to(shape)


class Signal:

    def __init__(self, nc, name):
        self.name = name
        self.sem = nc.alloc_semaphore(name)
        self.base = CREDIT

    def __call__(self, n):
        return self.sem, n + self.base


class Signals:

    def __init__(self, nc):
        self.all = []
        self.hi_ready = self.new(nc, "hi_ready")
        self.lo_ready = self.new(nc, "lo_ready")
        self.c_done = self.new(nc, "c_done")
        self.c_ready = self.new(nc, "c_ready")
        self.unit_done = self.new(nc, "unit_done")
        self.unit_ready = self.new(nc, "unit_ready")
        self.rotated = self.new(nc, "rotated")
        self.stats2 = self.new(nc, "stats2")
        self.means2 = self.new(nc, "means2")
        self.spread2 = self.new(nc, "spread2")
        self.vars2 = self.new(nc, "vars2")
        self.rstd2 = self.new(nc, "rstd2")
        self.nmean2 = self.new(nc, "nmean2")
        self.norm2 = self.new(nc, "norm2")
        self.g_steps = self.new(nc, "g_steps")
        self.g_compared = self.new(nc, "g_compared")
        self.g_rows = self.new(nc, "g_rows")
        self.fin_added = self.new(nc, "fin_added")
        self.em_ready = self.new(nc, "em_ready")
        self.zm_ready = self.new(nc, "zm_ready")
        self.scaled = self.new(nc, "scaled")
        self.based = self.new(nc, "based")
        self.kv_done = self.new(nc, "kv_done")
        self.kv_ready = self.new(nc, "kv_ready")
        self.at_done = self.new(nc, "at_done")
        self.z_added = self.new(nc, "z_added")
        self.z_ready = self.new(nc, "z_ready")
        self.at_ready = self.new(nc, "at_ready")
        self.at_turned = self.new(nc, "at_turned")
        self.att_ready = self.new(nc, "att_ready")
        self.ebias = self.new(nc, "ebias")
        self.h_done = self.new(nc, "h_done")
        self.h_ready = self.new(nc, "h_ready")
        self.res_added = self.new(nc, "res_added")
        self.fin_norm = self.new(nc, "fin_norm")
        self.fin_scaled = self.new(nc, "fin_scaled")
        self.fin_based = self.new(nc, "fin_based")
        self.tables = self.new(nc, "tables")
        self.xs_ready = self.new(nc, "xs_ready")
        self.ht_ready = self.new(nc, "ht_ready")
        self.q_sq = self.new(nc, "q_sq")
        self.k_sq = self.new(nc, "k_sq")
        self.q_rot = self.new(nc, "q_rot")
        self.k_rot = self.new(nc, "k_rot")
        self.q_ss = self.new(nc, "q_ss")
        self.k_ss = self.new(nc, "k_ss")
        self.q_norm = self.new(nc, "q_norm")
        self.k_norm = self.new(nc, "k_norm")
        self.q_turned = self.new(nc, "q_turned")
        self.k_turned = self.new(nc, "k_turned")
        self.floored = self.new(nc, "floored")
        self.powered = self.new(nc, "powered")
        self.parts_added = self.new(nc, "parts_added")
        self.biased = self.new(nc, "biased")
        self.x_shifted = self.new(nc, "x_shifted")
        self.shift_in = self.new(nc, "shift_in")
        self.g_done = self.new(nc, "g_done")
        self.a_done = self.new(nc, "a_done")
        self.gelued = self.new(nc, "gelued")
        self.gated = self.new(nc, "gated")
        self.staged = self.new(nc, "staged")
        self.v_staged = self.new(nc, "v_staged")
        self.oe_ready = self.new(nc, "oe_ready")
        self.o_turned = self.new(nc, "o_turned")
        self.scored = self.new(nc, "scored")
        self.maxed = self.new(nc, "maxed")
        self.shifted = self.new(nc, "shifted")
        self.exped = self.new(nc, "exped")
        self.turned = self.new(nc, "turned")
        self.pt_ready = self.new(nc, "pt_ready")
        self.mixed = self.new(nc, "mixed")
        self.inverted = self.new(nc, "inverted")
        self.divided = self.new(nc, "divided")
        self.added = self.new(nc, "added")
        self.on_turned = self.new(nc, "on_turned")
        self.ot_ready = self.new(nc, "ot_ready")
        self.projected = self.new(nc, "projected")
        self.xn_ready = self.new(nc, "xn_ready")
        self.x_turned = self.new(nc, "x_turned")
        self.xt_ready = self.new(nc, "xt_ready")
        self.xt_kept = self.new(nc, "xt_kept")
        self.x_kept = self.new(nc, "x_kept")
        self.q_done = self.new(nc, "q_done")
        self.k_done = self.new(nc, "k_done")
        self.v_done = self.new(nc, "v_done")
        self.q_ready = self.new(nc, "q_ready")
        self.k_ready = self.new(nc, "k_ready")
        self.v_ready = self.new(nc, "v_ready")
        self.stats = self.new(nc, "stats")
        self.means = self.new(nc, "means")
        self.spread = self.new(nc, "spread")
        self.vars = self.new(nc, "vars")
        self.rstd = self.new(nc, "rstd")
        self.nmean = self.new(nc, "nmean")
        self.summed = self.new(nc, "summed")
        self.stored = self.new(nc, "stored")
        self.ct_loaded = [self.new(nc, "ct_loaded0"), self.new(nc, "ct_loaded1")]
        self.second = Memory()
        self.second.stats, self.second.means, self.second.spread = self.stats2, self.means2, self.spread2
        self.second.vars, self.second.rstd, self.second.nmean = self.vars2, self.rstd2, self.nmean2

    def new(self, nc, name):
        self.all.append(Signal(nc, name))
        return self.all[-1]

    def close(self, **counts):
        for signal in self.all:
            signal.base += counts.get(signal.name, 0)


def pipeline(eng, n, depth, step):
    head = (depth - 1) + (depth - 1) % 2
    for k in range(head):
        step(k, k % 2, [0 <= k - d < n for d in range(depth)])
    with eng.Fori(head // 2, n // 2) as i:
        for p in range(2):
            step(i * 2 + p, p, [True] * depth)
    for k in range(n, n + depth - 1):
        step(k, k % 2, [0 <= k - d < n for d in range(depth)])


def dyn(start, size):
    return slice(start, start + size) if isinstance(start, int) else bass.ds(start, size)


def columns(parts):
    place, at = {}, 0
    for name, n in parts:
        place[name] = (at, n)
        at += n
    return place, at


CONSTS = [("ident", D), ("kmask", HU), ("kmask_wide", HU), ("qmask", NU), ("qmask_wide", 2), ("causal", S), ("band", S), ("shift", S),
          ("ones", D), ("blocks_sel", D + H), ("qcos", LD), ("qsin", LD), ("kcos", LD), ("ksin", LD),
          ("ropecos", S), ("ropesin", S), ("minus_half", 16), ("place", 4 * H), ("block", HD), ("lower", E * E),
          ("seqsel", B * E)]
FFN = [("wqkv", 3 * LH * LD), ("qs", LD), ("ks", LD), ("wo", LH * LD), ("lg", 1), ("lb", 1), ("w1", 2 * HID),
       ("b1", 6), ("w2", 3 * D), ("b2", D)]
EXPERT = [("wq", D), ("wk", D), ("wv", D), ("bq", 1), ("bk", 1), ("bv", D), ("ow", D), ("ob", D), ("n1w", D),
          ("n1b", D), ("n1wc", 1), ("n1bc", 1), ("l1", DFF), ("l1b", DFF // D), ("l2", DFF), ("l2b", D), ("n2w", D), ("n2b", D)]
WEIGHTS = ([("a_wq", D), ("a_wk", D), ("a_wv", D), ("x_wq", D), ("x_wk", D), ("x_wv", D), ("x_wo", D)]
           + [(f"f{d}_{n}", w) for d in range(DEPTH) for n, w in FFN]
           + [("m_down", D), ("m_q", 3 * D), ("m_k", 3 * D), ("m_v", D), ("m_o", D)]
           + [("y_wq", D), ("y_wkv", 2 * D), ("y_gamma", D), ("y_beta", D), ("y_dw", D), ("y_db", D),
              ("em", B)]
           + [("gate_w", E), ("gate_b", E)])
CPLACE, CCOLS = columns(CONSTS)
WPLACE, WCOLS = columns(WEIGHTS)
EPLACE, ECOLS = columns(EXPERT)


def attention(nc, m, s, *, causal, scale, wide, w_out, target):
    kmask = m.c("kmask_wide") if wide else m.c("kmask")

    with nc.Block() as block:
        @block.gpsimd
        def _(pool):
            def stage(b, p):
                pool.wait_ge(*s.hi_ready(b + 1))
                pool.wait_ge(*s.lo_ready(b))
                if wide:
                    pool.tensor_tensor(m.LO[:, p], m.QKT[:, dyn(b, 1), :].rearrange("p a (t s) -> p (a t) s", t=4),
                                       m.HI[:, p], ALU.subtract).then_inc(s.lo_ready.sem, 1)
                else:
                    pool.tensor_tensor(m.LO[:, p, 0], m.QT[:, dyn(b * S, S)], m.HI[:, p, 0], ALU.subtract)
                    pool.tensor_tensor(m.LO[:, p, 2], m.KT[:, dyn(b * S, S)], m.HI[:, p, 2],
                                       ALU.subtract).then_inc(s.lo_ready.sem, 1)
                pool.wait_ge(*s.scored((b - 1) * NU))
                pool.wait_ge(*s.lo_ready(b + 1))
                for i, part in enumerate((m.HI[:, p], m.LO[:, p])):
                    if wide:
                        pool.tensor_tensor(m.QS[:, p, i].rearrange("p (t h) s -> p t h s", h=2),
                                           bcast(part[:, 0:2, :], 2, 2),
                                           bcast(bcast(m.c("qmask_wide"), 1, 2), 3, S), ALU.mult)
                    else:
                        pool.tensor_tensor(m.QS[:, p, i], bcast(part[:, 0, :], 1, NU),
                                           bcast(m.c("qmask"), 2, S), ALU.mult)
                    for t in range(2 if wide else 1):
                        last = pool.tensor_tensor(m.KM[:, p, i, t], bcast(part[:, 2 + t, :], 1, HU),
                                                  bcast(kmask, 2, S), ALU.mult)
                last.then_inc(s.staged.sem, 1)

            def step(k, p, on):
                if on[0]:
                    stage(k, p)
                if on[1] and not wide:
                    pool.wait_ge(*s.mixed((k - 2) * NU))
                    pool.tensor_copy(m.VS[:, 1 - p, :, 0:HD],
                                     m.V[:, dyn(k - 1, 1), :, :].rearrange("p a h d -> p (a h) d")
                                     ).then_inc(s.v_staged.sem, 1)
            pipeline(pool, B, 2, step)

        @block.tensor
        def _(pe):
            def mix(b, q, r):
                pe.wait_ge(*s.pt_ready(b * NU + r + 1))
                if r == 0:
                    pe.wait_ge(*s.v_staged(b + 1))
                    pe.wait_ge(*s.oe_ready(b))
                for j in range(HU):
                    last = pe.matmul(m.ps[6][32 * j:32 * j + 32, r * S:(r + 1) * S], m.VS[:, q, r * HU + j, :],
                                     m.PT[:, r % 2, j * S:(j + 1) * S], start=True, stop=True,
                                     skip_group_check=True)
                last.then_inc(s.mixed.sem, 1)

            def step(k, p, on):
                b, q = k - 1, 1 - p
                for r in range(NU):
                    if on[1]:
                        pe.wait_ge(*s.exped(b * NU + r + 1))
                        pe.wait_ge(*s.pt_ready(b * NU + r - 1))
                        for j in range(HU):
                            last = pe.transpose(m.ps[4 + r % 2][:, j * S:(j + 1) * S],
                                                m.PR[:, r, j * S:(j + 1) * S], m.c("ident"))
                        last.then_inc(s.turned.sem, 1)
                    if on[0]:
                        pe.wait_ge(*s.staged(k + 1))
                        pe.wait_ge(*s.shifted(k * NU + r - NU + 1))
                        if causal:
                            pe.matmul(m.ps[r][:, :], m.ident_bf[:, :], bcast(m.causal_bf[:, :], 1, HU),
                                      start=True, stop=False)
                        for i, (qi, ki) in enumerate(((0, 0), (1, 0), (0, 1))):
                            last = pe.matmul(m.ps[r][:, :], m.QS[:, p, qi, r, :],
                                             m.KM[:, p, ki, r // 2 if wide else 0].rearrange("p j s -> p (j s)"),
                                             start=i == 0 and not causal, stop=i == 2)
                        last.then_inc(s.scored.sem, 1)
                    if w_out is not None and on[3] and r == 0:
                        pe.wait_ge(*s.divided(k - 2))
                        pe.transpose(m.ps[7][:, 0:S], m.ON[:, q, :], m.c("ident")).then_inc(s.on_turned.sem, 1)
                    if w_out is not None and on[3] and r == 1:
                        pe.wait_ge(*s.ot_ready(k - 2))
                        pe.matmul(m.ps[7][:, 0:D], m.OT[:, :], w_out, start=True,
                                  stop=True).then_inc(s.projected.sem, 1)
                    if r > 0 and on[1]:
                        mix(b, q, r - 1)
                    if r == 0 and on[2]:
                        mix(k - 2, p, NU - 1)
                    if on[2] and r == 2:
                        pe.wait_ge(*s.oe_ready(k - 1))
                        pe.wait_ge(*(s.added if w_out is not None else s.divided)(k - 2))
                        for u in range(NU):
                            last = pe.transpose(m.ps[7][:, u * S:(u + 1) * S], m.OE[:, u * S:(u + 1) * S],
                                                m.c("ident"))
                        last.then_inc(s.o_turned.sem, 1)
            pipeline(pe, B, 4, step)

        @block.scalar
        def _(act):
            def evacuate(b, r):
                act.wait_ge(*s.turned(b * NU + r + 1))
                act.wait_ge(*s.mixed(b * NU + r - 1))
                act.activation(m.PT[:, r % 2, :], m.ps[4 + r % 2][:, :], ACT.Copy).then_inc(s.pt_ready.sem, 1)

            def exp(b, r):
                act.wait_ge(*s.shifted(b * NU + r + 1))
                act.activation(m.PR[:, r, :], m.PR[:, r, :], ACT.Exp, scale=scale).then_inc(s.exped.sem, 1)

            def step(k, p, on):
                for r in range(NU):
                    if on[1]:
                        evacuate(k - 1, r)
                    if r < 2 and on[1]:
                        exp(k - 1, r + 2)
                    if r >= 2 and on[0]:
                        exp(k, r - 2)
                    if w_out is not None and on[3] and r == 0:
                        act.wait_ge(*s.on_turned(k - 2))
                        act.activation(m.OT[:, :], m.ps[7][:, 0:S], ACT.Copy).then_inc(s.ot_ready.sem, 1)
                    if on[2] and r == 0:
                        act.wait_ge(*s.mixed((k - 1) * NU))
                        act.wait_ge(*s.o_turned(k - 2))
                        act.activation(m.OE[:, :], m.ps[6][:, :], ACT.Copy).then_inc(s.oe_ready.sem, 1)
                    if wide and on[0] and r == 1:
                        act.wait_ge(*s.mixed((k - 1) * NU))
                        act.activation(m.VS[:, p, :, 0:HD],
                                       m.V[:, dyn(k, 1), :, :].rearrange("p a h d -> p (a h) d"),
                                       ACT.Copy).then_inc(s.v_staged.sem, 1)
            pipeline(act, B, 4, step)

        @block.vector
        def _(dve):
            def high(b, p):
                dve.wait_ge(*s.staged(b - 1))
                if wide:
                    dve.tensor_scalar(m.HI[:, p].bitcast(U32),
                                      m.QKT[:, dyn(b, 1), :].rearrange("p a (t s) -> p (a t) s", t=4).bitcast(U32),
                                      HIGH_BITS, None, ALU.bitwise_and).then_inc(s.hi_ready.sem, 1)
                else:
                    dve.tensor_scalar(m.HI[:, p, 0].bitcast(U32), m.QT[:, dyn(b * S, S)].bitcast(U32), HIGH_BITS,
                                      None, ALU.bitwise_and)
                    dve.tensor_scalar(m.HI[:, p, 2].bitcast(U32), m.KT[:, dyn(b * S, S)].bitcast(U32), HIGH_BITS,
                                      None, ALU.bitwise_and).then_inc(s.hi_ready.sem, 1)

            def maximum(b, r):
                dve.wait_ge(*s.scored(b * NU + r + 1))
                dve.tensor_reduce(m.mx[:, r, :], m.ps[r][:, :].rearrange("p (j s) -> p j s", j=HU),
                                  AXX, ALU.max).then_inc(s.maxed.sem, 1)

            def shift(b, r):
                dve.wait_ge(*s.maxed(b * NU + r + 1))
                dve.wait_ge(*s.turned(b * NU + r - NU + 1))
                dve.tensor_tensor(m.PR[:, r, :].rearrange("p (j s) -> p j s", j=HU),
                                  m.ps[r][:, :].rearrange("p (j s) -> p j s", j=HU),
                                  bcast(m.mx[:, r, :], 2, S), ALU.subtract).then_inc(s.shifted.sem, 1)

            o = m.ps[7][:, :].rearrange("p (h d) -> p h d", h=H)

            def invert(b):
                dve.wait_ge(*s.o_turned(b + 1))
                dve.reciprocal(m.rs[:, :], o[:, :, HD]).then_inc(s.inverted.sem, 1)

            def divide(b, p):
                dve.wait_ge(*s.inverted(b + 1))
                if w_out is not None:
                    dve.wait_ge(*s.on_turned(b - 1))
                dve.tensor_tensor(m.ON[:, p, :].rearrange("p (h d) -> p h d", h=H), o[:, :, 0:HD],
                                  bcast(m.rs[:, :], 2, HD), ALU.mult).then_inc(s.divided.sem, 1)

            def add(b, p):
                x = m.X[:, dyn(b, 1), :].rearrange("p a d -> p (a d)")
                if w_out is not None:
                    dve.wait_ge(*s.projected(b + 1))
                    src = m.ps[7][:, 0:D]
                else:
                    dve.wait_ge(*s.divided(b + 1))
                    src = m.ON[:, p, :]
                dst = x if target == "x" else m.QT[:, dyn(b * S, S)]
                dve.tensor_tensor(dst, src, x, ALU.add).then_inc(s.added.sem, 1)

            def step(k, p, on):
                if on[2]:
                    maximum(k - 2, 0)
                    maximum(k - 2, 1)
                    shift(k - 2, 0)
                if on[5]:
                    add(k - 5, 1 - p)
                if on[2]:
                    maximum(k - 2, 2)
                    shift(k - 2, 1)
                if on[0]:
                    high(k, p)
                if on[4]:
                    invert(k - 4)
                if on[2]:
                    maximum(k - 2, 3)
                if on[4]:
                    divide(k - 4, p)
                if on[2]:
                    shift(k - 2, 2)
                    shift(k - 2, 3)
            pipeline(dve, B, 6, step)
    s.close(hi_ready=B, lo_ready=B, staged=B, v_staged=B, scored=NU * B, maxed=NU * B, shifted=NU * B, exped=NU * B, turned=NU * B,
            pt_ready=NU * B, mixed=NU * B, oe_ready=B, o_turned=B, inverted=B, divided=B, added=B)
    if w_out is not None:
        s.close(on_turned=B, ot_ready=B, projected=B)


def ln_stats(dve, m, s, g, p, n, src, eps):
    for j in range(n):
        last = dve.bn_stats(m.st[:, p, j, :], src(j))
    last.then_inc(s.stats.sem, 1)
    dve.wait_ge(*s.stats(g + 1))
    st = m.st[:, p, 0:n, :]
    dve.tensor_tensor(m.df[:, p, 0:n], st[:, :, 1], st[:, :, 4], ALU.subtract)
    dve.tensor_tensor(m.sm[:, p, 0:n], st[:, :, 1], st[:, :, 4], ALU.add)
    dve.scalar_tensor_tensor(m.cv[:, p, 0:n], st[:, :, 2], eps * D, st[:, :, 5], ALU.add,
                             ALU.add).then_inc(s.means.sem, 1)
    dve.wait_ge(*s.means(g + 1))
    dve.scalar_tensor_tensor(m.dd[:, p, 0:n], m.df[:, p, 0:n], 0.25, m.df[:, p, 0:n], ALU.mult,
                             ALU.mult).then_inc(s.spread.sem, 1)
    dve.wait_ge(*s.spread(g + 1))
    dve.scalar_tensor_tensor(m.ve[:, p, 0:n], m.cv[:, p, 0:n], 1.0 / D, m.dd[:, p, 0:n], ALU.mult,
                             ALU.add).then_inc(s.vars.sem, 1)


def ln_apply(dve, m, s, g, p, n, src, dst):
    dve.wait_ge(*s.rstd(g + 1))
    dve.scalar_tensor_tensor(m.nm[:, p, 0:n], m.sm[:, p, 0:n], -0.5, m.rv[:, p, 0:n], ALU.mult,
                             ALU.mult).then_inc(s.nmean.sem, 1)
    dve.wait_ge(*s.nmean(g + 1))
    for j in range(n):
        last = dve.tensor_scalar(dst(j), src(j), m.rv[:, p, j:j + 1], m.nm[:, p, j:j + 1], ALU.mult, ALU.add)
    return last


def rstd_on(pool, m, s, g, p, n):
    pool.wait_ge(*s.vars(g + 1))
    pool.tensor_tensor(m.rv[:, p, 0:n], m.ve[:, p, 0:n], m.c("minus_half")[:, 0:n], ALU.pow).then_inc(s.rstd.sem, 1)


def project(nc, m, s, *, ln, source, ctx, wq, wk, wv, bq=None, bk=None, bv=None, keep=False):
    v_at = 3 if ln else 1
    with nc.Block() as block:
        if ctx is not None:
            @block.sync
            def _(sp):
                def step(g, p, on):
                    sp.wait_ge(*s.v_done(g - 1))
                    sp.dma_start(m.CT[:, p, :], ctx[:, dyn(g * G * S, G * S)]).then_inc(s.ct_loaded[p].sem, 16)
                pipeline(sp, NG, 1, step)

        @block.gpsimd
        def _(pool):
            def step(k, p, on):
                if on[0]:
                    if source == "xt":
                        pool.wait_ge(*s.v_done(k - 1))
                        pool.tensor_copy(m.XT[:, p, :], m.XTA[:, dyn(k * G * S, G * S)]).then_inc(s.xt_ready.sem, 1)
                    elif ln:
                        rstd_on(pool, m, s, k, p, G)
                    else:
                        pool.wait_ge(*s.x_turned(k - 1))
                        pool.tensor_copy(m.XN[:, p], m.X[:, dyn(k * G, G), :]).then_inc(s.xn_ready.sem, 1)
                if on[1]:
                    g, q = k - 1, 1 - p
                    x = m.X[:, dyn(g * G, G), :]
                    if ln:
                        pool.wait_ge(*s.xn_ready(g + 1))
                        pool.tensor_copy(x, m.XN[:, q]).then_inc(s.x_kept.sem, 1)
                    if keep:
                        pool.wait_ge(*s.xt_ready(g + 1))
                        pool.tensor_copy(m.XTA[:, dyn(g * G * S, G * S)], m.XT[:, q, :]).then_inc(s.xt_kept.sem, 1)
            pipeline(pool, NG, 2, step)

        @block.tensor
        def _(pe):
            def turn(g, p):
                pe.wait_ge(*s.xn_ready(g + 1))
                pe.wait_ge(*s.xt_ready(g - 1))
                for j in range(G):
                    last = pe.transpose(m.ps[p][:, j * S:(j + 1) * S], m.XN[:, p, j, :], m.c("ident"))
                last.then_inc(s.x_turned.sem, 1)

            def keys_values(g, p, src):
                pe.wait_ge(*s.k_ready(g - 1))
                pe.matmul(m.ps[4 + p][:, :], wk, src[:, p, :], start=True, stop=True).then_inc(s.k_done.sem, 1)
                pe.wait_ge(*s.v_ready(g - 1))
                for j in range(G):
                    last = pe.matmul(m.ps[6 + p][:, j * D:(j + 1) * D], src[:, p, j * S:(j + 1) * S], wv,
                                     start=True, stop=True)
                last.then_inc(s.v_done.sem, 1)

            def step(k, p, on):
                if source == "x" and on[0]:
                    turn(k, p)
                if on[1]:
                    g, q = k - 1, 1 - p
                    if ctx is not None:
                        pe.wait_ge(s.ct_loaded[q].sem, (k - 1 - q) * 8 + 16 + s.ct_loaded[q].base)
                        keys_values(g, q, m.CT)
                    pe.wait_ge(*s.xt_ready(g + 1))
                    pe.wait_ge(*s.q_ready(g - 1))
                    pe.matmul(m.ps[2 + q][:, :], wq, m.XT[:, q, :], start=True, stop=True).then_inc(s.q_done.sem, 1)
                    if ctx is None:
                        keys_values(g, q, m.XT)
            pipeline(pe, NG, 2, step)

        @block.scalar
        def _(act):
            def step(k, p, on):
                if source == "x" and on[0]:
                    act.wait_ge(*s.x_turned(k + 1))
                    act.wait_ge(*s.q_done(k - 1))
                    act.wait_ge(*s.v_done(k - 1))
                    if keep:
                        act.wait_ge(*s.xt_kept(k - 1))
                    act.activation(m.XT[:, p, :], m.ps[p][:, :], ACT.Copy).then_inc(s.xt_ready.sem, 1)
                if on[1]:
                    g, q = k - 1, 1 - p
                    cols = dyn(g * (G * S), G * S)
                    act.wait_ge(*s.q_done(g + 1))
                    if bq is None:
                        act.activation(m.QT[:, cols], m.ps[2 + q][:, :], ACT.Copy).then_inc(s.q_ready.sem, 1)
                    else:
                        act.activation(m.QT[:, cols], m.ps[2 + q][:, :], ACT.Identity,
                                       bias=bq).then_inc(s.q_ready.sem, 1)
                    act.wait_ge(*s.k_done(g + 1))
                    if bk is None:
                        act.activation(m.KT[:, cols], m.ps[4 + q][:, :], ACT.Copy).then_inc(s.k_ready.sem, 1)
                    else:
                        act.activation(m.KT[:, cols], m.ps[4 + q][:, :], ACT.Identity,
                                       bias=bk).then_inc(s.k_ready.sem, 1)
                    if bv is None:
                        act.wait_ge(*s.v_done(g + 1))
                        act.activation(m.V[:, dyn(g * G, G), :, 0:HD],
                                       m.ps[6 + q][:, :].rearrange("p (b h d) -> p b h d", b=G, h=H),
                                       ACT.Copy).then_inc(s.v_ready.sem, 1)
            pipeline(act, NG, 2, step)

        @block.vector
        def _(dve):
            def step(k, p, on):
                x = lambda g: lambda j: m.X[:, dyn(g * G + j, 1), :].rearrange("p a d -> p (a d)")
                if ln and on[0]:
                    ln_stats(dve, m, s, k, p, G, x(k), 1e-5)
                g, q = k - 1, 1 - p
                if ln and on[1]:
                    dve.wait_ge(*s.x_turned(g - 1))
                    dve.wait_ge(*s.x_kept(g - 1))
                    ln_apply(dve, m, s, g, q, G, x(g), lambda j: m.XN[:, q, j, :]).then_inc(s.xn_ready.sem, 1)
                if bv is not None and on[v_at]:
                    g, q = k - v_at, 1 - p
                    dve.wait_ge(*s.v_done(g + 1))
                    for j in range(G):
                        last = dve.tensor_tensor(
                            m.V[:, dyn(g * G + j, 1), :, 0:HD].rearrange("p a h d -> p (a h) d"),
                            m.ps[6 + q][:, j * D:(j + 1) * D].rearrange("p (h d) -> p h d", h=H),
                            bv.rearrange("p (h d) -> p h d", h=H), ALU.add)
                    last.then_inc(s.v_ready.sem, 1)
            if ln or bv is not None:
                pipeline(dve, NG, 1 + v_at, step)
    s.close(q_done=NG, k_done=NG, v_done=NG, q_ready=NG, k_ready=NG, v_ready=NG, xt_ready=NG)
    if source == "x":
        s.close(xn_ready=NG, x_turned=NG)
    if ln:
        s.close(stats=NG, means=NG, spread=NG, vars=NG, rstd=NG, nmean=NG, x_kept=NG)
    if keep:
        s.close(xt_kept=NG)
    if ctx is not None:
        for q in range(2):
            s.ct_loaded[q].base += 16 * (NG // 2)


def local_attention(nc, m, s, d):
    W = LH // 2
    wqkv, wo = m.w(f"f{d}_wqkv"), m.w(f"f{d}_wo")
    half = LD // 2
    fields = m.local

    with nc.Block() as block:
        @block.vector
        def _(dve):
            for i, (co, si, sc) in enumerate((("qcos", "qsin", "qs"), ("kcos", "ksin", "ks"))):
                sc = m.w(f"f{d}_{sc}")
                dve.tensor_tensor(fields.straight[:, i, :], m.c(co), sc, ALU.mult)
                dve.tensor_tensor(fields.swapped[:, i, 0:half], m.c(si)[:, 0:half], sc[:, half:LD], ALU.mult)
                dve.tensor_tensor(fields.swapped[:, i, half:LD], m.c(si)[:, half:LD], sc[:, 0:half],
                                  ALU.mult).then_inc(s.tables.sem, 1)

        @block.gpsimd
        def _(pool):
            pool.memset(fields.HT[:, :, 0:1], 0.0)
            pool.memset(fields.QZ[:, :, :], 0.0)
            pool.memset(fields.V[:, :, :, LD:LD + 1], 1.0)
    s.close(tables=2)

    with nc.Block() as block:
        @block.gpsimd
        def _(pool):
            def finish(i, b, p, rotated, summed, turned, normed):
                pool.wait_ge(*rotated(b + 1))
                pool.wait_ge(*turned(b - 1))
                pool.tensor_tensor(fields.QN[:, p, i], fields.T1[:, i], fields.T2[:, i],
                                   ALU.add).then_inc(s.parts_added.sem, 1)
                pool.wait_ge(*summed(b + 1))
                pool.tensor_tensor(fields.RN[:, i], fields.SS[:, i], m.c("minus_half")[:, 0:LH],
                                   ALU.pow).then_inc(s.powered.sem, 1)
                pool.wait_ge(*s.powered(2 * b + i + 1))
                pool.wait_ge(*s.parts_added(2 * b + i + 1))
                qn = fields.QN[:, p, i].rearrange("p (h d) -> p h d", h=LH)
                pool.tensor_tensor(qn, qn, bcast(fields.RN[:, i], 2, LD), ALU.mult).then_inc(normed.sem, 1)

            def step(k, p, on):
                if on[0]:
                    pool.wait_ge(*s.x_turned(k - 1))
                    pool.tensor_copy(fields.XS[:, p, :], m.X[:, dyn(k, 1), :].rearrange("p a d -> p (a d)")
                                     ).then_inc(s.xs_ready.sem, 1)
                if on[1]:
                    finish(0, k - 1, 1 - p, s.q_rot, s.q_ss, s.q_turned, s.q_norm)
                    finish(1, k - 1, 1 - p, s.k_rot, s.k_ss, s.k_turned, s.k_norm)
            pipeline(pool, B, 2, step)

        @block.tensor
        def _(pe):
            def project_to(bank, at, q, done):
                pe.matmul(m.ps[bank][:, :], fields.HT[:, q, :], wqkv[:, at * LH * LD:(at + 1) * LH * LD],
                          start=True, stop=True).then_inc(done.sem, 1)

            def scores(b, u):
                pe.matmul(m.ps[4 + u][:, :], m.ident_bf[:, :], bcast(m.band_bf[:, :], 1, W),
                          start=True, stop=False, skip_group_check=True)
                for j in range(W):
                    h = u * W + j
                    last = pe.matmul(m.ps[4 + u][:, j * S:(j + 1) * S], fields.QZ[:, h, :],
                                     fields.KT[:, h // 2, :], start=False, stop=j == W - 1, skip_group_check=True)
                last.then_inc(s.scored.sem, 1)

            def turn_probs(b, u):
                pe.wait_ge(*s.exped(2 * b + u + 1))
                for j in range(W):
                    last = pe.transpose(m.ps[6 - 2 * u][:, j * S:(j + 1) * S], fields.PR[:, u, j * S:(j + 1) * S],
                                        m.c("ident"))
                last.then_inc(s.turned.sem, 1)

            def mix(b, p, u):
                pe.wait_ge(*s.pt_ready(2 * b + u + 1))
                for j in range(W):
                    last = pe.matmul(m.ps[7 if u == 0 else 2][:, j * (LD + 1):(j + 1) * (LD + 1)],
                                     fields.PT[:, u, j * S:(j + 1) * S], fields.V[:, p, u * W + j, :],
                                     start=True, stop=True)
                last.then_inc(s.mixed.sem, 1)

            def step(k, p, on):
                b, c, q = k - 2, k - 3, 1 - p
                if on[1]:
                    pe.wait_ge(*s.ht_ready(k))
                    project_to(0, 0, q, s.q_done)
                if on[3]:
                    pe.wait_ge(*s.k_ready(c + 1))
                    turn_probs(c, 0)
                if on[4]:
                    pe.wait_ge(*s.ot_ready(k - 3))
                    for i in range(4):
                        last = pe.matmul(m.ps[3][:, 0:D], fields.OT[:, i * S:(i + 1) * S], wo[:, i * D:(i + 1) * D],
                                         start=i == 0, stop=i == 3)
                    last.then_inc(s.projected.sem, 1)
                if on[1]:
                    pe.wait_ge(*s.k_rot(k - 1))
                    project_to(1, 1, q, s.k_done)
                if on[3]:
                    turn_probs(c, 1)
                if on[0]:
                    pe.wait_ge(*s.xs_ready(k + 1))
                    pe.wait_ge(*s.q_rot(k))
                    pe.transpose(m.ps[0][:, 0:S], fields.XS[:, p, :], m.c("ident")).then_inc(s.x_turned.sem, 1)
                if on[2]:
                    pe.wait_ge(*s.q_norm(b + 1))
                    pe.wait_ge(*s.added(k - 3))
                    for i in range(4):
                        last = pe.transpose(m.ps[3][:, i * S:(i + 1) * S], fields.QN[:, p, 0, i * S:(i + 1) * S],
                                            m.c("ident"))
                    last.then_inc(s.q_turned.sem, 1)
                    pe.wait_ge(*s.k_norm(b + 1))
                    pe.wait_ge(*s.pt_ready(2 * b - 1))
                    for i in range(4):
                        last = pe.transpose(m.ps[6][:, i * S:(i + 1) * S], fields.QN[:, p, 1, i * S:(i + 1) * S],
                                            m.c("ident"))
                    last.then_inc(s.k_turned.sem, 1)
                if on[3]:
                    pe.wait_ge(*s.v_ready(c + 1))
                    pe.wait_ge(*s.divided(2 * c - 1))
                    mix(c, q, 0)
                    if on[2]:
                        pe.wait_ge(*s.v_ready(k - 1))
                    mix(c, q, 1)
                if on[2]:
                    pe.wait_ge(*s.pt_ready(2 * b))
                    pe.wait_ge(*s.q_ready(b + 1))
                    pe.wait_ge(*s.k_ready(b + 1))
                    pe.wait_ge(*s.shifted(2 * b))
                    scores(b, 0)
                    scores(b, 1)
                if on[1]:
                    if on[3]:
                        pe.wait_ge(*s.divided(2 * c + 2))
                    pe.wait_ge(*s.v_ready(k - 1))
                    project_to(2, 2, q, s.v_done)
                if on[3]:
                    if on[2]:
                        pe.wait_ge(*s.q_ready(k - 1))
                    pe.wait_ge(*s.divided(2 * c + 2))
                    for i in range(4):
                        last = pe.transpose(m.ps[3][:, i * S:(i + 1) * S], fields.ON[:, i * S:(i + 1) * S],
                                            m.c("ident"))
                    last.then_inc(s.on_turned.sem, 1)
            pipeline(pe, B, 5, step)

        @block.scalar
        def _(act):
            def squares(i, b, done, summed, squared):
                act.wait_ge(*done(b + 1))
                act.wait_ge(*summed(b))
                act.activation(fields.SQ[:, i], m.ps[i][:, :], ACT.Square).then_inc(squared.sem, 1)

            def exp(b, u):
                act.wait_ge(*s.shifted(2 * b + u + 1))
                act.activation(fields.PR[:, u, :], fields.PR[:, u, :], ACT.Exp, scale=8.0).then_inc(s.exped.sem, 1)

            def evacuate(b, u):
                act.wait_ge(*s.turned(2 * b + u + 1))
                act.wait_ge(*s.mixed(2 * b + u - 1))
                act.activation(fields.PT[:, u, :], m.ps[6 - 2 * u][:, :], ACT.Copy).then_inc(s.pt_ready.sem, 1)

            def step(k, p, on):
                b, c = k - 2, k - 3
                if on[1]:
                    squares(0, k - 1, s.q_done, s.q_ss, s.q_sq)
                if on[3]:
                    evacuate(c, 0)
                if on[1]:
                    squares(1, k - 1, s.k_done, s.k_ss, s.k_sq)
                if on[3]:
                    evacuate(c, 1)
                if on[0]:
                    act.wait_ge(*s.x_turned(k + 1))
                    act.wait_ge(*s.v_done(k - 1))
                    act.activation(fields.HT[0:64, p, :], m.ps[0][0:64, 0:S], ACT.Copy)
                    act.activation(fields.HT[64:128, p, 1:S], m.ps[0][64:128, 0:S - 1],
                                   ACT.Copy).then_inc(s.ht_ready.sem, 1)
                if on[2]:
                    act.wait_ge(*s.q_turned(b + 1))
                    act.wait_ge(*s.scored(2 * b))
                    qz = fields.QZ[:, :, :].rearrange("p (c w) s -> p c w s", w=2)
                    qt = m.ps[3][:, :].rearrange("p (c s) -> p c s", c=4)
                    act.activation(qz[0:64, :, 0, :], qt[0:64], ACT.Copy)
                    act.activation(qz[64:128, :, 1, :], qt[64:128], ACT.Copy).then_inc(s.q_ready.sem, 1)
                    act.wait_ge(*s.k_turned(b + 1))
                    act.activation(fields.KT[:, :, :].rearrange("p c s -> p (c s)"), m.ps[6][:, :],
                                   ACT.Copy).then_inc(s.k_ready.sem, 1)
                    exp(b, 0)
                if on[1]:
                    act.wait_ge(*s.v_done(k))
                    act.wait_ge(*s.mixed(2 * (k - 2)))
                    act.activation(fields.V[:, 1 - p, :, 0:LD],
                                   m.ps[2][:, :].rearrange("p (h d) -> p h d", h=LH),
                                   ACT.Copy).then_inc(s.v_ready.sem, 1)
                if on[3]:
                    act.wait_ge(*s.on_turned(c + 1))
                    act.wait_ge(*s.projected(c))
                    act.activation(fields.OT[:, :], m.ps[3][:, :], ACT.Copy).then_inc(s.ot_ready.sem, 1)
                if on[2]:
                    exp(b, 1)
            pipeline(act, B, 4, step)

        @block.vector
        def _(dve):
            def rotate(i, b, squared, normed, rotated):
                dve.wait_ge(*squared(b + 1))
                dve.wait_ge(*normed(b))
                src = m.ps[i][:, :].rearrange("p (h d) -> p h d", h=LH)
                dve.tensor_tensor(fields.T1[:, i].rearrange("p (h d) -> p h d", h=LH), src,
                                  bcast(fields.straight[:, i, :], 1, LH), ALU.mult)
                t2 = fields.T2[:, i].rearrange("p (h d) -> p h d", h=LH)
                dve.tensor_tensor(t2[:, :, 0:half], src[:, :, half:LD],
                                  bcast(fields.swapped[:, i, 0:half], 1, LH), ALU.mult)
                dve.tensor_tensor(t2[:, :, half:LD], src[:, :, 0:half],
                                  bcast(fields.swapped[:, i, half:LD], 1, LH), ALU.mult).then_inc(rotated.sem, 1)

            def sums(i, b, squared, normed, summed):
                dve.wait_ge(*squared(b + 1))
                dve.wait_ge(*normed(b))
                dve.tensor_reduce(fields.SS[:, i], fields.SQ[:, i].rearrange("p (h d) -> p h d", h=LH), AXX,
                                  ALU.add).then_inc(s.floored.sem, 1)
                dve.wait_ge(*s.floored(2 * b + i + 1))
                dve.tensor_scalar(fields.SS[:, i], fields.SS[:, i], 1e-24, None, ALU.max).then_inc(summed.sem, 1)

            def soft(b, u):
                dve.wait_ge(*s.scored(2 * b + u + 1))
                sc = m.ps[4 + u][:, :].rearrange("p (j s) -> p j s", j=W)
                dve.tensor_reduce(m.mx[:, u, :], sc, AXX, ALU.max).then_inc(s.maxed.sem, 1)
                dve.wait_ge(*s.maxed(2 * b + u + 1))
                dve.wait_ge(*s.turned(2 * b + u - 1))
                dve.tensor_tensor(fields.PR[:, u, :].rearrange("p (j s) -> p j s", j=W), sc,
                                  bcast(m.mx[:, u, :], 2, S), ALU.subtract).then_inc(s.shifted.sem, 1)

            def divide(b, u):
                dve.wait_ge(*s.mixed(2 * b + u + 1))
                o = m.ps[7 if u == 0 else 2][:, 0:W * (LD + 1)].rearrange("p (j d) -> p j d", j=W)
                dve.reciprocal(m.rs[:, u * W:(u + 1) * W], o[:, :, LD]).then_inc(s.inverted.sem, 1)
                dve.wait_ge(*s.inverted(2 * b + u + 1))
                dve.wait_ge(*s.on_turned(b))
                dve.tensor_tensor(fields.ON[:, u * W * LD:(u + 1) * W * LD].rearrange("p (j d) -> p j d", j=W),
                                  o[:, :, 0:LD], bcast(m.rs[:, u * W:(u + 1) * W], 2, LD), ALU.mult).then_inc(s.divided.sem, 1)

            def step(k, p, on):
                if on[1]:
                    rotate(0, k - 1, s.q_sq, s.q_norm, s.q_rot)
                if on[4]:
                    dve.wait_ge(*s.projected(k - 3))
                    x = m.X[:, dyn(k - 4, 1), :].rearrange("p a d -> p (a d)")
                    dve.tensor_tensor(x, m.ps[3][:, 0:D], x, ALU.add).then_inc(s.added.sem, 1)
                if on[1]:
                    sums(0, k - 1, s.q_sq, s.q_norm, s.q_ss)
                if on[1]:
                    rotate(1, k - 1, s.k_sq, s.k_norm, s.k_rot)
                    sums(1, k - 1, s.k_sq, s.k_norm, s.k_ss)
                if on[3]:
                    divide(k - 3, 0)
                    divide(k - 3, 1)
                if on[2]:
                    soft(k - 2, 0)
                    soft(k - 2, 1)
            pipeline(dve, B, 5, step)
    s.close(xs_ready=B, x_turned=B, ht_ready=B, q_done=B, k_done=B, v_done=B, q_sq=B, k_sq=B, q_rot=B, k_rot=B,
            q_ss=B, k_ss=B, q_norm=B, k_norm=B, q_turned=B, k_turned=B, q_ready=B, k_ready=B, v_ready=B,
            scored=2 * B, maxed=2 * B, shifted=2 * B, exped=2 * B, turned=2 * B, pt_ready=2 * B, mixed=2 * B,
            inverted=2 * B, divided=2 * B, on_turned=B, ot_ready=B, projected=B, added=B, floored=2 * B,
            powered=2 * B, parts_added=2 * B)


def gated_mlp(nc, m, s, d):
    f = m.mlp
    w1, w2, b1, b2 = (m.w(f"f{d}_{n}") for n in ("w1", "w2", "b1", "b2"))
    lg, lb = m.w(f"f{d}_lg"), m.w(f"f{d}_lb")
    NC = len(HCH)

    with nc.Block() as block:
        @block.gpsimd
        def _(pool):
            def step(g, p, on):
                pool.wait_ge(*s.xn_ready(g - 1))
                pool.tensor_copy(f.XS[:, p], m.X[:, dyn(g * G, G), :]).then_inc(s.xs_ready.sem, 1)
                rstd_on(pool, m, s, g, p, G)
            pipeline(pool, NG, 1, step)

        @block.tensor
        def _(pe):
            def step(k, p, on):
                if on[2]:
                    pe.wait_ge(*s.gated((k - 1) * NC))
                    pe.wait_ge(*s.added(k - 2))
                    for j in range(G):
                        for c, (at, n) in enumerate(HCH):
                            last = pe.matmul(m.ps[7][:, j * D:(j + 1) * D], f.HH[0:n, p, c, j * S:(j + 1) * S],
                                             w2[0:n, c * D:(c + 1) * D], start=c == 0, stop=c == NC - 1,
                                             skip_group_check=True)
                    last.then_inc(s.projected.sem, 1)
                if on[0]:
                    pe.wait_ge(*s.xs_ready(k + 1))
                    pe.wait_ge(*s.xt_ready(k))
                    pe.matmul(m.ps[0][:, 0:G * 64], m.c("shift"), f.XS[:, p, :, 64:D], start=True,
                              stop=True).then_inc(s.x_shifted.sem, 1)
                if on[1]:
                    g, q = k - 1, 1 - p
                    pe.wait_ge(*s.xt_ready(g + 1))
                    for c, (at, n) in enumerate(HCH):
                        u = g * NC + c
                        pe.wait_ge(*s.gated(u - NC + 1))
                        pe.matmul(m.ps[1 + c][0:n, :], w1[:, HID + at:HID + at + n], f.HT[:, q, :], start=True,
                                  stop=True).then_inc(s.g_done.sem, 1)
                        pe.matmul(m.ps[4 + c][0:n, :], w1[:, at:at + n], f.HT[:, q, :], start=True,
                                  stop=True).then_inc(s.a_done.sem, 1)
                if on[0]:
                    pe.wait_ge(*s.xn_ready(k + 1))
                    for j in range(G):
                        last = pe.transpose(m.ps[0][:, j * S:(j + 1) * S], f.XN[:, p, j, :], m.c("ident"))
                    last.then_inc(s.x_turned.sem, 1)
            pipeline(pe, NG, 3, step)

        @block.scalar
        def _(act):
            def step(k, p, on):
                if on[1]:
                    for c, (at, n) in enumerate(HCH):
                        u = (k - 1) * NC + c
                        act.wait_ge(*s.g_done(u + 1))
                        act.wait_ge(*s.gated(u - NC + 1))
                        act.activation(f.GT[0:n, c, :], m.ps[1 + c][0:n, :], ACT.Gelu,
                                       bias=b1[0:n, NC + c:NC + c + 1]).then_inc(s.gelued.sem, 1)
                if on[0]:
                    act.wait_ge(*s.x_turned(k + 1))
                    act.wait_ge(*s.a_done((k - 1) * NC))
                    act.activation(f.HT[:, p, :], m.ps[0][:, :], ACT.Identity, bias=lb,
                                   scale=lg).then_inc(s.xt_ready.sem, 1)
            pipeline(act, NG, 2, step)

        @block.vector
        def _(dve):
            def step(k, p, on):
                if on[0]:
                    dve.wait_ge(*s.x_shifted(k + 1))
                    dve.tensor_copy(f.XS[:, p, :, 64:D], m.ps[0][:, 0:G * 64].rearrange("p (j d) -> p j d", j=G)
                                    ).then_inc(s.shift_in.sem, 1)
                    dve.wait_ge(*s.shift_in(k + 1))
                    dve.wait_ge(*s.x_turned(k - 1))
                    ln_stats(dve, m, s, k, p, G, lambda j: f.XS[:, p, j, :], 1e-5)
                    x = m.X[:, dyn(k * G, G), :]
                    dve.tensor_tensor(x, x, bcast(b2, 1, G), ALU.add).then_inc(s.biased.sem, 1)
                for c, (at, n) in enumerate(HCH):
                    if on[0] and c == 1:
                        ln_apply(dve, m, s, k, p, G, lambda j: f.XS[:, p, j, :],
                                 lambda j: f.XN[:, p, j, :]).then_inc(s.xn_ready.sem, 1)
                    if on[2] and c == 1:
                        g = k - 2
                        dve.wait_ge(*s.projected(g + 1))
                        dve.wait_ge(*s.biased(g + 1))
                        x = m.X[:, dyn(g * G, G), :]
                        dve.tensor_tensor(x, m.ps[7][:, :].rearrange("p (j d) -> p j d", j=G), x,
                                          ALU.add).then_inc(s.added.sem, 1)
                    if on[1]:
                        q = 1 - p
                        u = (k - 1) * NC + c
                        dve.wait_ge(*s.gelued(u + 1))
                        dve.wait_ge(*s.a_done(u + 1))
                        dve.wait_ge(*s.projected(k - 2))
                        dve.scalar_tensor_tensor(f.HH[0:n, q, c, :], m.ps[4 + c][0:n, :], b1[0:n, c:c + 1],
                                                 f.GT[0:n, c, :], ALU.add, ALU.mult).then_inc(s.gated.sem, 1)
            pipeline(dve, NG, 3, step)
    s.close(xs_ready=NG, biased=NG, stats=NG, means=NG, spread=NG, vars=NG, rstd=NG, nmean=NG, x_shifted=NG,
            shift_in=NG, xn_ready=NG, x_turned=NG, xt_ready=NG, g_done=NG * NC, a_done=NG * NC, gelued=NG * NC,
            gated=NG * NC, projected=NG, added=NG)


def normalize(nc, m, s, *, add=None, keep_to=None, out=None):
    with nc.Block() as block:
        @block.gpsimd
        def _(pool):
            def step(k, p, on):
                if on[0] and add is not None:
                    pool.wait_ge(*s.xn_ready(k - 1))
                    pool.tensor_tensor(m.XN2[:, p], m.X[:, dyn(k * G, G), :], add[:, dyn(k * G, G), :],
                                       ALU.add).then_inc(s.summed.sem, 1)
                if on[1]:
                    rstd_on(pool, m, s, k - 1, 1 - p, G)
            pipeline(pool, NG, 2, step)

        @block.vector
        def _(dve):
            def tiles(g, p):
                x = lambda j: m.X[:, dyn(g * G + j, 1), :].rearrange("p a d -> p (a d)")
                return x, x if add is None else lambda j: m.XN2[:, p, j, :]

            def step(k, p, on):
                if on[0]:
                    if add is not None:
                        dve.wait_ge(*s.summed(k + 1))
                    ln_stats(dve, m, s, k, p, G, tiles(k, p)[1], 1e-5)
                if on[1]:
                    x, src = tiles(k - 1, 1 - p)
                    ln_apply(dve, m, s, k - 1, 1 - p, G, src, x).then_inc(s.xn_ready.sem, 1)
            pipeline(dve, NG, 2, step)

        if keep_to is not None:
            @block.scalar
            def _(act):
                def step(g, p, on):
                    act.wait_ge(*s.xn_ready(g + 1))
                    act.activation(keep_to[:, dyn(g * G, G), :], m.X[:, dyn(g * G, G), :], ACT.Copy)
                pipeline(act, NG, 1, step)

        if out is not None:
            @block.sync
            def _(sp):
                def step(g, p, on):
                    sp.wait_ge(*s.xn_ready(g + 1))
                    sp.dma_start(out[dyn(g * G, G), :, :].rearrange("b s d -> s b d"),
                                 m.X[:, dyn(g * G, G), :]).then_inc(s.stored.sem, 16)
                pipeline(sp, NG, 1, step)
                sp.wait_ge(*s.stored(16 * NG))
    s.close(stats=NG, means=NG, spread=NG, vars=NG, rstd=NG, nmean=NG, xn_ready=NG)
    if add is not None:
        s.close(summed=NG)


def project_latent(nc, m, s):
    f = Memory()
    (f.XN, f.SUM, f.XT, f.CT, f.PART, f.STR
     ) = carve(m.ring, [(2, G, D), (G, D), (2, G * S), (2, G * S), (2, G * S), (2, 2, G * S)])
    weights = {0: m.w("m_q"), 1: m.w("m_k")}

    with nc.Block() as block:
        @block.gpsimd
        def _(pool):
            def add_up(g, which):
                for t in range(2):
                    pool.wait_ge(*s.unit_ready(6 * g + 3 * which + t + 2))
                    tile = 2 * which + t
                    pool.tensor_tensor(m.QKT[:, dyn(g * G, G), tile * S:(tile + 1) * S],
                                       f.STR[:, which, t].rearrange("p (b s) -> p b s", b=G),
                                       f.PART[:, which].rearrange("p (b s) -> p b s", b=G),
                                       ALU.add).then_inc(s.rotated.sem, 1)

            def step(k, p, on):
                if on[0]:
                    pool.wait_ge(*s.xn_ready(k))
                    pool.tensor_tensor(f.SUM[:, :, :], m.X[:, dyn(k * G, G), :], m.XR[:, dyn(k * G, G), :],
                                       ALU.add).then_inc(s.summed.sem, 1)
                    rstd_on(pool, m, s, k, p, G)
                if on[1]:
                    add_up(k - 1, 0)
                    add_up(k - 1, 1)
            pipeline(pool, NG, 2, step)

        @block.tensor
        def _(pe):
            def step(k, p, on):
                g, q = k - 1, 1 - p
                if on[1]:
                    pe.wait_ge(*s.xt_ready(g + 1))
                    pe.wait_ge(*s.c_ready(g))
                    pe.matmul(m.ps[2][:, :], m.w("m_down"), f.XT[:, q, :], start=True,
                              stop=True).then_inc(s.c_done.sem, 1)
                    for which, src in ((0, f.XT), (1, f.CT)):
                        if which == 1:
                            pe.wait_ge(*s.c_ready(g + 1))
                        for i in range(3):
                            u = 6 * g + 3 * which + i
                            pe.wait_ge(*s.unit_ready(u - 2))
                            pe.matmul(m.ps[5 + i][:, :], weights[which][:, i * D:(i + 1) * D], src[:, q, :],
                                      start=True, stop=True).then_inc(s.unit_done.sem, 1)
                    pe.wait_ge(*s.v_ready(g - 1))
                    for j in range(G):
                        last = pe.matmul(m.ps[3 + q][:, j * D:(j + 1) * D], f.CT[:, q, j * S:(j + 1) * S],
                                         m.w("m_v"), start=True, stop=True)
                    last.then_inc(s.v_done.sem, 1)
                if on[0]:
                    pe.wait_ge(*s.xn_ready(k + 1))
                    pe.wait_ge(*s.xt_ready(k - 1))
                    for j in range(G):
                        last = pe.transpose(m.ps[p][:, j * S:(j + 1) * S], f.XN[:, p, j, :], m.c("ident"))
                    last.then_inc(s.x_turned.sem, 1)
            pipeline(pe, NG, 2, step)

        @block.scalar
        def _(act):
            def step(k, p, on):
                g, q = k - 1, 1 - p
                if on[1]:
                    act.wait_ge(*s.c_done(g + 1))
                    act.wait_ge(*s.v_done(g - 1))
                    act.activation(f.CT[:, q, :], m.ps[2][:, :], ACT.Copy).then_inc(s.c_ready.sem, 1)
                    act.wait_ge(*s.v_done(g + 1))
                    act.activation(m.V[:, dyn(g * G, G), :, 0:HD],
                                   m.ps[3 + q][:, :].rearrange("p (b h d) -> p b h d", b=G, h=H),
                                   ACT.Copy).then_inc(s.v_ready.sem, 1)
                if on[0]:
                    act.wait_ge(*s.x_turned(k + 1))
                    act.wait_ge(*s.v_done(k - 1))
                    act.activation(f.XT[:, p, :], m.ps[p][:, :], ACT.Copy).then_inc(s.xt_ready.sem, 1)
                    act.wait_ge(*s.xn_ready(k + 1))
                    act.activation(m.X[:, dyn(k * G, G), :], f.XN[:, p], ACT.Copy).then_inc(s.x_kept.sem, 1)
            pipeline(act, NG, 2, step)

        @block.vector
        def _(dve):
            def rotate(g, which):
                for i in range(3):
                    dve.wait_ge(*s.unit_done(6 * g + 3 * which + i + 1))
                    dve.wait_ge(*s.rotated(4 * g - 2 + 2 * which))
                    dst = f.PART[:, which] if i == 0 else f.STR[:, which, i - 1]
                    dve.tensor_tensor(dst.rearrange("p (b s) -> p b s", b=G),
                                      m.ps[5 + i][:, :].rearrange("p (b s) -> p b s", b=G),
                                      bcast(m.c("ropesin" if i == 0 else "ropecos"), 1, G),
                                      ALU.mult).then_inc(s.unit_ready.sem, 1)

            def step(k, p, on):
                if on[0]:
                    dve.wait_ge(*s.summed(k + 1))
                    ln_stats(dve, m, s, k, p, G, lambda j: f.SUM[:, j, :], 1e-5)
                if on[1]:
                    rotate(k - 1, 0)
                if on[0]:
                    dve.wait_ge(*s.x_turned(k - 1))
                    dve.wait_ge(*s.x_kept(k - 1))
                    ln_apply(dve, m, s, k, p, G, lambda j: f.SUM[:, j, :],
                             lambda j: f.XN[:, p, j, :]).then_inc(s.xn_ready.sem, 1)
                if on[1]:
                    rotate(k - 1, 1)
            pipeline(dve, NG, 2, step)
    s.close(summed=NG, rotated=4 * NG, xn_ready=NG, x_kept=NG, c_done=NG, c_ready=NG, unit_done=6 * NG,
            unit_ready=6 * NG, v_done=NG, v_ready=NG, x_turned=NG, xt_ready=NG, stats=NG, means=NG, spread=NG,
            vars=NG, rstd=NG, nmean=NG)


def project_linear(nc, m, s, ctx):
    f = Memory()
    (f.XN, f.XT, f.CT, f.U
     ) = carve(m.ring, [(2, G, D), (2, G * S), (2, G * S), (2, 3 * G, D)])
    places = [m.QT, m.KT, m.XTA]

    with nc.Block() as block:
        @block.sync
        def _(sp):
            def step(g, p, on):
                sp.wait_ge(*s.v_done(g - 1))
                sp.dma_start(f.CT[:, p, :], ctx[:, dyn(g * G * S, G * S)]).then_inc(s.ct_loaded[p].sem, 16)
            pipeline(sp, NG, 1, step)

        @block.gpsimd
        def _(pool):
            def step(k, p, on):
                g, q = k - 1, 1 - p
                if on[1]:
                    rstd_on(pool, m.second, s.second, g, q, 3 * G)
                if on[0]:
                    rstd_on(pool, m, s, k, p, G)
                if on[1]:
                    for i in range(3):
                        u = f.U[:, q, i * G:(i + 1) * G]
                        pool.wait_ge(*s.norm2(g + 1))
                        pool.tensor_tensor(u, u, bcast(m.w("y_gamma"), 1, G), ALU.mult).then_inc(s.scaled.sem, 1)
            pipeline(pool, NG, 2, step)

        @block.tensor
        def _(pe):
            def tokens(bank, src, q, w, done):
                for j in range(G):
                    last = pe.matmul(m.ps[bank][:, j * D:(j + 1) * D], src[:, q, j * S:(j + 1) * S], w,
                                     start=True, stop=True)
                last.then_inc(done.sem, 1)

            def step(k, p, on):
                if on[1]:
                    g, q = k - 1, 1 - p
                    pe.wait_ge(*s.norm2(g - 1))
                    pe.wait_ge(*s.xt_ready(g + 1))
                    tokens(2 + q, f.XT, q, m.w("y_wq"), s.q_done)
                if on[0]:
                    pe.wait_ge(*s.norm2(k - 1))
                    pe.wait_ge(s.ct_loaded[p].sem, k * 8 - p * 8 + 16 + s.ct_loaded[p].base)
                    tokens(4 + p, f.CT, p, m.w("y_wkv")[:, 0:D], s.k_done)
                    tokens(6 + p, f.CT, p, m.w("y_wkv")[:, D:2 * D], s.v_done)
                    pe.wait_ge(*s.xn_ready(k + 1))
                    pe.wait_ge(*s.xt_ready(k - 1))
                    for j in range(G):
                        last = pe.transpose(m.ps[p][:, j * S:(j + 1) * S], f.XN[:, p, j, :], m.c("ident"))
                    last.then_inc(s.x_turned.sem, 1)
            pipeline(pe, NG, 2, step)

        @block.scalar
        def _(act):
            def step(k, p, on):
                act.wait_ge(*s.x_turned(k + 1))
                act.wait_ge(*s.q_done(k - 1))
                act.activation(f.XT[:, p, :], m.ps[p][:, :], ACT.Copy).then_inc(s.xt_ready.sem, 1)
                act.activation(m.X[:, dyn(k * G, G), :], f.XN[:, p], ACT.Copy).then_inc(s.x_kept.sem, 1)
            pipeline(act, NG, 1, step)

        @block.vector
        def _(dve):
            def step(k, p, on):
                x = lambda j: m.X[:, dyn(k * G + j, 1), :].rearrange("p a d -> p (a d)")
                g, q = k - 1, 1 - p
                qkv = lambda j: m.ps[2 + 2 * (j // G) + q][:, (j % G) * D:(j % G + 1) * D]
                if on[1]:
                    dve.wait_ge(*s.q_done(g + 1))
                    ln_stats(dve, m.second, s.second, g, q, 3 * G, qkv, 1e-6)
                if on[0]:
                    ln_stats(dve, m, s, k, p, G, x, 1e-5)
                if on[2]:
                    for i in range(3):
                        dve.wait_ge(*s.scaled(3 * (k - 2) + i + 1))
                        last = dve.tensor_tensor(
                            places[i][:, dyn((k - 2) * G * S, G * S)].rearrange("p (b d) -> p b d", b=G),
                            f.U[:, p, i * G:(i + 1) * G], bcast(m.w("y_beta"), 1, G), ALU.add)
                    last.then_inc(s.based.sem, 1)
                if on[0]:
                    dve.wait_ge(*s.x_turned(k - 1))
                    dve.wait_ge(*s.x_kept(k - 1))
                    ln_apply(dve, m, s, k, p, G, x, lambda j: f.XN[:, p, j, :]).then_inc(s.xn_ready.sem, 1)
                if on[1]:
                    dve.wait_ge(*s.based(g - 1))
                    ln_apply(dve, m.second, s.second, g, q, 3 * G, qkv,
                             lambda j: f.U[:, q, j, :]).then_inc(s.norm2.sem, 1)
            pipeline(dve, NG, 3, step)
    s.close(v_done=NG, k_done=NG, q_done=NG, norm2=NG, scaled=3 * NG, based=NG, xn_ready=NG, x_turned=NG,
            xt_ready=NG, x_kept=NG, **{n: NG for n in ("stats", "means", "spread", "vars", "rstd", "nmean", "stats2",
                                                       "means2", "spread2", "vars2", "rstd2", "nmean2")})
    for q in range(2):
        s.ct_loaded[q].base += 16 * (NG // 2)


def linear_attention(nc, m, s):
    N = D + H
    f = Memory()
    (f.Q, f.K, f.V1, f.QT, f.KV, f.ZM, f.AF, f.O, f.ON, f.DEN, f.RZ, f.EM
     ) = carve(m.ring, [(G, D), (G, D), (G, N), (2, G * S), (2, G, N), (G, H, HD), (G * S,), (G, D), (G, D),
        (G, H), (G, H), (G,)])
    spread = [a.rearrange("p (e b h n) -> p e b h n", e=HD, b=G, h=H)
              for a in (m.arena[:, 0:HD * G * S], m.XR.rearrange("p b d -> p (b d)"))]
    n2, eps = G // 2, 1e-6
    em = lambda g: bcast(m.w("em")[:, dyn(g * G, G)], 2, D)

    with nc.Block() as block:
        @block.vector
        def _(dve):
            dve.memset(f.V1[:, :, D:N], 1.0)

    with nc.Block() as block:
        @block.gpsimd
        def _(pool):
            def step(k, p, on):
                if on[0]:
                    pool.wait_ge(*s.kv_done(k))
                    pool.wait_ge(*s.v_staged(k))
                    pool.tensor_copy(f.EM[:, :], m.w("em")[:, dyn(k * G, G)]).then_inc(s.em_ready.sem, 1)
                    pool.tensor_tensor(f.V1[:, :, 0:D], m.XTA[:, dyn(k * G * S, G * S)].rearrange(
                        "p (b d) -> p b d", b=G), em(k), ALU.mult)
                    pool.wait_ge(*s.staged(k + 1))
                    pool.wait_ge(*s.em_ready(k + 1))
                    pool.tensor_tensor(f.K[:, :, :], f.K[:, :, :], bcast(f.EM[:, :], 2, D),
                                       ALU.mult).then_inc(s.v_staged.sem, 1)
                if on[3]:
                    g = k - 3
                    rstd_on(pool, m, s, g, 1 - p, G)
                    pool.wait_ge(*s.fin_norm(g + 1))
                    pool.tensor_tensor(f.ON[:, :, :], f.ON[:, :, :], bcast(m.w("y_gamma"), 1, G),
                                       ALU.mult).then_inc(s.fin_scaled.sem, 1)
            pipeline(pool, NG, 4, step)

        @block.tensor
        def _(pe):
            def step(k, p, on):
                q = 1 - p
                if on[1]:
                    g = k - 1
                    pe.wait_ge(*s.q_ready(g + 1))
                    pe.wait_ge(*s.kv_ready(2 * g + 2))
                    pe.wait_ge(*s.at_ready(g))
                    for j in range(G):
                        last = pe.matmul(m.ps[3 + j // n2][:, (j % n2) * N:(j % n2 + 1) * N],
                                         f.QT[:, q, j * S:(j + 1) * S], f.KV[:, q, j, :], start=True, stop=True)
                    last.then_inc(s.at_done.sem, 1)
                if on[3]:
                    g = k - 3
                    pe.wait_ge(*s.att_ready(g + 1))
                    pe.wait_ge(*s.ebias(g))
                    for j in range(G):
                        last = pe.matmul(m.ps[6][:, j * D:(j + 1) * D], f.AF[:, j * S:(j + 1) * S], m.w("y_dw"),
                                         start=True, stop=True)
                    last.then_inc(s.projected.sem, 1)
                if on[2]:
                    g = k - 2
                    pe.wait_ge(*s.at_ready(g + 1))
                    pe.wait_ge(*s.att_ready(g))
                    for e in range(HD):
                        at = e // 2 * 32
                        last = pe.matmul(m.ps[5][at:at + 32, :], m.c("place")[:, (e % 2) * 32:(e % 2) * 32 + 32],
                                         spread[p][:, e].rearrange("p b h n -> p (b h n)"), start=e % 2 == 0,
                                         stop=e % 2 == 1, skip_group_check=True)
                    last.then_inc(s.at_turned.sem, 1)
                if on[0]:
                    pe.wait_ge(*s.v_staged(k + 1))
                    pe.wait_ge(*s.q_ready(k))
                    for j in range(G):
                        last = pe.transpose(m.ps[0][:, j * S:(j + 1) * S], f.Q[:, j, :], m.c("ident"))
                    last.then_inc(s.q_done.sem, 1)
                    pe.wait_ge(*s.kv_ready(2 * k))
                    for j in range(G):
                        last = pe.matmul(m.ps[1 + j // n2][:, (j % n2) * N:(j % n2 + 1) * N], f.K[:, j, :],
                                         f.V1[:, j, :], start=True, stop=True)
                    last.then_inc(s.kv_done.sem, 1)
            pipeline(pe, NG, 4, step)

        @block.scalar
        def _(act):
            def step(k, p, on):
                if on[2]:
                    act.wait_ge(*s.at_turned(k - 1))
                    act.wait_ge(*s.projected(k - 2))
                    act.activation(f.AF[:, :], m.ps[5][:, :], ACT.Copy).then_inc(s.att_ready.sem, 1)
                if on[0]:
                    act.wait_ge(*s.q_done(k + 1))
                    act.wait_ge(*s.at_done(k - 1))
                    act.activation(f.QT[:, p, :], m.ps[0][:, :], ACT.Copy).then_inc(s.q_ready.sem, 1)
            pipeline(act, NG, 3, step)

        @block.vector
        def _(dve):
            def group(area, g):
                return area[:, dyn(g * G * S, G * S)].rearrange("p (b d) -> p b d", b=G)

            def step(k, p, on):
                q, c = 1 - p, k - 3
                if on[0]:
                    dve.wait_ge(*s.kv_done(k))
                    dve.tensor_scalar(f.Q[:, :, :], group(m.QT, k), 0.0, eps, ALU.max, ALU.add)
                    dve.tensor_scalar(f.K[:, :, :], group(m.KT, k), 0.0, eps, ALU.max, ALU.add
                                      ).then_inc(s.staged.sem, 1)
                if on[1]:
                    g = k - 1
                    dve.wait_ge(*s.at_done(g + 1))
                    at = [m.ps[3 + i][:, 0:n2 * N].rearrange("p (b n) -> p b n", b=n2) for i in range(2)]
                    for i in range(2):
                        last = dve.tensor_scalar(f.DEN[:, i * n2:(i + 1) * n2, :], at[i][:, :, D:N], eps, None, ALU.add)
                    last.then_inc(s.z_added.sem, 1)
                    dve.wait_ge(*s.z_added(g + 1))
                    dve.reciprocal(f.RZ[:, :, :], f.DEN[:, :, :]).then_inc(s.z_ready.sem, 1)
                    dve.wait_ge(*s.z_ready(g + 1))
                    dve.tensor_tensor(f.ZM[:, :, :, :].rearrange("p b h n -> p (b h) n"),
                                      bcast(f.RZ[:, :, :].rearrange("p b h -> p (b h)"), 2, HD),
                                      bcast(m.c("block"), 1, G * H), ALU.mult).then_inc(s.zm_ready.sem, 1)
                    dve.wait_ge(*s.zm_ready(g + 1))
                    dve.wait_ge(*s.at_turned(g - 1))
                    for j in range(G):
                        last = dve.tensor_tensor(
                            spread[q][:, :, j],
                            bcast(at[j // n2][:, j % n2, 0:D].rearrange("p (h e) -> p e h", h=H), 3, HD),
                            bcast(f.ZM[:, j], 1, HD), ALU.mult)
                    last.then_inc(s.at_ready.sem, 1)
                if on[3]:
                    dve.wait_ge(*s.projected(c + 1))
                    dve.tensor_tensor(f.O[:, :, :], m.ps[6][:, :].rearrange("p (b d) -> p b d", b=G),
                                      bcast(m.w("y_db"), 1, G), ALU.add).then_inc(s.ebias.sem, 1)
                    dve.wait_ge(*s.ebias(c + 1))
                    ln_stats(dve, m, s, c, q, G, lambda j: f.O[:, j, :], eps)
                if on[0]:
                    dve.wait_ge(*s.kv_done(k + 1))
                    dve.wait_ge(*s.at_done(k - 1))
                    for i in range(2):
                        kv = m.ps[1 + i][:, 0:n2 * N].rearrange("p (b n) -> p b n", b=n2)
                        dve.tensor_tensor(f.KV[:, p, i * n2:(i + 1) * n2, :], kv, bcast(m.c("blocks_sel"), 1, n2),
                                          ALU.mult).then_inc(s.kv_ready.sem, 1)
                if on[3]:
                    ln_apply(dve, m, s, c, q, G, lambda j: f.O[:, j, :],
                             lambda j: f.ON[:, j, :]).then_inc(s.fin_norm.sem, 1)
                    dve.wait_ge(*s.fin_scaled(c + 1))
                    dve.tensor_tensor(f.ON[:, :, :], f.ON[:, :, :], bcast(m.w("y_beta"), 1, G),
                                      ALU.add).then_inc(s.fin_based.sem, 1)
                    dve.wait_ge(*s.fin_based(c + 1))
                    x = m.X[:, dyn(c * G, G), :]
                    dve.tensor_tensor(x, f.ON[:, :, :], x, ALU.add).then_inc(s.added.sem, 1)
                    dve.wait_ge(*s.added(c + 1))
            pipeline(dve, NG, 4, step)
    s.close(**{n: NG for n in ("staged", "v_staged", "em_ready", "zm_ready", "q_done", "q_ready", "kv_done", "at_done", "at_ready", "projected",
                               "at_turned", "att_ready", "z_added", "z_ready", "ebias", "fin_norm", "fin_scaled",
                               "fin_based", "added", "stats", "means", "spread", "vars", "rstd", "nmean")},
            kv_ready=2 * NG)


def gates(nc, m, s):
    f = Memory()
    (f.SUM, f.MEAN, f.L, f.MX, f.SH, f.EX, f.ES, f.ER, f.GTR, f.EQ, f.EQL, f.BEF, f.CNT, f.GM,
     f.ROWS
     ) = carve(m.ring, [(B,), (B,), (E,), (1,), (E,), (E,), (1,), (1,), (E, E), (E, E), (E, E), (E, E), (E,), (E,),
                        (B, E)])
    b = slice(0, B)
    with nc.Block() as block:
        @block.gpsimd
        def _(pool):
            pool.memset(m.XR[:, :, :], 0.0)

        @block.tensor
        def _(pe):
            pe.wait_ge(*s.g_steps(2))
            pe.matmul(m.ps[0][b, 0:E], f.MEAN[:, :], m.w("gate_w"), start=True, stop=True).then_inc(s.g_done.sem, 1)
            pe.wait_ge(*s.g_rows(1))
            pe.matmul(m.ps[1][:, 0:B * E], m.c("ones")[b, :], f.ROWS[b].rearrange("p b e -> p (b e)"), start=True,
                      stop=True).then_inc(s.g_done.sem, 1)

        @block.scalar
        def _(act):
            act.wait_ge(*s.g_steps(5))
            act.activation(f.EX[b], f.SH[b], ACT.Exp).then_inc(s.exped.sem, 1)

        @block.vector
        def _(dve):
            dve.tensor_reduce(f.SUM[:, :], m.XTA.rearrange("p (b s) -> p b s", b=B), AXX, ALU.add
                              ).then_inc(s.g_steps.sem, 1)
            dve.wait_ge(*s.g_steps(1))
            dve.tensor_scalar(f.MEAN[:, :], f.SUM[:, :], 1.0 / S, None, ALU.mult).then_inc(s.g_steps.sem, 1)
            dve.wait_ge(*s.g_done(1))
            dve.tensor_tensor(f.L[b], m.ps[0][b, 0:E], m.w("gate_b")[b], ALU.add).then_inc(s.g_steps.sem, 1)
            dve.wait_ge(*s.g_steps(3))
            dve.tensor_reduce(f.MX[b], f.L[b], AXX, ALU.max).then_inc(s.g_steps.sem, 1)
            mine, other = bcast(f.L[b], 2, E), bcast(f.L[b], 1, E)
            dve.tensor_tensor(f.GTR[b], other, mine, ALU.is_gt)
            dve.tensor_tensor(f.EQ[b], other, mine, ALU.is_equal).then_inc(s.g_compared.sem, 1)
            dve.wait_ge(*s.g_steps(4))
            dve.tensor_tensor(f.SH[b], f.L[b], bcast(f.MX[b, 0], 1, E), ALU.subtract).then_inc(s.g_steps.sem, 1)
            dve.wait_ge(*s.g_compared(1))
            dve.tensor_tensor(f.EQL[b], f.EQ[b], m.c("lower")[b].rearrange("p (j i) -> p j i", j=E),
                              ALU.mult).then_inc(s.g_compared.sem, 1)
            dve.wait_ge(*s.g_compared(2))
            dve.tensor_tensor(f.BEF[b], f.EQL[b], f.GTR[b], ALU.add).then_inc(s.g_compared.sem, 1)
            dve.wait_ge(*s.g_compared(3))
            dve.tensor_reduce(f.CNT[b], f.BEF[b], AXX, ALU.add).then_inc(s.g_compared.sem, 1)
            dve.wait_ge(*s.exped(1))
            dve.tensor_reduce(f.ES[b], f.EX[b], AXX, ALU.add).then_inc(s.g_steps.sem, 1)
            dve.wait_ge(*s.g_compared(4))
            dve.scalar_tensor_tensor(f.GM[b], f.CNT[b], 1.5, f.EX[b], ALU.is_lt, ALU.mult).then_inc(s.g_compared.sem, 1)
            dve.wait_ge(*s.g_steps(6))
            dve.reciprocal(f.ER[b], f.ES[b]).then_inc(s.g_steps.sem, 1)
            dve.wait_ge(*s.g_steps(7))
            dve.wait_ge(*s.g_compared(5))
            dve.scalar_tensor_tensor(f.ROWS[b], bcast(f.GM[b], 1, B), f.ER[b, 0:1],
                                     m.c("seqsel")[b].rearrange("p (b e) -> p b e", b=B), ALU.mult,
                                     ALU.mult).then_inc(s.g_rows.sem, 1)
            dve.wait_ge(*s.g_done(2))
            dve.tensor_copy(m.G[:, :], m.ps[1][:, 0:B * E])
    s.close(g_steps=7, g_compared=5, g_rows=1, g_done=2, exped=1)


def expert_mlp(nc, m, s, w, e):
    f = Memory()
    (f.YB, f.U, f.XT, f.R, f.O, f.ON, f.OW, f.NB
     ) = carve(m.ring, [(2, G, D), (2, G, D), (2, G * S), (2, G, D), (G, D), (G, D), (G, D), (D,)])
    HH = m.KT.rearrange("p (a c s) -> p a c s", a=2, c=DFF // D)
    NC = DFF // D
    ACC = m.XR

    with nc.Block() as block:
        @block.vector
        def _(dve):
            dve.tensor_tensor(f.NB[:, :], w("n1b"), w("l2b"), ALU.add)

    with nc.Block() as block:
        @block.gpsimd
        def _(pool):
            def step(k, p, on):
                g, q = k - 1, 1 - p
                if on[4]:
                    pool.wait_ge(*s.norm2(k - 3))
                    pool.wait_ge(*s.fin_based(k - 4))
                    pool.tensor_tensor(f.OW[:, :, :], f.ON[:, :, :], bcast(w("n2w"), 1, G),
                                       ALU.mult).then_inc(s.fin_scaled.sem, 1)
                if on[1]:
                    rstd_on(pool, m, s, g, q, G)
                if on[0]:
                    pool.wait_ge(*s.xn_ready(k - 1))
                    pool.tensor_tensor(f.YB[:, p], m.Y[:, dyn(k * G, G), :], bcast(w("ob"), 1, G),
                                       ALU.add).then_inc(s.summed.sem, 1)
                if on[3]:
                    rstd_on(pool, m.second, s.second, k - 3, q, G)
                if on[1]:
                    pool.wait_ge(*s.xn_ready(g + 1))
                    pool.wait_ge(*s.res_added(g - 1))
                    pool.tensor_tensor(f.R[:, q], f.U[:, q], bcast(w("n1w"), 1, G), ALU.mult).then_inc(s.scaled.sem, 1)
                    pool.wait_ge(*s.scaled(g + 1))
                    pool.tensor_tensor(f.R[:, q], f.R[:, q], bcast(f.NB[:, :], 1, G), ALU.add
                                       ).then_inc(s.based.sem, 1)
            pipeline(pool, NG, 5, step)

        @block.tensor
        def _(pe):
            def step(k, p, on):
                q = 1 - p
                if on[2]:
                    g = k - 2
                    pe.wait_ge(*s.h_ready((g + 1) * NC))
                    pe.wait_ge(*s.res_added(g - 1))
                    for j in range(G):
                        for c in range(NC):
                            last = pe.matmul(m.ps[5 + p][:, j * D:(j + 1) * D], HH[:, p, c, j * S:(j + 1) * S],
                                             w("l2")[:, c * D:(c + 1) * D], start=c == 0, stop=c == NC - 1,
                                             skip_group_check=True)
                    last.then_inc(s.projected.sem, 1)
                if on[1]:
                    g = k - 1
                    pe.wait_ge(*s.xt_ready(g + 1))
                    for c in range(NC):
                        pe.wait_ge(*s.h_ready(g * NC + c - NC + 1))
                        pe.matmul(m.ps[1 + c][:, :], w("l1")[:, c * D:(c + 1) * D], f.XT[:, q, :], start=True,
                                  stop=True).then_inc(s.h_done.sem, 1)
                if on[0]:
                    pe.wait_ge(*s.xn_ready(k + 1))
                    pe.wait_ge(*s.xt_ready(k))
                    for j in range(G):
                        last = pe.transpose(m.ps[0][:, j * S:(j + 1) * S], f.U[:, p, j, :], m.c("ident"))
                    last.then_inc(s.x_turned.sem, 1)
            pipeline(pe, NG, 3, step)

        @block.scalar
        def _(act):
            def step(k, p, on):
                if on[1]:
                    g, q = k - 1, 1 - p
                    act.wait_ge(*s.projected(g - 1))
                    for c in range(NC):
                        act.wait_ge(*s.h_done(g * NC + c + 1))
                        act.activation(HH[:, q, c, :], m.ps[1 + c][:, :], ACT.Relu,
                                       bias=w("l1b")[:, c:c + 1]).then_inc(s.h_ready.sem, 1)
                if on[0]:
                    act.wait_ge(*s.x_turned(k + 1))
                    act.wait_ge(*s.h_done((k - 1) * NC))
                    act.activation(f.XT[:, p, :], m.ps[0][:, :], ACT.Identity, bias=w("n1bc"),
                                   scale=w("n1wc")).then_inc(s.xt_ready.sem, 1)
            pipeline(act, NG, 2, step)

        @block.vector
        def _(dve):
            def step(k, p, on):
                yb = lambda j: f.YB[:, p, j, :]
                g = k - 2
                if on[0]:
                    dve.wait_ge(*s.summed(k + 1))
                    ln_stats(dve, m, s, k, p, G, yb, 1e-5)
                if on[3]:
                    dve.wait_ge(*s.fin_scaled(k - 2))
                    dve.tensor_tensor(f.OW[:, :, :], f.OW[:, :, :], bcast(w("n2b"), 1, G),
                                      ALU.add).then_inc(s.fin_added.sem, 1)
                if on[2]:
                    dve.wait_ge(*s.projected(g + 1))
                    dve.wait_ge(*s.based(g + 1))
                    dve.wait_ge(*s.norm2(g))
                    dve.tensor_tensor(f.O[:, :, :], m.ps[5 + p][:, :].rearrange("p (b d) -> p b d", b=G), f.R[:, p],
                                      ALU.add).then_inc(s.res_added.sem, 1)
                if on[0]:
                    dve.wait_ge(*s.x_turned(k - 1))
                    dve.wait_ge(*s.scaled(k - 1))
                    ln_apply(dve, m, s, k, p, G, yb, lambda j: f.U[:, p, j, :]).then_inc(s.xn_ready.sem, 1)
                if on[2]:
                    dve.wait_ge(*s.res_added(g + 1))
                    ln_stats(dve, m.second, s.second, g, p, G, lambda j: f.O[:, j, :], 1e-5)
                if on[3]:
                    dve.wait_ge(*s.fin_added(k - 2))
                    for j in range(G):
                        acc = ACC[:, dyn((k - 3) * G + j, 1), :].rearrange("p a d -> p (a d)")
                        last = dve.scalar_tensor_tensor(acc, f.OW[:, j, :], m.G[:, dyn(((k - 3) * G + j) * E + e, 1)],
                                                        acc, ALU.mult, ALU.add)
                    last.then_inc(s.fin_based.sem, 1)
                if on[2]:
                    dve.wait_ge(*s.fin_scaled(g))
                    ln_apply(dve, m.second, s.second, g, p, G, lambda j: f.O[:, j, :],
                             lambda j: f.ON[:, j, :]).then_inc(s.norm2.sem, 1)
            pipeline(dve, NG, 4, step)
    s.close(h_done=NG * NC, h_ready=NG * NC, **{n: NG for n in (
        "summed", "xn_ready", "scaled", "based", "norm2", "fin_scaled", "fin_added", "fin_based", "projected",
        "x_turned", "xt_ready", "res_added", "stats", "means", "spread", "vars", "rstd", "nmean", "stats2",
        "means2", "spread2", "vars2", "rstd2", "nmean2")})


def carve(area, shapes):
    views, at = [], 0
    for dims in shapes:
        n = int(np.prod(dims))
        ap = area[:, at:at + n]
        names = "abcd"[:len(dims)]
        if len(dims) > 1:
            ap = ap.rearrange(f"p ({' '.join(names)}) -> p {' '.join(names)}", **dict(zip(names, dims)))
        views.append(ap)
        at += n
    assert at <= area.shape[1]
    return views


def local_buffers(area):
    C = LH * LD
    f = Memory()
    (f.straight, f.swapped, f.XS, f.HT, f.SQ, f.T1, f.T2, f.SS, f.RN, f.QN, f.QZ, f.KT, f.V, f.PR, f.PT,
     f.ON, f.OT
     ) = carve(area, [(2, LD), (2, LD), (2, D), (2, S), (2, C), (2, C), (2, C), (2, LH), (2, LH), (2, 2, C),
        (LH, S), (4, S), (2, LH, LD + 1), (2, C), (2, C), (C,), (C,)])
    return f


def mlp_buffers(area):
    f = Memory()
    (f.XS, f.XN, f.HT, f.GT, f.HH
     ) = carve(area, [(2, G, D), (2, G, D), (2, G * S), (3, G * S), (2, 3, G * S)])
    return f


def program(nc, x, ctx_t, weights, experts, consts, out):
    m = Memory()
    sb = nc.alloc_sbuf_tensor
    m.W = sb("W", [128, WCOLS], F32)
    m.C = sb("C", [128, CCOLS], F32)
    m.X = sb("X", [S, B, D], F32)

    def c(name):
        at, n = CPLACE[name]
        return m.C[:, at:at + n]

    def w(name):
        at, n = WPLACE[name]
        return m.W[:, at:at + n]
    m.c, m.w = c, w
    e0 = WPLACE["f0_wqkv"][0]
    assert e0 + 2 * ECOLS <= WPLACE["m_down"][0]
    m.EW = m.W[:, e0:e0 + 2 * ECOLS].rearrange("p (a c) -> p a c", a=2)
    TOK = B * S
    arena = sb("arena", [128, 4 * TOK + B * H * HD], F32)
    a0 = B * H * HD
    m.arena = arena
    m.V = arena[:, 0:a0].rearrange("p (b h d) -> p b h d", b=B, h=H)
    m.QT = arena[:, a0:a0 + TOK]
    m.KT = arena[:, a0 + TOK:a0 + 2 * TOK]
    m.XTA = arena[:, a0 + 2 * TOK:a0 + 3 * TOK]
    m.XR = arena[:, a0 + 3 * TOK:a0 + 4 * TOK].rearrange("p (b d) -> p b d", b=B)
    m.QKT = arena[:, a0:a0 + 4 * TOK].rearrange("p (b c) -> p b c", b=B)
    m.Y = m.QT.rearrange("p (b d) -> p b d", b=B)
    ring = sb("ring", [128, 7040], F32)
    m.ring = ring
    m.HI = ring[:, 0:1024].rearrange("p (a t s) -> p a t s", a=2, t=4)
    m.LO = ring[:, 1024:2048].rearrange("p (a t s) -> p a t s", a=2, t=4)
    m.QS = sb("QS", [128, 2, 2, NU, S], F32R)
    m.KM = sb("KM", [128, 2, 2, 2, HU, S], F32R)
    m.PR = ring[:, 3072:5120].rearrange("p (a c) -> p a c", a=4)
    m.PT = ring[:, 5120:6144].rearrange("p (a c) -> p a c", a=2)
    m.ON = ring[:, 6144:6400].rearrange("p (a c) -> p a c", a=2)
    m.OT = ring[:, 6400:6528]
    m.OE = ring[:, 6528:7040]
    m.VS = sb("VS", [128, 2, H, 32], F32)
    m.XN = ring[:, 0:1024].rearrange("p (a b d) -> p a b d", a=2, b=G)
    m.XN2 = ring[:, 1024:2048].rearrange("p (a b d) -> p a b d", a=2, b=G)
    m.XT = ring[:, 2048:3072].rearrange("p (a c) -> p a c", a=2)
    m.CT = ring[:, 3072:4096].rearrange("p (a c) -> p a c", a=2)
    m.local = local_buffers(arena[:, 0:2 * TOK + a0])
    m.mlp = mlp_buffers(arena[:, 0:2 * TOK + a0])
    m.mx = sb("mx", [128, 4, 4], F32)
    m.rs = sb("rs", [128, H], F32)
    m.st = sb("st", [128, 2, 3 * G, 6], F32)
    m.df, m.sm, m.cv, m.dd, m.ve, m.rv, m.nm = (sb(n, [128, 2, 3 * G], F32)
                                                for n in ("df", "sm", "cv", "dd", "ve", "rv", "nm"))
    t = m.second = Memory()
    t.st, t.c = sb("st2", [128, 2, 3 * G, 6], F32), c
    t.df, t.sm, t.cv, t.dd, t.ve, t.rv, t.nm = (sb(n + "2", [128, 2, 3 * G], F32)
                                                for n in ("df", "sm", "cv", "dd", "ve", "rv", "nm"))
    m.G = sb("gates", [128, B * E], F32)
    m.GW = sb("gate_work", [128, 64], F32)
    m.ident_bf = sb("ident_bf", [128, 128], BF16)
    m.causal_bf = sb("causal_bf", [128, 128], BF16)
    m.band_bf = sb("band_bf", [128, 128], BF16)
    m.ps = [nc.alloc_psum_tensor(f"bank{i}", [128, 512], F32) for i in range(8)]

    s = Signals(nc)
    e_loaded = [nc.alloc_semaphore(f"expert_loaded{q}") for q in range(2)]
    x_loaded, w_loaded, rest_loaded, built = (nc.alloc_semaphore(n) for n in ("x_loaded", "w_loaded", "rest_loaded",
                                                                             "built"))

    with nc.Block() as block:
        @block.sync
        def _(sp):
            sp.dma_start(m.C[:, :], consts).then_inc(w_loaded, 16)
            sp.dma_start(m.X[:, :, :], x.rearrange("b s d -> s b d")).then_inc(x_loaded, 16)
            first = WPLACE["f0_wqkv"][0]
            sp.dma_start(m.W[:, 0:first], weights[:, 0:first]).then_inc(x_loaded, 16)
            sp.dma_start(m.W[:, first:WCOLS], weights[:, first:WCOLS]).then_inc(rest_loaded, 16)
            sp.wait_ge(x_loaded, 32)

        @block.gpsimd
        def _(pool):
            for sig in s.all:
                pool.sem_inc(sig.sem, CREDIT)

        @block.vector
        def _(dve):
            dve.memset(m.VS[:, :, :, HD + 1:32], 0.0)
            dve.memset(m.VS[:, :, :, HD:HD + 1], 1.0)
            dve.wait_ge(w_loaded, 16)
            dve.tensor_copy(m.ident_bf[:, :], m.c("ident"))
            dve.tensor_copy(m.causal_bf[:, :], m.c("causal"))
            dve.tensor_copy(m.band_bf[:, :], m.c("band")).then_inc(built, 1)

    r8 = float(HD) ** -0.5
    project(nc, m, s, ln=False, source="x", ctx=None, wq=w("a_wq"), wk=w("a_wk"), wv=w("a_wv"))
    attention(nc, m, s, causal=False, scale=r8, wide=False, w_out=None, target="x")
    project(nc, m, s, ln=True, source="x", ctx=ctx_t, wq=w("x_wq"), wk=w("x_wk"), wv=w("x_wv"))
    attention(nc, m, s, causal=True, scale=r8, wide=False, w_out=w("x_wo"), target="x")
    normalize(nc, m, s, keep_to=m.XR)
    with nc.Block() as block:
        @block.sync
        def _(sp):
            sp.wait_ge(rest_loaded, 16)
    for d in range(DEPTH):
        local_attention(nc, m, s, d)
        gated_mlp(nc, m, s, d)
    with nc.Block() as block:
        @block.sync
        def _(sp):
            sp.dma_start(m.EW[:, 0, :], experts[0]).then_inc(e_loaded[0], 16)
    project_latent(nc, m, s)
    attention(nc, m, s, causal=True, scale=float(HD + RD) ** -0.5, wide=True, w_out=w("m_o"), target="x")
    project_linear(nc, m, s, ctx_t)
    linear_attention(nc, m, s)
    for e in range(E):
        with nc.Block() as block:
            @block.sync
            def _(sp):
                if e + 1 < E:
                    sp.dma_start(m.EW[:, (e + 1) % 2, :], experts[e + 1]).then_inc(e_loaded[(e + 1) % 2], 16)
                sp.wait_ge(e_loaded[e % 2], 16 * (e // 2 + 1))

        def we(name):
            at, n = EPLACE[name]
            return m.EW[:, e % 2, at:at + n]
        project(nc, m, s, ln=e == 0, source="x" if e == 0 else "xt", ctx=None, wq=we("wq"), wk=we("wk"), wv=we("wv"),
                bq=we("bq"), bk=we("bk"), bv=we("bv"), keep=e == 0)
        if e == 0:
            gates(nc, m, s)
        attention(nc, m, s, causal=False, scale=r8, wide=False, w_out=we("ow"), target="y")
        expert_mlp(nc, m, s, we, e)
    normalize(nc, m, s, add=m.XR, out=out)


def shape_tables():
    f = np.float32
    t = {n: np.zeros((128, k), f) for n, k in CONSTS}
    p = np.arange(128)
    t["ident"][p, p] = 1
    t["ones"][:] = 1
    t["minus_half"][:] = -0.5
    t["kmask"][p, (p // HD) % HU] = 1
    t["kmask_wide"][p, (p // HD) % HU] = 1
    t["kmask_wide"][(p % 64) >= 32] = 1
    i, j = p[:, None], p[None, :]
    t["qmask"][p, p // 32] = 1
    t["qmask_wide"][p, p // 64] = 1
    t["causal"][:] = np.where(j > i, NEG, 0)
    t["band"][:] = np.where((j > i) | (i > j + WINDOW), NEG, 0)
    t["shift"][p[:-1], p[:-1] + 1] = 1
    t["blocks_sel"][:, 0:D] = (i // HD) == (j // HD)
    t["blocks_sel"][p, D + p // HD] = 1
    half = np.arange(0, LD, 2, dtype=f)
    freqs = p[:, None].astype(f) * (f(1.0) / f(10000.0) ** (half / f(LD)))[None]
    base = (half + f(0.4 * LD)) / f(1.4 * LD)
    power = (p - S // 2).astype(f) / f(WINDOW // 2)
    sc = base[None] ** power[:, None]
    cos, sin = np.cos(freqs), np.sin(freqs)
    t["qcos"][:] = np.concatenate([cos * sc, cos * sc], 1)
    t["qsin"][:] = np.concatenate([-sin * sc, sin * sc], 1)
    t["kcos"][:] = np.concatenate([cos / sc, cos / sc], 1)
    t["ksin"][:] = np.concatenate([-sin / sc, sin / sc], 1)
    fr = np.outer(p.astype(f), f(1.0) / f(10000.0) ** (np.arange(0, RD, 2, dtype=f) / f(RD)))
    cos, sin = np.cos(fr).T, np.sin(fr).T
    still, none = np.ones((32, S), f), np.zeros((32, S), f)
    t["ropecos"][:] = np.concatenate([still, cos, cos] * 2)
    t["ropesin"][:] = np.concatenate([none, -sin, sin] * 2)
    for par in range(2):
        t["place"][p, par * 2 * H + par * H + p % H] = 1
    t["block"][p, p // H] = 1
    t["lower"][:] = [i < j for j in range(E) for i in range(E)]
    for b in range(B):
        t["seqsel"][b, b * E:(b + 1) * E] = 1
    return np.concatenate([t[n] for n, _ in CONSTS], 1)


def pack_weights(a):
    def rep(v):
        return np.broadcast_to(np.asarray(v).reshape(1, -1), (128, np.asarray(v).size))

    def pad(v, rows=128):
        z = np.zeros((rows, v.shape[1]), np.float32)
        z[:v.shape[0]] = v
        return z

    def rows_to_chunks(v):
        return v.reshape(-1, 128, v.shape[1]).transpose(1, 0, 2).reshape(128, -1)

    def latent(heads, rope):
        none = np.zeros((D, 32), np.float32)
        part = [heads[:, i:i + 32] for i in range(0, D, 32)]
        partner = np.concatenate([rope[:, RD // 2:], rope[:, :RD // 2]], 1)
        return np.concatenate([none, partner, none, partner, part[0], rope, part[1], rope,
                               part[2], rope, part[3], rope], 1)

    w = {
        "a_wq": a["L0_attn_Wq"].T, "a_wk": np.tile(a["L0_attn_Wk"].T, (1, H)),
        "a_wv": np.tile(a["L0_attn_Wv"].T, (1, H)),
        "x_wq": a["L0_xattn_Wq"].T, "x_wk": a["L0_xattn_Wk"].T, "x_wv": a["L0_xattn_Wv"].T,
        "x_wo": a["L0_xattn_Wo"].T,
        "m_down": a["L1_attn_W_kv_down"],
        "m_q": latent(a["L1_attn_W_q"], a["L1_attn_W_q_rope"]),
        "m_k": latent(a["L1_attn_W_k_up"], a["L1_attn_W_k_rope"]), "m_v": a["L1_attn_W_v_up"],
        "m_o": a["L1_attn_W_o"],
        "y_wq": a["L1_xattn_wq"], "y_wkv": np.concatenate([a["L1_xattn_wk"], a["L1_xattn_wv"]], 1),
        "y_gamma": rep(a["L1_xattn_ln_gamma"]), "y_beta": rep(a["L1_xattn_ln_beta"]),
        "y_dw": a["L1_xattn_dense_w"].reshape(H, HD, D).transpose(1, 0, 2).reshape(D, D), "y_db": rep(a["L1_xattn_dense_b"]),
        "em": a["mask_BxS2_ff1"].T,
        "gate_w": a["L1_ffn_gate_w"].T, "gate_b": rep(a["L1_ffn_gate_b"]),
    }
    for d in range(DEPTH):
        b1 = a["L0_ffn_b1"][d]
        cols = []
        for half in (0, HID):
            for at, n in HCH:
                cols.append(pad(b1[half + at:half + at + n].reshape(n, 1)))
        w.update({
            f"f{d}_wqkv": a["L0_ffn_wqkv"][d], f"f{d}_qs": rep(a["L0_ffn_q_scale"][d]),
            f"f{d}_ks": rep(a["L0_ffn_k_scale"][d]), f"f{d}_wo": rows_to_chunks(a["L0_ffn_wo"][d]),
            f"f{d}_lg": a["L0_ffn_ln_g"][d].reshape(D, 1), f"f{d}_lb": a["L0_ffn_ln_b"][d].reshape(D, 1),
            f"f{d}_w1": a["L0_ffn_w1"][d], f"f{d}_b1": np.concatenate(cols, 1),
            f"f{d}_w2": rows_to_chunks(pad(a["L0_ffn_w2"][d], 384)), f"f{d}_b2": rep(a["L0_ffn_b2"][d]),
        })
    for e in range(E):
        iw, ib = a["L1_ffn_in_proj_w"][e], a["L1_ffn_in_proj_b"][e]
        w.update({
            f"e{e}_wq": iw[0:D].T, f"e{e}_wk": iw[D:2 * D].T, f"e{e}_wv": iw[2 * D:].T,
            f"e{e}_bq": ib[0:D].reshape(D, 1), f"e{e}_bk": ib[D:2 * D].reshape(D, 1), f"e{e}_bv": rep(ib[2 * D:]),
            f"e{e}_ow": a["L1_ffn_out_proj_w"][e].T, f"e{e}_ob": rep(a["L1_ffn_out_proj_b"][e]),
            f"e{e}_n1w": rep(a["L1_ffn_ln1_w"][e]), f"e{e}_n1b": rep(a["L1_ffn_ln1_b"][e]),
            f"e{e}_n1wc": a["L1_ffn_ln1_w"][e].reshape(D, 1), f"e{e}_n1bc": a["L1_ffn_ln1_b"][e].reshape(D, 1),
            f"e{e}_l1": a["L1_ffn_lin1_w"][e].T, f"e{e}_l1b": a["L1_ffn_lin1_b"][e].reshape(DFF // D, D).T,
            f"e{e}_l2": rows_to_chunks(a["L1_ffn_lin2_w"][e].T), f"e{e}_l2b": rep(a["L1_ffn_lin2_b"][e]),
            f"e{e}_n2w": rep(a["L1_ffn_ln2_w"][e]), f"e{e}_n2b": rep(a["L1_ffn_ln2_b"][e]),
        })
    experts = np.stack([np.concatenate([w[f"e{e}_{n}"] for n, _ in EXPERT], 1) for e in range(E)])
    return np.ascontiguousarray(np.concatenate([w[n] for n, _ in WEIGHTS], 1)), experts


def kernel(**inputs):
    import concourse.bacc as _bacc
    from concourse.bass_utils import run_bass_kernel_spmd as _run

    a = {n: np.asarray(v) for n, v in inputs.items()}
    weights, experts = pack_weights(a)
    arrays = {
        "x": np.ascontiguousarray(a["x"]),
        "ctx_t": np.ascontiguousarray(a["ctx_1024"].reshape(B * S, D).T),
        "weights": weights,
        "experts": experts,
        "consts": shape_tables(),
    }
    nc = _bacc.Bacc("TRN2", target_bir_lowering=False, num_devices=1)
    args = [nc.dram_tensor(n, v.shape, F32, kind="ExternalInput").ap() for n, v in arrays.items()]
    out = nc.dram_tensor("out", (B, S, D), F32, kind="ExternalOutput").ap()
    program(nc, *args, out)
    r = _run(nc, [arrays], core_ids=[0])
    return r.results[0]["out"]
```
